# Optimizing a Trainium2 kernel written in Bass

```python
import numpy as np
import jax
import jax.numpy as jnp

def _softmax(x, axis=-1):
    return jax.nn.softmax(x, axis=axis)

def _gelu(x):
    return jax.nn.gelu(x, approximate=True)

def _silu(x):
    return jax.nn.silu(x)

def _sigmoid(x):
    return jax.nn.sigmoid(x)

def _layernorm(x, axis=-1, eps=1e-05):
    m = jnp.mean(x, axis=axis, keepdims=True)
    v = jnp.var(x, axis=axis, keepdims=True)
    return (x - m) / jnp.sqrt(v + eps)

def _scatter_add(tgt, idx, src, axis=0):
    return tgt.at[idx].add(src)

def _segment_sum(src, seg, n):
    return jax.ops.segment_sum(src, seg, n)
kernel_name = 'mk_macaron_d1_jaxref_r4_16e6c2'

def setup_inputs(seed: int=0):
    np.random.seed(seed)
    _w = jnp.asarray

    def _L0_attn_setup():
        import jax, jax.numpy as jnp
        import numpy as np
        B, T, C = (4, 1024, 256)
        H = 16
        LS = 64
        EPS = 1e-06

        def rmsnorm(x, w):
            xf = x.astype(jnp.float32)
            y = xf * jax.lax.rsqrt(jnp.mean(xf * xf, axis=-1, keepdims=True) + EPS)
            return y.astype(x.dtype) * w
        key = jax.random.key(seed)
        k1, k2, k3 = jax.random.split(key, 3)
        x = jax.random.normal(k1, (B, T, C), dtype=jnp.float32)
        w_qkv = jax.random.normal(k2, (C, 3 * C), dtype=jnp.float32) * (1.0 / np.sqrt(C))
        ln_w = jnp.ones((C,), dtype=jnp.float32)
        w_proj = jax.random.normal(k3, (C, C), dtype=jnp.float32) * (1.0 / np.sqrt(C))
        return {'x': x, 'w_qkv': w_qkv, 'ln_w': ln_w, 'w_proj': w_proj}
    _L0_attn_in = _L0_attn_setup()

    def _L0_ffn_setup():
        import jax, jax.numpy as jnp
        import numpy as np
        B, S, H = (4, 512, 256)
        E, K = (8, 2)
        I_R, I_S = (4 * H, 8 * H)
        CAP_FACTOR = 1.25
        SCALE = 1.0
        key = jax.random.key(seed)
        ks = jax.random.split(key, 9)
        std = 0.02
        return {'x': jax.random.normal(ks[0], (B, S, H), jnp.float32), 'router_w': std * jax.random.normal(ks[1], (E, H), jnp.float32), 'rg': std * jax.random.normal(ks[2], (E, H, I_R), jnp.float32), 'ru': std * jax.random.normal(ks[3], (E, H, I_R), jnp.float32), 'rd': std * jax.random.normal(ks[4], (E, I_R, H), jnp.float32), 'sg': std * jax.random.normal(ks[5], (H, I_S), jnp.float32), 'su': std * jax.random.normal(ks[6], (H, I_S), jnp.float32), 'sd': std * jax.random.normal(ks[7], (I_S, H), jnp.float32)}
    _L0_ffn_in = _L0_ffn_setup()
    _d = {'L0_attn_x': _L0_attn_in['x'], 'L0_attn_w_qkv': _L0_attn_in['w_qkv'], 'L0_attn_ln_w': _L0_attn_in['ln_w'], 'L0_attn_w_proj': _L0_attn_in['w_proj'], 'L0_ffn_router_w': _L0_ffn_in['router_w'], 'L0_ffn_rg': _L0_ffn_in['rg'], 'L0_ffn_ru': _L0_ffn_in['ru'], 'L0_ffn_rd': _L0_ffn_in['rd'], 'L0_ffn_sg': _L0_ffn_in['sg'], 'L0_ffn_su': _L0_ffn_in['su'], 'L0_ffn_sd': _L0_ffn_in['sd']}
    _x0 = _d['L0_attn_x']
    _d['L0_attn_x'] = jax.random.normal(jax.random.fold_in(jax.random.key(seed), 1), (2, 2048, 256), dtype=_x0.dtype)
    del _x0
    return _d

def reference(L0_attn_x, L0_attn_w_qkv, L0_attn_ln_w, L0_attn_w_proj, L0_ffn_router_w, L0_ffn_rg, L0_ffn_ru, L0_ffn_rd, L0_ffn_sg, L0_ffn_su, L0_ffn_sd):

    def _L0_attn_ref(x, w_qkv, ln_w, w_proj):
        import jax, jax.numpy as jnp
        import numpy as np
        B, T, C = (4, 1024, 256)
        H = 16
        LS = 64
        EPS = 1e-06

        def rmsnorm(x, w):
            xf = x.astype(jnp.float32)
            y = xf * jax.lax.rsqrt(jnp.mean(xf * xf, axis=-1, keepdims=True) + EPS)
            return y.astype(x.dtype) * w
        Bx, Tx, Cx = x.shape
        ng = Tx // LS
        hd = Cx // H
        xg = x.reshape(Bx, ng, LS, Cx)
        qkv = jnp.einsum('bglc,cd->bgld', xg, w_qkv)
        q, k, v = jnp.split(qkv, 3, axis=-1)
        q = rmsnorm(q, ln_w)
        k = rmsnorm(k, ln_w)
        q = q.reshape(Bx, ng, LS, H, hd).transpose(0, 1, 3, 2, 4)
        k = k.reshape(Bx, ng, LS, H, hd).transpose(0, 1, 3, 2, 4)
        v = v.reshape(Bx, ng, LS, H, hd).transpose(0, 1, 3, 2, 4)
        scale = 1.0 / np.sqrt(hd)
        att = jnp.einsum('bghqd,bghkd->bghqk', q, k) * scale
        causal = jnp.tril(jnp.ones((LS, LS), dtype=bool))
        att = jnp.where(causal, att, -jnp.finfo(att.dtype).max)
        att = jax.nn.softmax(att, axis=-1)
        y = jnp.einsum('bghqk,bghkd->bghqd', att, v)
        y = y.transpose(0, 1, 3, 2, 4).reshape(Bx, Tx, Cx)
        return jnp.einsum('btc,cd->btd', y, w_proj)

    def _L0_ffn_ref(x, router_w, rg, ru, rd, sg, su, sd):
        import jax, jax.numpy as jnp
        import numpy as np
        B, S, H = (4, 512, 256)
        E, K = (8, 2)
        I_R, I_S = (4 * H, 8 * H)
        CAP_FACTOR = 1.25
        SCALE = 1.0
        b, s, h = x.shape
        T = b * s
        capacity = max(int(CAP_FACTOR * T / E), 1)
        xf = x.reshape(T, h)
        eps = jnp.finfo(x.dtype).eps
        xn = xf * jax.lax.rsqrt(jnp.mean(xf * xf, axis=-1, keepdims=True) + eps)
        logits = xn @ router_w.T
        probs = jax.nn.softmax(logits, axis=-1)
        topk_p, topk_i = jax.lax.top_k(probs, K)
        rw = topk_p / jnp.sum(topk_p, axis=-1, keepdims=True)
        one_hot = jax.nn.one_hot(topk_i, E, dtype=x.dtype)
        mask = one_hot.sum(1)
        wdense = (one_hot * rw[..., None]).sum(1)
        sel = mask.T.astype(bool)
        order = jnp.argsort(~sel, axis=1, stable=True)
        dispatch = order[:, :capacity]
        count = sel.sum(axis=1)
        valid = (jnp.arange(capacity)[None, :] < count[:, None]).astype(x.dtype)
        xg = xf[dispatch]
        gate = jax.nn.silu(jnp.einsum('ech,ehi->eci', xg, rg))
        up = jnp.einsum('ech,ehi->eci', xg, ru)
        eout = jnp.einsum('eci,eih->ech', gate * up, rd)
        w = jnp.take_along_axis(wdense.T, dispatch, axis=1)
        contrib = eout * (w * valid)[..., None]
        routed = jnp.zeros_like(xf).at[dispatch.reshape(-1)].add(contrib.reshape(-1, h))
        shared = jax.nn.silu(x @ sg) * (x @ su) @ sd
        return shared + SCALE * routed.reshape(b, s, h)
    x = L0_attn_x
    x = x + 0.5 * _L0_ffn_ref(_layernorm(x, axis=-1), L0_ffn_router_w, L0_ffn_rg, L0_ffn_ru, L0_ffn_rd, L0_ffn_sg, L0_ffn_su, L0_ffn_sd)
    x = x + _L0_attn_ref(_layernorm(x, axis=-1), L0_attn_w_qkv, L0_attn_ln_w, L0_attn_w_proj)
    x = x + 0.5 * _L0_ffn_ref(_layernorm(x, axis=-1), L0_ffn_router_w, L0_ffn_rg, L0_ffn_ru, L0_ffn_rd, L0_ffn_sg, L0_ffn_su, L0_ffn_sd)
    return x

_drawn_inputs = setup_inputs


def setup_inputs(seed=0):
    import zlib

    import numpy as np

    out = dict(_drawn_inputs(seed))
    spreads = {'L0_attn_ln_w': (1.0, 0.2)}
    factors = {'L0_ffn_router_w': 3.758, 'L0_ffn_rg': 3.293, 'L0_ffn_ru': 3.254, 'L0_ffn_rd': 3.248}
    for name, (base, spread) in spreads.items():
        noise = np.random.default_rng([zlib.crc32(name.encode()), seed]).standard_normal(out[name].shape)
        drawn = base * np.exp(spread * noise) if base else spread * noise
        out[name] = jnp.asarray(drawn.astype(out[name].dtype))
    for name, factor in factors.items():
        out[name] = (out[name] * factor).astype(out[name].dtype)
    return out
```

```python
from contextlib import ExitStack

import concourse.bass as bass
from concourse import mybir

F32 = mybir.dt.float32
F32R = mybir.dt.float32r
I32 = mybir.dt.int32
ALU = mybir.AluOpType
ACT = mybir.ActivationFunctionType
AX = mybir.AxisListType.X

P = 128
LN_EPS = 1e-5
RMS_EPS = 1e-6
ROUTER_EPS = 2.0 ** -23
FAR = 1.0e6
GROUP = 64
HD = 16


class Step:

    def __init__(self, index, period, reg=None, count=0):
        self.index, self.period, self.reg, self.count = index, period, reg, count
        self.first = index == 0
        self.mod = index % period

    def at(self, f):
        if self.reg is None:
            return f(self.index)
        v = [f(self.index + self.period * n) for n in range(self.count)]
        slope = v[1] - v[0] if self.count > 1 else 0
        assert all(v[n] == v[0] + n * slope for n in range(self.count))
        return v[0] if slope == 0 else self.reg * slope + v[0]


def wait(eng, semaphore, value):
    if not isinstance(value, int) or value > 0:
        eng.wait_ge(semaphore, value)


def sweep(eng, n, period, body, head=1, tail=0):
    for b in range(head):
        body(Step(b, period))
    count = (n - head - tail) // period
    done = head
    if count > 1:
        with eng.Fori(0, count) as i:
            for r in range(period):
                body(Step(head + r, period, i, count))
        done += period * count
    for b in range(done, n):
        body(Step(b, period))


def program(nc, x_in, w_qkv, ln_w, w_proj, router_w, rg, ru, rd, sg, su, sd, out):
    B, S, C = x_in.shape
    T = B * S
    E = router_w.shape[0]
    I = rg.shape[2]
    SU = sg.shape[1] // I
    TOPK = 2
    CAP = int(1.25 * T / E)
    KC = C // P
    NCH = I // P
    NT = T // P
    BT = 512 // P
    NB = T // 512
    SB = 512
    EB = CAP // 2
    NEB = 2 * E
    NH = C // HD
    assert C == 256 and KC == 2 and I == 1024 and SU == 2 and NCH == 8 and EB == 320 and NB == 8
    PIECE = 2 * KC * P + C
    ROW = C + 1 + E
    EPART = [(0, 128), (128, 128), (256, 64)]
    UNITS = SU + E
    FB = SU * NB + NEB

    x_rows = x_in.rearrange("b s c -> (b s) c").rearrange("(t p) c -> p t c", p=P)
    out_rows = out.rearrange("b s c -> (b s) c")

    with ExitStack() as ctx:
        def dram(name, shape, dt):
            return nc.dram_tensor(name, shape, dt, kind="Internal").ap()

        def sb(name, shape, dt, on=ctx):
            return on.enter_context(nc.sbuf_tensor(name, shape, dt))

        def psum(name, shape):
            return ctx.enter_context(nc.psum_tensor(name, shape, F32))

        def sem(name):
            return ctx.enter_context(nc.semaphore(name))

        zh_d = dram("zh_d", [P, KC, T], F32)
        zl_d = dram("zl_d", [P, KC, T], F32)
        zn_d = dram("zn_d", [T, C], F32)
        slots_d = [dram(f"slots{f}_d", [E * CAP, ROW], F32) for f in range(2)]
        y_d = [dram(f"y{f}_d", [T + P, C], F32) for f in range(2)]
        zn_rows = zn_d.rearrange("(t p) c -> p t c", p=P)
        y_rows = [y[0:T, :].rearrange("(t p) c -> p t c", p=P) for y in y_d]

        x = sb("x", [P, NT, C], F32)
        w0 = sb("w0", [P, 2, NCH, PIECE], F32R)
        stage = sb("stage", [P, 2, PIECE], F32)
        ident = sb("ident", [P, P], F32)
        below_s = sb("below_s", [P, P], F32)
        below = sb("below", [P, P], F32R)
        causal = sb("causal", [P, P], F32)
        one_row = sb("one_row", [P, NT], F32)
        empty = sb("empty", [P, ROW], F32)
        ones = sb("ones", [P, P], F32R)
        router = sb("router", [P, KC, 2, E], F32R)
        router_s = sb("router_s", [P, KC, E], F32)
        mhalf = sb("mhalf", [P, NT], F32)
        st = sb("st", [P, BT, 6], F32)
        lnd = sb("lnd", [P, BT], F32)
        lnm = sb("lnm", [P, BT], F32)
        lnv = sb("lnv", [P, BT], F32)
        lndd = sb("lndd", [P, BT], F32)
        lnv2 = sb("lnv2", [P, BT], F32)
        mean = sb("mean", [P, BT], F32)
        var = sb("var", [P, NT], F32)
        vare = sb("vare", [P, NT], F32)
        rstd = sb("rstd", [P, NT], F32)
        ra = sb("ra", [P, NT], F32)
        rb = sb("rb", [P, NT], F32)
        m1 = sb("m1", [P, NT], F32)
        m2 = sb("m2", [P, NT], F32)
        lg = sb("lg", [P, NT, E], F32)
        pr = sb("pr", [P, NT, E], F32)
        pick = sb("pick", [P, NT, E], F32)
        oh = sb("oh", [P, TOPK, NT, E], F32)
        mask = sb("mask", [P, NT, E], F32R)
        prio = sb("prio", [P, NT, E], F32)
        base = sb("base", [P, NT, E], F32)
        slot_i = sb("slot_i", [P, TOPK, NT], I32)
        table = sb("table", [P, NT, 1 + E], F32)
        srow = sb("srow", [P, 2, ROW], F32)
        sidx = sb("sidx", [P, 2, TOPK], I32)
        wmeta = sb("wmeta", [P, 4, 3], F32)
        tmeta = sb("tmeta", [P, 4, 3], I32)
        o_t = sb("o_t", [P, KC, SB], F32)
        ffn_mem = ExitStack()
        w1 = sb("w1", [P, 2, NCH, PIECE], F32R, ffn_mem)
        zh = sb("zh", [P, 2, KC, SB], F32R, ffn_mem)
        zl = sb("zl", [P, 2, KC, SB], F32R, ffn_mem)
        sg_s = sb("sg_s", [P, 2, SB], F32, ffn_mem)
        h_s = sb("h_s", [P, 2, SB], F32, ffn_mem)
        hh = sb("hh", [P, 2, SB], F32R, ffn_mem)
        hl = sb("hl", [P, 2, SB], F32R, ffn_mem)
        zn = sb("zn", [P, 2, BT, C], F32, ffn_mem)
        xr = sb("xr", [P, 2, 3, ROW], F32, ffn_mem)
        eo = sb("eo", [P, 2, 3, C], F32, ffn_mem)
        ffn_mem.close()
        att = ExitStack()
        aw_s = sb("aw_s", [P, KC, 4 * C], F32, att)
        aw = sb("aw", [P, 2, KC, 4 * C], F32R, att)
        lnw = sb("lnw", [P, C], F32, att)
        azn = sb("azn", [P, C], F32, att)
        azh = sb("azh", [P, KC, P], F32R, att)
        azl = sb("azl", [P, KC, P], F32R, att)
        qk = sb("qk", [P, 2, C], F32, att)
        qcat = sb("qcat", [P, NH, 64], F32, att)
        kcat = sb("kcat", [P, NH, 64], F32, att)
        q_t = sb("q_t", [P, NH // 2, P], F32R, att)
        k_t = sb("k_t", [P, NH // 2, P], F32R, att)
        s_s = sb("s_s", [P, NH, GROUP], F32, att)
        p_s = sb("p_s", [P, NH, GROUP], F32, att)
        smax = sb("smax", [P, NH], F32, att)
        ph = sb("ph", [P, NH // 2, P], F32R, att)
        pl = sb("pl", [P, NH // 2, P], F32R, att)
        vh = sb("vh", [P, NH // 2, 66], F32R, att)
        vl = sb("vl", [P, NH // 2, 66], F32R, att)
        rden = sb("rden", [P, NH], F32, att)
        y_s = sb("y_s", [P, C], F32, att)
        yh = sb("yh", [P, KC, P], F32R, att)
        yl = sb("yl", [P, KC, P], F32R, att)
        sqj = sb("sqj", [P, C], F32, att)
        ssq = sb("ssq", [P, 2], F32, att)
        qke = sb("qke", [P, 2], F32, att)
        qkr = sb("qkr", [P, 2], F32, att)
        ast = sb("ast", [P, 8], F32, att)
        amean = sb("amean", [P, 1], F32, att)
        alv = sb("alv", [P, 2], F32, att)
        ard = sb("ard", [P, 1], F32, att)
        att.close()

        gate_p = psum("gate_p", [P, 2, 512])
        up_p = psum("up_p", [P, 2, 512])
        out_p = psum("out_p", [P, 2, 512])
        misc = psum("misc", [P, 2, 512])

        names = """const x_l0 x_l1 gate_full silu_done up_full h_done hh_done down_done hl_done out_full
            ot_act ot_dve misc_full misc_free st_in0 st_in1 wh_done wl_done ln_st ln_a ln_b ln_c ln_var
            ln_rstd ln_z zh_done zsv0 zsv1 zin0 zin1 r_in rt rt_rms rt_rs rt_exp rt_in rt_mask
            rt_pos sr_in0 sr_in1 sidx_in scat0 scat1 pool_step routed xr_in0 xr_in1 meta_done
            eo_done sadd0 sadd1 x_sh y_sv0 y_sv1 init out_done
            aw_in aw_h aw_l av apool a_t a_zh a_zl a_qkv a_sq a_qn a_qc a_qlo a_qt a_qe a_s a_mk
            a_exp a_pt a_ph a_pl a_vh a_vl a_y a_yn a_yt a_yh a_yl a_o a_x a_const a_ke a_kt
            sums_done sp_step dve_step a_masked a_max a_rden pool_const""".split()
        sm = {n: sem(n) for n in names}
        W = [w0, w1]
        x_l = [sm["x_l0"], sm["x_l1"]]
        zsv = [sm["zsv0"], sm["zsv1"]]
        zin = [sm["zin0"], sm["zin1"]]
        st_in = [sm["st_in0"], sm["st_in1"]]
        sr_in = [sm["sr_in0"], sm["sr_in1"]]
        scat = [sm["scat0"], sm["scat1"]]
        xr_in = [sm["xr_in0"], sm["xr_in1"]]
        sadd = [sm["sadd0"], sm["sadd1"]]
        y_sv = [sm["y_sv0"], sm["y_sv1"]]

        PH = {"s0": 0, "s1": NB, "e": 2 * NB}
        LEN = {"s0": NB, "s1": NB, "e": NEB}

        def blk(f, phase, b):
            return FB * f + PH[phase] + b

        use = {}
        for f in range(2):
            def add(*key):
                use[(f, *key)] = len(use)
            add("T", "s0", 0)
            add("R", "s0", 0)
            for b in range(NB):
                if b:
                    add("O", "s0", b - 1)
                if b < NB - 1:
                    add("T", "s0", b + 1)
                    add("R", "s0", b + 1)
            add("M", "s0", 0)
            for b in range(NB):
                add("O", *(("s1", b - 1) if b else ("s0", NB - 1)))
            add("T", "e", 0)
            for b in range(NEB):
                add("O", *(("e", b - 1) if b else ("s1", NB - 1)))
                if b < NEB - 1:
                    add("T", "e", b + 1)
            add("O", "e", NEB - 1)

        POOL_CONSTS = 9

        def hooks(f, phase, s):
            b, n = s.index, LEN[phase]
            last = s.reg is None and b == n - 1
            got = {}
            if phase == "s0":
                if not s.first:
                    got[1] = ("O", "s0", -1)
                if not last:
                    got[3] = ("T", "s0", 1)
                    got[5] = ("R", "s0", 1)
            elif phase == "s1":
                got[1] = ("O", "s0", NB - 1) if s.first else ("O", "s1", -1)
            else:
                got[1] = ("O", "s1", NB - 1) if s.first else ("O", "e", -1)
                if not last:
                    got[4] = ("T", "e", 1)
            return got

        def use_at(f, phase, s, hook):
            what, ph2, off = hook
            if s.first and ph2 != phase:
                return use[(f, what, ph2, off)]
            return s.at(lambda b: use[(f, what, ph2, b + off)])

        def out_used(f, phase, s):
            def count(b):
                if b >= 2:
                    return use[(f, "O", phase, b - 2)] + 1
                if phase == "s0":
                    return use[(f, "O", "s0", 0)] - 3 + 1
                return use[(f, "O", {"s1": "s0", "e": "s1"}[phase], NB - 2 + b)] + 1
            return s.at(count)

        def piece_of(f, unit, j):
            return (f * UNITS + unit) * NCH + j

        def splits(f, phase, s):
            if phase == "e":
                cs = {1: 0, 3: 1, 5: 2, 7: 3}
                return {c: (s.index % 2) * 4 + j for c, j in cs.items()}
            return {6: None}

        def split_piece(f, phase, s, c):
            cs = splits(f, phase, s)
            if c not in cs:
                return None
            if phase == "e":
                j = cs[c]
                unit = lambda b: SU + b // 2 + 1
                if s.reg is None and s.index >= NEB - 2 and f == 1:
                    return None
                return (s.at(lambda b: piece_of(f, unit(b), 0) + j), j, unit(s.index) % 2)
            u = 1 if phase == "s0" else 2
            return (s.at(lambda b: piece_of(f, u, b)), None, u % 2)

        AV = 5
        RT = 35
        XB = NEB // 2
        block = ctx.enter_context(nc.Block())

        @block.tensor
        def _(pe):
            def split_product(dst, pairs, n):
                k = 0
                for ah, al, bh, bl in pairs:
                    for a, b in ((ah, bh), (ah, bl), (al, bh)):
                        last = pe.matmul(dst, a, b, start=(k == 0), stop=(k == 3 * n - 1))
                        k += 1
                return last

            def gate_up(f, phase, s, c, buf, ncol):
                par = c % 2
                n = lambda b: NCH * blk(f, phase, b) + c
                z = s.mod % 2
                g0 = 0
                for which, psb, done in ((0, gate_p, "gate_full"), (1, up_p, "up_full")):
                    if n(s.index) >= 2:
                        pe.wait_ge(sm["silu_done" if which == 0 else "h_done"], s.at(lambda b: n(b) - 1))
                    k0 = which * KC * P
                    w = W[buf]
                    split_product(psb[:, par, 0:ncol],
                                  [(w[:, 0, c, k0 + k * P:k0 + (k + 1) * P], w[:, 1, c, k0 + k * P:k0 + (k + 1) * P],
                                    zh[:, z, k, 0:ncol], zl[:, z, k, 0:ncol]) for k in range(KC)], KC).then_inc(sm[done], 1)

            def down(n_of, s, c, buf, ncol, blk_of):
                pe.wait_ge(sm["hl_done"], s.at(lambda b: n_of(b) + 1))
                if c == 0 and blk_of(s.index) > 0:
                    pe.wait_ge(sm["ot_act"], s.at(blk_of))
                    pe.wait_ge(sm["ot_dve"], s.at(blk_of))
                w = W[buf]
                par = c % 2
                for k in range(KC):
                    o = 2 * KC * P + k * P
                    for j, (hi, a) in enumerate(((0, hh), (0, hl), (1, hh))):
                        last = pe.matmul(out_p[:, k, 0:ncol], w[:, hi, c, o:o + P], a[:, par, 0:ncol],
                                         start=(c == 0 and j == 0), stop=(c == NCH - 1 and j == 2))
                last.then_inc(sm["down_done"], 1)

            def z_transposes(f, phase, s, off, m):
                nxt = lambda b: b + off
                if phase == "s0":
                    pe.wait_ge(sm["ln_z"], s.at(lambda b: NB * f + nxt(b) + 1))
                else:
                    par = (s.mod + off) % 2
                    pe.wait_ge(xr_in[par], s.at(lambda b: 32 * (XB * f + nxt(b) // 2 + 1)))
                wait(pe, sm["misc_free"], m)
                par = (s.mod + off) % 2
                for k in range(KC):
                    if phase == "s0":
                        for j in range(BT):
                            last = pe.transpose(misc[:, k, j * P:(j + 1) * P], zn[:, par, j, k * P:(k + 1) * P], ident[:, :])
                    else:
                        for j, (at, rows) in enumerate(EPART):
                            last = pe.transpose(misc[:, k, at:at + rows], xr[0:rows, par, j, k * P:(k + 1) * P],
                                                ident[0:rows, 0:rows])
                last.then_inc(sm["misc_full"], 1)

            def router_product(s, off, m):
                pe.wait_ge(sm["misc_free"], m)
                par = (s.mod + off) % 2
                for j in range(BT):
                    c = slice(j * P, (j + 1) * P)
                    last = split_product(misc[:, 0, j * E:(j + 1) * E],
                                         [(zh[:, par, k, c], zl[:, par, k, c], router[:, k, 0, :], router[:, k, 1, :])
                                          for k in range(KC)], KC)
                last.then_inc(sm["misc_full"], 1)

            def out_transposes(expert, count, m):
                pe.wait_ge(sm["ot_act"], count)
                pe.wait_ge(sm["ot_dve"], count)
                pe.wait_ge(sm["misc_free"], m)
                parts = EPART if expert else [(j * P, P) for j in range(BT)]
                for j, (at, rows) in enumerate(parts):
                    for k in range(KC):
                        o = (j % 2) * C + k * P
                        last = pe.transpose(misc[0:rows, j // 2, o:o + P], o_t[:, k, at:at + rows], ident[:, :])
                last.then_inc(sm["misc_full"], 1)

            def route_product(f, m):
                pe.wait_ge(sm["rt_mask"], f + 1)
                pe.wait_ge(sm["misc_free"], m)
                mk = mask[:, :, :].rearrange("p t e -> p (t e)")
                pe.matmul(misc[:, 0, 0:NT * E], below[:, :], mk, start=True, stop=True)
                pe.matmul(misc[:, 1, 0:NT * E], ones[:, :], mk, start=True, stop=True).then_inc(sm["misc_full"], 1)

            def do_hook(f, phase, s, hook):
                what, ph2, off = hook
                m = use_at(f, phase, s, hook)
                if what == "T":
                    z_transposes(f, ph2, s, off, m)
                elif what == "R":
                    router_product(s, off, m)
                else:
                    out_transposes(ph2 == "e", s.at(lambda b: blk(f, phase, b)), m)

            def ffn(f):
                z_transposes(f, "s0", Step(0, 2), 0, use[(f, "T", "s0", 0)])
                if f == 0:
                    pe.wait_ge(sm["rt_in"], 2)
                router_product(Step(0, 2), 0, use[(f, "R", "s0", 0)])
                prev = [None]
                for phase in ("s0", "s1", "e"):
                    period = 4 if phase == "e" else 2
                    ncol = EB if phase == "e" else SB

                    def body(s, phase=phase, ncol=ncol):
                        unit = (lambda b: SU + b // 2) if phase == "e" else (lambda b: 0 if phase == "s0" else 1)
                        buf = unit(s.index) % 2
                        first_of_unit = s.first or (phase == "e" and s.index % 2 == 0)
                        if phase == "s1":
                            pe.wait_ge(zin[s.mod % 2], s.at(lambda b: 32 * (NB // 2 * f + b // 2 + 1)))
                        else:
                            pe.wait_ge(sm["misc_free"], s.at(lambda b: use[(f, "T", phase, b)] + 1))
                        hk = hooks(f, phase, s)
                        for c in range(NCH):
                            if first_of_unit:
                                pe.wait_ge(sm["wl_done"], s.at(lambda b: piece_of(f, unit(b), c) + 1))
                            gate_up(f, phase, s, c, buf, ncol)
                            if c:
                                down(lambda b: NCH * blk(f, phase, b) + c - 1, s, c - 1, buf, ncol,
                                     lambda b: blk(f, phase, b))
                            elif not (phase == "s0" and s.first):
                                if s.first:
                                    pbuf = 0 if phase == "s1" else 1
                                    pcol = SB
                                else:
                                    pbuf = unit(s.index - 1) % 2
                                    pcol = ncol
                                down(lambda b: NCH * blk(f, phase, b) - 1, s, NCH - 1, pbuf, pcol,
                                     lambda b: blk(f, phase, b) - 1)
                            if c in hk:
                                do_hook(f, phase, s, hk[c])

                    sweep(pe, LEN[phase], period, body)
                    if phase == "s0":
                        route_product(f, use[(f, "M", "s0", 0)])
                    if phase == "s1":
                        z_transposes(f, "e", Step(0, 4), 0, use[(f, "T", "e", 0)])
                s = Step(FB * f + FB, 1)
                down(lambda b: NCH * b - 1, s, NCH - 1, (UNITS - 1) % 2, EB, lambda b: b - 1)
                out_transposes(True, FB * (f + 1), use[(f, "O", "e", NEB - 1)])

            def attention():
                def tile(s):
                    n = lambda k: s.at(lambda b: b + k)
                    pe.wait_ge(sm["av"], s.at(lambda b: AV * b + 4))
                    wait(pe, sm["a_o"], n(0))
                    for k in range(KC):
                        last = pe.transpose(misc[:, 0, k * P:(k + 1) * P], azn[:, k * P:(k + 1) * P], ident[:, :])
                    last.then_inc(sm["a_t"], 1)
                    if s.first:
                        pe.wait_ge(sm["aw_l"], 1)
                    pe.wait_ge(sm["a_zl"], n(1))
                    split_product(gate_p[:, 0, :], [(azh[:, k, :], azl[:, k, :], aw[:, 0, k, 0:512], aw[:, 1, k, 0:512])
                                                    for k in range(KC)], KC)
                    split_product(gate_p[:, 1, 0:C], [(azh[:, k, :], azl[:, k, :], aw[:, 0, k, 512:768], aw[:, 1, k, 512:768])
                                                      for k in range(KC)], KC).then_inc(sm["a_qkv"], 1)
                    pe.wait_ge(sm["a_qlo"], n(1))
                    for j in range(NH // 2):
                        last = pe.transpose(misc[:, j // 4, (j % 4) * P:(j % 4 + 1) * P],
                                            qcat[:, 2 * j:2 * j + 2, :].rearrange("p h d -> p (h d)"), ident[:, :])
                    last.then_inc(sm["a_qt"], 1)
                    pe.wait_ge(sm["a_qe"], n(1))
                    for j in range(NH // 2):
                        last = pe.transpose(misc[:, j // 4, (j % 4) * P:(j % 4 + 1) * P],
                                            kcat[:, 2 * j:2 * j + 2, :].rearrange("p h d -> p (h d)"), ident[:, :])
                    last.then_inc(sm["a_kt"], 1)
                    pe.wait_ge(sm["a_ke"], n(1))
                    for j in range(NH // 2):
                        for r, bank in ((0, up_p), (1, out_p)):
                            rows = slice(64 * r, 64 * r + 3 * HD)
                            last = pe.matmul(bank[:, j // 4, (j % 4) * P:(j % 4 + 1) * P], q_t[rows, j, :], k_t[rows, j, :],
                                             start=True, stop=True)
                    last.then_inc(sm["a_s"], 1)
                    pe.wait_ge(sm["a_exp"], n(1))
                    for j in range(NH // 2):
                        last = pe.transpose(misc[:, j // 4, (j % 4) * P:(j % 4 + 1) * P],
                                            p_s[:, 2 * j:2 * j + 2, :].rearrange("p h d -> p (h d)"), ident[:, :])
                    last.then_inc(sm["a_pt"], 1)
                    pe.wait_ge(sm["a_pl"], n(1))
                    pe.wait_ge(sm["a_vl"], n(1))
                    for j in range(NH // 2):
                        o = (j % 4) * 66
                        last = split_product(gate_p[:, j // 4, o:o + 66], [(ph[:, j, :], pl[:, j, :], vh[:, j, :], vl[:, j, :])], 1)
                    last.then_inc(sm["a_y"], 1)
                    pe.wait_ge(sm["a_yn"], n(1))
                    for k in range(KC):
                        last = pe.transpose(misc[:, 0, k * P:(k + 1) * P], y_s[:, k * P:(k + 1) * P], ident[:, :])
                    last.then_inc(sm["a_yt"], 1)
                    pe.wait_ge(sm["a_yl"], n(1))
                    split_product(misc[:, 1, 0:C], [(yh[:, k, :], yl[:, k, :], aw[:, 0, k, 768:1024], aw[:, 1, k, 768:1024])
                                                    for k in range(KC)], KC).then_inc(sm["a_x"], 1)
                sweep(pe, NT, 2, tile)

            pe.wait_ge(sm["const"], 1)
            ffn(0)
            attention()
            ffn(1)

        @block.scalar
        def _(act):
            def z_high(f, phase, s, off, m):
                par = (s.mod + off) % 2
                ncol = SB if phase == "s0" else EB
                act.wait_ge(sm["misc_full"], m + 1)
                wait(act, sm["up_full"], s.at(lambda b: NCH * (blk(f, phase, b + off) - 1)))
                if phase == "s0":
                    act.wait_ge(zsv[par], s.at(lambda b: 48 * (NB // 2 * f + (b + off) // 2 + 1)))
                nc.scalar.copy(zh[:, par, :, 0:ncol], misc[:, :, 0:ncol]).then_inc(sm["zh_done"], 1)

            def ffn(f):
                z_high(f, "s0", Step(0, 2), 0, use[(f, "T", "s0", 0)])
                for phase in ("s0", "s1", "e"):
                    period = 4 if phase == "e" else 2
                    ncol = EB if phase == "e" else SB

                    def body(s, phase=phase, ncol=ncol):
                        hk = hooks(f, phase, s)
                        for c in range(NCH):
                            par = c % 2
                            n = lambda b: NCH * blk(f, phase, b) + c
                            act.wait_ge(sm["gate_full"], s.at(lambda b: n(b) + 1))
                            if n(s.index) >= 2:
                                act.wait_ge(sm["h_done"], s.at(lambda b: n(b) - 1))
                            nc.scalar.activation(sg_s[:, par, 0:ncol], gate_p[:, par, 0:ncol], ACT.Silu).then_inc(sm["silu_done"], 1)
                            if c == 0 and not (phase == "s0" and s.first):
                                g = lambda b: blk(f, phase, b)
                                pcol = ncol if not s.first else SB
                                act.wait_ge(sm["down_done"], s.at(lambda b: NCH * g(b)))
                                act.wait_ge(sm["misc_full"], out_used(f, phase, s))
                                nc.scalar.copy(o_t[:, 0, 0:pcol], out_p[:, 0, 0:pcol]).then_inc(sm["ot_act"], 1)
                            if c in hk and hk[c][0] == "T":
                                z_high(f, hk[c][1], s, hk[c][2], use_at(f, phase, s, hk[c]))
                            piece = split_piece(f, phase, s, c)
                            if piece is not None:
                                weights_high(f, phase, s, c, piece)
                            act.wait_ge(sm["h_done"], s.at(lambda b: n(b) + 1))
                            if n(s.index) >= 2:
                                act.wait_ge(sm["down_done"], s.at(lambda b: n(b) - 1))
                            nc.scalar.copy(hh[:, par, 0:ncol], h_s[:, par, 0:ncol]).then_inc(sm["hh_done"], 1)

                    sweep(act, LEN[phase], period, body)
                    if phase == "s0":
                        act.wait_ge(sm["rt_rms"], 2 * f + 2)
                        nc.scalar.activation(pr[:, :, :], lg[:, :, :], ACT.Exp).then_inc(sm["rt_exp"], 1)
                    if phase == "s1":
                        z_high(f, "e", Step(0, 4), 0, use[(f, "T", "e", 0)])
                act.wait_ge(sm["down_done"], NCH * FB * (f + 1))
                act.wait_ge(sm["misc_full"], use[(f, "O", "e", NEB - 2)] + 1)
                nc.scalar.copy(o_t[:, 0, 0:EB], out_p[:, 0, 0:EB]).then_inc(sm["ot_act"], 1)

            def weights_high(f, phase, s, c, piece):
                n, j, buf = piece
                par = (s.mod if j is None else j) % 2
                if phase == "e":
                    v = s.at(lambda b: 48 * (piece_of(f, SU + b // 2 + 1, j) // 2 + 1))
                    u = s.at(lambda b: NCH * blk(f, "e", b // 2 * 2))
                else:
                    v = s.at(lambda b: 48 * (piece_of(f, 1 if phase == "s0" else 2, b) // 2 + 1))
                    u = NCH * blk(f, phase, 0)
                act.wait_ge(st_in[par], v)
                wait(act, sm["down_done"], u)
                if j is None:
                    dst = W[buf][:, 0, bass.ds(s.at(lambda b: b), 1), :].rearrange("p a c -> p (a c)") if s.reg is not None \
                        else W[buf][:, 0, s.index, :]
                else:
                    dst = W[buf][:, 0, j, :]
                nc.scalar.copy(dst, stage[:, par, :]).then_inc(sm["wh_done"], 1)

            def attention():
                act.wait_ge(sm["aw_in"], 48)
                nc.scalar.copy(aw[:, 0, :, :], aw_s[:, :, :]).then_inc(sm["aw_h"], 1)

                def tile(s):
                    n = lambda k: s.at(lambda b: b + k)
                    act.wait_ge(sm["a_t"], n(1))
                    nc.scalar.copy(azh[:, :, :], misc[:, 0, 0:C].rearrange("p (k c) -> p k c", k=KC)).then_inc(sm["a_zh"], 1)
                    act.wait_ge(sm["a_qkv"], n(1))
                    for j in range(2):
                        nc.scalar.activation(sqj[:, :], gate_p[:, 0, j * C:(j + 1) * C], ACT.Square,
                                             accum_out=ssq[:, j:j + 1]).then_inc(sm["a_sq"], 1)
                        act.wait_ge(sm["a_sq"], s.at(lambda b: 2 * b + j + 1))
                    for g in range(2):
                        for r in range(2):
                            src = gate_p[64 * g:64 * g + 64, 1, 0:C].rearrange("p (j r d) -> p j r d", r=2, d=HD)[:, :, r, :]
                            o = 32 * g + HD * r
                            last = nc.scalar.copy(vh[64 * r:64 * r + 64, :, o:o + HD], src)
                    last.then_inc(sm["a_vh"], 1)
                    act.wait_ge(sm["a_qn"], n(1))
                    q3 = qk[:, 0, :].rearrange("p (h d) -> p h d", d=HD)
                    k3 = qk[:, 1, :].rearrange("p (h d) -> p h d", d=HD)
                    r_ = lambda t: t.bitcast(F32R)
                    nc.scalar.copy(r_(qcat[:, :, 0:HD]), q3)
                    nc.scalar.copy(r_(qcat[:, :, HD:2 * HD]), q3)
                    nc.scalar.copy(r_(kcat[:, :, 0:HD]), k3)
                    nc.scalar.copy(r_(kcat[:, :, 2 * HD:3 * HD]), k3).then_inc(sm["a_qc"], 1)
                    act.wait_ge(sm["a_qt"], n(1))
                    nc.scalar.copy(q_t[:, :, :], misc[:, :, :].rearrange("p b (j c) -> p (b j) c", c=P)).then_inc(sm["a_qe"], 1)
                    act.wait_ge(sm["a_mk"], n(1))
                    nc.scalar.activation(p_s[:, :, :], s_s[:, :, :], ACT.Exp, scale=float(HD) ** -0.5).then_inc(sm["a_exp"], 1)
                    act.wait_ge(sm["a_pt"], n(1))
                    nc.scalar.copy(ph[:, :, :], misc[:, :, :].rearrange("p b (j c) -> p (b j) c", c=P)).then_inc(sm["a_ph"], 1)
                    act.wait_ge(sm["a_yt"], n(1))
                    nc.scalar.copy(yh[:, :, :], misc[:, 0, 0:C].rearrange("p (k c) -> p k c", k=KC)).then_inc(sm["a_yh"], 1)
                sweep(act, NT, 2, tile)

            for j in range(NCH):
                act.wait_ge(st_in[j % 2], 48 * (j // 2 + 1))
                nc.scalar.copy(w0[:, 0, j, :], stage[:, j % 2, :]).then_inc(sm["wh_done"], 1)
            act.wait_ge(sm["r_in"], 16 * KC)
            nc.scalar.copy(router[:, :, 0, :], router_s[:, :, :]).then_inc(sm["rt_in"], 1)
            ffn(0)
            attention()
            ffn(1)

        @block.vector
        def _(dve):
            v = nc.vector

            def ln(f, s, off):
                par = (s.mod + off) % 2
                nb = lambda b: b + off
                L = lambda k: s.at(lambda b: NB * f + nb(b) + k)
                if f == 0:
                    dve.wait_ge(x_l[par], s.at(lambda b: 16 * (nb(b) // 2 + 1)))
                elif s.first and off == 0:
                    dve.wait_ge(sm["a_o"], NT)
                xt = s.at(lambda b: BT * nb(b))
                for j in range(BT):
                    last = v.bn_stats(st[:, j, :], xtile(s, off, j))
                last.then_inc(sm["ln_st"], 1)
                dve.wait_ge(sm["ln_st"], L(1))
                v.tensor_tensor(lnd[:, :], st[:, :, 1], st[:, :, 4], ALU.subtract)
                v.tensor_tensor(lnm[:, :], st[:, :, 1], st[:, :, 4], ALU.add)
                v.tensor_tensor(lnv[:, :], st[:, :, 2], st[:, :, 5], ALU.add).then_inc(sm["ln_a"], 1)
                dve.wait_ge(sm["ln_a"], L(1))
                v.tensor_tensor(lndd[:, :], lnd[:, :], lnd[:, :], ALU.mult)
                v.tensor_scalar(mean[:, :], lnm[:, :], 0.5, None, ALU.mult).then_inc(sm["ln_b"], 1)
                dve.wait_ge(sm["ln_b"], L(1))
                v.scalar_tensor_tensor(out=lnv2[:, :], in0=lndd[:, :], scalar=C / 4.0, in1=lnv[:, :],
                                       op0=ALU.mult, op1=ALU.add).then_inc(sm["ln_c"], 1)
                dve.wait_ge(sm["ln_c"], L(1))
                cols = bass.ds(xt, BT)
                v.tensor_scalar(var[:, cols], lnv2[:, :], 1.0 / C, None, ALU.mult)
                v.tensor_scalar(vare[:, cols], lnv2[:, :], 1.0 / C, LN_EPS, ALU.mult, ALU.add).then_inc(sm["ln_var"], 1)

            def xtile(s, off, j):
                t = s.at(lambda b: BT * (b + off) + j)
                return x[:, bass.ds(t, 1), :].rearrange("p a c -> p (a c)")

            def ln_rows(f, s, off):
                par = (s.mod + off) % 2
                nb = lambda b: b + off
                dve.wait_ge(sm["ln_rstd"], s.at(lambda b: NB * f + nb(b) + 1))
                dve.wait_ge(zsv[par], s.at(lambda b: 48 * (NB // 2 * f + nb(b) // 2 + 1)))
                for j in range(BT):
                    t = s.at(lambda b: BT * nb(b) + j)
                    last = v.tensor_scalar(zn[:, par, j, :], xtile(s, off, j), mean[:, j:j + 1],
                                           rstd[:, bass.ds(t, 1)], ALU.subtract, ALU.mult)
                last.then_inc(sm["ln_z"], 1)

            def z_low(f, phase, s, off, m):
                par = (s.mod + off) % 2
                ncol = SB if phase == "s0" else EB
                if phase == "s0":
                    dve.wait_ge(sm["zh_done"], s.at(lambda b: (NB + NEB) * f + b + off + 1))
                else:
                    dve.wait_ge(sm["zh_done"], s.at(lambda b: (NB + NEB) * f + NB + b + off + 1))
                v.tensor_tensor(zl[:, par, :, 0:ncol], misc[:, :, 0:ncol], zh[:, par, :, 0:ncol],
                                ALU.subtract).then_inc(sm["misc_free"], 1)

            def meta(f, s, off):
                par, q = (s.mod + off) % 2, (s.mod + off) % 4
                nb = lambda b: b + off
                dve.wait_ge(xr_in[par], s.at(lambda b: 32 * (XB * f + nb(b) // 2 + 1)))
                dve.wait_ge(sm["sums_done"], s.at(lambda b: NEB * f + nb(b) + 2))
                col = s.at(lambda b: C + 1 + nb(b) // 2)
                for j, (at, rows) in enumerate(EPART):
                    v.tensor_copy(wmeta[0:rows, q, j:j + 1], xr[0:rows, par, j, bass.ds(col, 1)])
                    last = v.tensor_copy(tmeta[0:rows, q, j:j + 1], xr[0:rows, par, j, C:C + 1])
                last.then_inc(sm["meta_done"], 1)

            def logits(f, s, off, m):
                dve.wait_ge(sm["misc_full"], m + 1)
                t = s.at(lambda b: BT * (b + off))
                v.tensor_copy(lg[:, bass.ds(t, BT), :], misc[:, 0, 0:BT * E].rearrange("p (t e) -> p t e", e=E)).then_inc(sm["misc_free"], 1)

            def add_shared(f, phase, s, tile0, m):
                dve.wait_ge(sm["misc_full"], m + 1)
                xs = x[:, bass.ds(tile0, BT), :].rearrange("p t c -> p (t c)")
                v.scalar_tensor_tensor(out=xs, in0=misc[:, :, :].rearrange("p a b -> p (a b)"), scalar=0.5, in1=xs,
                                       op0=ALU.mult, op1=ALU.add).then_inc(sm["misc_free"], 1)

            def expert_rows(f, b_at, par, q, m):
                dve.wait_ge(sm["misc_full"], m + 1)
                dve.wait_ge(sm["sums_done"], b_at(lambda b: NEB * f + b + 4))
                for j, (at, rows) in enumerate(EPART):
                    o = (j % 2) * C
                    last = v.tensor_scalar(eo[0:rows, par, j, :], misc[0:rows, j // 2, o:o + C], wmeta[0:rows, q, j:j + 1],
                                           0.5, ALU.mult, ALU.mult)
                last.then_inc(sm["misc_free"], 1)

            def weights_low(f, phase, s, c, piece):
                n, j, buf = piece
                par = (s.mod if j is None else j) % 2
                dve.wait_ge(sm["wh_done"], s.at(lambda b: (piece_of(f, 1 if phase == 's0' else 2, b) if j is None else piece_of(f, SU + b // 2 + 1, j)) + 1))
                if j is None:
                    jj = bass.ds(s.at(lambda b: b), 1)
                    hi = W[buf][:, 0, jj, :].rearrange("p a c -> p (a c)")
                    lo = W[buf][:, 1, jj, :].rearrange("p a c -> p (a c)")
                else:
                    hi, lo = W[buf][:, 0, j, :], W[buf][:, 1, j, :]
                v.tensor_tensor(lo, stage[:, par, :], hi, ALU.subtract).then_inc(sm["wl_done"], 1)

            def route(f):
                k = [0]

                def then(ins):
                    k[0] += 1
                    ins.then_inc(sm["rt"], 1)
                    dve.wait_ge(sm["rt"], RT * f + k[0])

                bc = lambda t: t[:, :].unsqueeze(2).broadcast_to([P, NT, E])
                TT, TS = v.tensor_tensor, v.tensor_scalar
                a = [P, NT, E]
                then(TT(ra[:, :], rstd[:, :], rstd[:, :], ALU.mult))
                then(TT(ra[:, :], ra[:, :], var[:, :], ALU.mult))
                v.tensor_scalar(ra[:, :], ra[:, :], ROUTER_EPS, None, ALU.add).then_inc(sm["rt_rms"], 1)
                dve.wait_ge(sm["rt_rs"], f + 1)
                then(TT(lg[:, :, :], lg[:, :, :], bc(rb), ALU.mult))
                then(v.tensor_reduce(m1[:, :], lg[:, :, :], AX, ALU.max))
                TT(lg[:, :, :], lg[:, :, :], bc(m1), ALU.subtract).then_inc(sm["rt_rms"], 1)
                dve.wait_ge(sm["rt_exp"], f + 1)
                then(v.tensor_reduce(ra[:, :], pr[:, :, :], AX, ALU.add))
                then(v.reciprocal(rb[:, :], ra[:, :]))
                then(TT(pr[:, :, :], pr[:, :, :], bc(rb), ALU.mult))
                for c, best in enumerate((m1, m2)):
                    then(v.tensor_reduce(best[:, :], pr[:, :, :], AX, ALU.max))
                    then(TT(pick[:, :, :], pr[:, :, :], bc(best), ALU.is_equal))
                    then(TT(pick[:, :, :], pick[:, :, :], prio[:, :, :], ALU.mult))
                    then(v.tensor_reduce(ra[:, :], pick[:, :, :], AX, ALU.max))
                    then(TT(oh[:, c, :, :], pick[:, :, :], bc(ra), ALU.is_equal))
                    if c == 0:
                        then(v.scalar_tensor_tensor(out=pr[:, :, :], in0=oh[:, 0, :, :], scalar=-2.0, in1=pr[:, :, :],
                                                    op0=ALU.mult, op1=ALU.add))
                TT(mask[:, :, :], oh[:, 0, :, :], oh[:, 1, :, :], ALU.add).then_inc(sm["rt_mask"], 1)
                then(TT(ra[:, :], m1[:, :], m2[:, :], ALU.add))
                then(v.reciprocal(rb[:, :], ra[:, :]))
                TT(m1[:, :], m1[:, :], rb[:, :], ALU.mult)
                then(TT(m2[:, :], m2[:, :], rb[:, :], ALU.mult))
                TT(lg[:, :, :], oh[:, 0, :, :], bc(m1), ALU.mult)
                then(TT(pick[:, :, :], oh[:, 1, :, :], bc(m2), ALU.mult))
                then(TT(table[:, :, 1:1 + E], lg[:, :, :], pick[:, :, :], ALU.add))
                dve.wait_ge(sm["misc_full"], use[(f, "M", "s0", 0)] + 1)
                v.tensor_copy(pick[:, :, :], misc[:, 1, 0:NT * E].rearrange("p (t e) -> p t e", e=E))
                then(v.tensor_copy(lg[:, :, :], misc[:, 0, 0:NT * E].rearrange("p (t e) -> p t e", e=E)))
                for e in range(E):
                    last = v.tensor_tensor_scan(pr[:, :, e], one_row[:, :], pick[:, :, e], 0.0, ALU.mult, ALU.add)
                then(last)
                then(TT(lg[:, :, :], lg[:, :, :], pr[:, :, :], ALU.add))
                TT(lg[:, :, :], lg[:, :, :], pick[:, :, :], ALU.subtract).then_inc(sm["misc_free"], 1)
                dve.wait_ge(sm["misc_free"], use[(f, "M", "s0", 0)] + 1)
                then(TS(pick[:, :, :], lg[:, :, :], float(CAP), FAR, ALU.is_ge, ALU.mult))
                then(TT(lg[:, :, :], lg[:, :, :], pick[:, :, :], ALU.add))
                then(TT(lg[:, :, :], lg[:, :, :], base[:, :, :], ALU.add))
                for c in range(TOPK):
                    then(TT(pick[:, :, :], oh[:, c, :, :], lg[:, :, :], ALU.mult))
                    then(v.tensor_reduce(ra[:, :], pick[:, :, :], AX, ALU.add))
                    then(v.tensor_copy(slot_i[:, c, :], ra[:, :]))
                assert k[0] == RT, k[0]

            def ffn(f):
                s0 = Step(0, 2)
                ln(f, s0, 0)
                ln_rows(f, s0, 0)
                z_low(f, "s0", s0, 0, use[(f, "T", "s0", 0)])
                if f == 0:
                    dve.wait_ge(sm["rt_in"], 1)
                    v.tensor_tensor(router[:, :, 1, :], router_s[:, :, :], router[:, :, 0, :], ALU.subtract).then_inc(sm["rt_in"], 1)
                logits(f, s0, 0, use[(f, "R", "s0", 0)])
                for phase in ("s0", "s1", "e"):
                    period = 4 if phase == "e" else 2
                    ncol = EB if phase == "e" else SB

                    def body(s, phase=phase, ncol=ncol):
                        hk = hooks(f, phase, s)
                        last = s.reg is None and s.index == LEN[phase] - 1
                        for c in range(NCH):
                            par = c % 2
                            n = lambda b: NCH * blk(f, phase, b) + c
                            dve.wait_ge(sm["silu_done"], s.at(lambda b: n(b) + 1))
                            dve.wait_ge(sm["up_full"], s.at(lambda b: n(b) + 1))
                            v.tensor_tensor(h_s[:, par, 0:ncol], up_p[:, par, 0:ncol], sg_s[:, par, 0:ncol],
                                            ALU.mult).then_inc(sm["h_done"], 1)
                            if c == 0 and not (phase == "s0" and s.first):
                                pcol = ncol if not s.first else SB
                                dve.wait_ge(sm["down_done"], s.at(lambda b: NCH * blk(f, phase, b)))
                                dve.wait_ge(sm["misc_full"], out_used(f, phase, s))
                                v.tensor_copy(o_t[:, 1, 0:pcol], out_p[:, 1, 0:pcol]).then_inc(sm["ot_dve"], 1)
                            if phase == "s0" and not last and c == 1:
                                ln(f, s, 1)
                            if phase == "s0" and not last and c == 2:
                                ln_rows(f, s, 1)
                            if phase == "e" and not last and c == 3:
                                meta(f, s, 1)
                            piece = split_piece(f, phase, s, c)
                            if piece is not None:
                                weights_low(f, phase, s, c, piece)
                            if c in hk:
                                what, ph2, off = hk[c]
                                m = use_at(f, phase, s, hk[c])
                                if what == "T":
                                    z_low(f, ph2, s, off, m)
                                elif what == "R":
                                    logits(f, s, off, m)
                                elif ph2 == "e":
                                    expert_rows(f, lambda g: s.at(lambda b: g(b - 1)), (s.mod - 1) % 2, (s.mod - 1) % 4, m)
                                else:
                                    t0 = BT * off if off > 0 else s.at(lambda b: BT * (b - 1))
                                    add_shared(f, ph2, s, t0, m)
                            dve.wait_ge(sm["hh_done"], s.at(lambda b: n(b) + 1))
                            v.tensor_tensor(hl[:, par, 0:ncol], h_s[:, par, 0:ncol], hh[:, par, 0:ncol],
                                            ALU.subtract).then_inc(sm["hl_done"], 1)

                    sweep(dve, LEN[phase], period, body)
                    if phase == "s0":
                        route(f)
                    if phase == "s1":
                        meta(f, Step(0, 4), 0)
                        z_low(f, "e", Step(0, 4), 0, use[(f, "T", "e", 0)])
                dve.wait_ge(sm["down_done"], NCH * FB * (f + 1))
                dve.wait_ge(sm["misc_full"], use[(f, "O", "e", NEB - 2)] + 1)
                v.tensor_copy(o_t[:, 1, 0:EB], out_p[:, 1, 0:EB]).then_inc(sm["ot_dve"], 1)
                expert_rows(f, lambda g: g(NEB - 1), 1, 3, use[(f, "O", "e", NEB - 1)])

            def attention():
                for par in range(2):
                    dve.wait_ge(x_l[par], 16 * NB)
                dve.wait_ge(sm["aw_h"], 1)
                v.tensor_tensor(aw[:, 1, :, :], aw_s[:, :, :], aw[:, 0, :, :], ALU.subtract).then_inc(sm["aw_l"], 1)
                v.memset(qcat[:, :, :], 0.0)
                v.memset(kcat[:, :, :], 0.0)
                v.memset(vh[:, :, :].bitcast(F32), 0.0)
                v.memset(vl[:, :, :].bitcast(F32), 0.0).then_inc(sm["a_const"], 1)
                dve.wait_ge(sm["a_const"], 1)
                for r in range(2):
                    v.memset(vh[64 * r:64 * r + 64, :, 64 + r:65 + r].bitcast(F32), 1.0).then_inc(sm["a_const"], 1)

                def tile(s):
                    n = lambda k: s.at(lambda b: b + k)
                    a = lambda k: s.at(lambda b: AV * b + k)
                    t = s.at(lambda b: b)
                    xt = x[:, bass.ds(t, 1), :].rearrange("p a c -> p (a c)")
                    v.bn_stats(ast[:, 0:6], xt).then_inc(sm["av"], 1)
                    dve.wait_ge(sm["av"], a(1))
                    dve.sem_inc(sm["dve_step"], 1)
                    v.bn_aggr(alv[:, :], ast[:, 0:6]).then_inc(sm["av"], 1)
                    dve.wait_ge(sm["av"], a(2))
                    v.tensor_scalar(ast[:, 6:7], alv[:, 1:2], LN_EPS, None, ALU.add).then_inc(sm["av"], 1)
                    dve.wait_ge(sm["apool"], s.at(lambda b: 2 * b + 1))
                    v.tensor_scalar(azn[:, :], xt, alv[:, 0:1], ard[:, 0:1], ALU.subtract, ALU.mult).then_inc(sm["av"], 1)
                    dve.wait_ge(sm["a_zh"], n(1))
                    v.tensor_tensor(azl[:, :, :], misc[:, 0, 0:C].rearrange("p (k c) -> p k c", k=KC), azh[:, :, :],
                                    ALU.subtract).then_inc(sm["a_zl"], 1)
                    dve.wait_ge(sm["a_sq"], s.at(lambda b: 2 * b + 2))
                    v.tensor_scalar(qke[:, :], ssq[:, :], 1.0 / C, RMS_EPS, ALU.mult, ALU.add).then_inc(sm["av"], 1)
                    dve.wait_ge(sm["apool"], s.at(lambda b: 2 * b + 2))
                    for j in range(2):
                        last = v.scalar_tensor_tensor(out=qk[:, j, :], in0=gate_p[:, 0, j * C:(j + 1) * C], scalar=qkr[:, j:j + 1],
                                                      in1=lnw[:, :], op0=ALU.mult, op1=ALU.mult)
                    last.then_inc(sm["a_qn"], 1)
                    dve.wait_ge(sm["a_vh"], n(1))
                    for g in range(2):
                        for r in range(2):
                            src = gate_p[64 * g:64 * g + 64, 1, 0:C].rearrange("p (j r d) -> p j r d", r=2, d=HD)[:, :, r, :]
                            o = 32 * g + HD * r
                            rows = slice(64 * r, 64 * r + 64)
                            last = v.tensor_tensor(vl[rows, :, o:o + HD], src, vh[rows, :, o:o + HD], ALU.subtract)
                    last.then_inc(sm["a_vl"], 1)
                    dve.wait_ge(sm["a_qc"], n(1))
                    q3 = qk[:, 0, :].rearrange("p (h d) -> p h d", d=HD)
                    k3 = qk[:, 1, :].rearrange("p (h d) -> p h d", d=HD)
                    v.tensor_tensor(qcat[:, :, 2 * HD:3 * HD].bitcast(F32R), q3, qcat[:, :, 0:HD], ALU.subtract)
                    v.tensor_tensor(kcat[:, :, HD:2 * HD].bitcast(F32R), k3, kcat[:, :, 0:HD], ALU.subtract).then_inc(sm["a_qlo"], 1)
                    dve.wait_ge(sm["a_kt"], n(1))
                    v.tensor_copy(k_t[:, :, :], misc[:, :, :].rearrange("p b (j c) -> p (b j) c", c=P)).then_inc(sm["a_ke"], 1)
                    dve.wait_ge(sm["a_s"], n(1))
                    for r, bank in ((0, up_p), (1, out_p)):
                        for g in range(2):
                            rows = slice(64 * g, 64 * g + 64)
                            src = bank[rows, :, :].rearrange("p b (j c) -> p (b j) c", c=P)[:, :, 64 * g:64 * g + 64]
                            dst = s_s[rows, :, :].rearrange("p (j r) c -> p j r c", r=2)[:, :, r, :]
                            last = v.tensor_tensor(dst, src, causal[rows, rows].unsqueeze(1).broadcast_to([64, NH // 2, GROUP]), ALU.add)
                    last.then_inc(sm["a_masked"], 1)
                    dve.wait_ge(sm["a_masked"], n(1))
                    v.tensor_reduce(smax[:, :], s_s[:, :, :], AX, ALU.max).then_inc(sm["a_max"], 1)
                    dve.wait_ge(sm["a_max"], n(1))
                    v.tensor_tensor(s_s[:, :, :], s_s[:, :, :], smax[:, :].unsqueeze(2).broadcast_to([P, NH, GROUP]),
                                    ALU.subtract).then_inc(sm["a_mk"], 1)
                    dve.wait_ge(sm["a_ph"], n(1))
                    v.tensor_tensor(pl[:, :, :], misc[:, :, :].rearrange("p b (j c) -> p (b j) c", c=P), ph[:, :, :],
                                    ALU.subtract).then_inc(sm["a_pl"], 1)
                    dve.wait_ge(sm["a_y"], n(1))
                    yp = gate_p[:, :, 0:4 * 66].rearrange("p b (j c) -> p b j c", c=66)
                    rd4 = rden[:, :].rearrange("p (b j r) -> p b j r", b=2, r=2)
                    for b in range(2):
                        last = v.reciprocal(rd4[:, b, :, :], yp[:, b, :, 64:66])
                    last.then_inc(sm["a_rden"], 1)
                    dve.wait_ge(sm["a_rden"], n(1))
                    for g in range(2):
                        rows = slice(64 * g, 64 * g + 64)
                        for b in range(2):
                            src = yp[rows, b, :, 32 * g:32 * g + 32].rearrange("p j (r d) -> p j r d", d=HD)
                            dst = y_s[rows, :].rearrange("p (b j r d) -> p b j r d", b=2, r=2, d=HD)[:, b]
                            last = v.tensor_tensor(dst, src, rd4[rows, b].unsqueeze(3).broadcast_to([64, 4, 2, HD]), ALU.mult)
                    last.then_inc(sm["a_yn"], 1)
                    dve.wait_ge(sm["a_yh"], n(1))
                    v.tensor_tensor(yl[:, :, :], misc[:, 0, 0:C].rearrange("p (k c) -> p k c", k=KC), yh[:, :, :],
                                    ALU.subtract).then_inc(sm["a_yl"], 1)
                    dve.wait_ge(sm["a_x"], n(1))
                    v.tensor_tensor(xt, misc[:, 1, 0:C], xt, ALU.add).then_inc(sm["a_o"], 1)
                sweep(dve, NT, 2, tile)

            v.memset(ones[:, :].bitcast(F32), 1.0)
            v.memset(mhalf[:, :], -0.5)
            v.memset(one_row[:, :], 1.0)
            dve.wait_ge(sm["pool_const"], POOL_CONSTS)
            v.tensor_copy(below[:, :], below_s[:, :]).then_inc(sm["const"], 1)
            for j in range(NCH):
                dve.wait_ge(sm["wh_done"], j + 1)
                v.tensor_tensor(w0[:, 1, j, :], stage[:, j % 2, :], w0[:, 0, j, :], ALU.subtract).then_inc(sm["wl_done"], 1)
            ffn(0)
            attention()
            ffn(1)

        @block.gpsimd
        def _(pool):
            g = nc.gpsimd

            def after(*counts):
                for semaphore, value in counts:
                    pool.wait_ge(semaphore, value)
                pool.sem_inc(sm["pool_step"], 1)

            k = [0]
            whole = pick[:, :, :].rearrange("p t e -> p (t e)").bitcast(I32)

            def then(ins):
                k[0] += 1
                ins.then_inc(sm["pool_const"], 1)
                pool.wait_ge(sm["pool_const"], k[0])

            g.memset(ident[:, :], 0.0)
            g.memset(below_s[:, :], 1.0)
            g.memset(causal[:, :], 0.0)
            then(g.memset(empty[:, :], 0.0))
            g.affine_select(out=ident[:, :], in_=ident[:, :], compare_op=ALU.not_equal, fill=1.0, base=0,
                            pattern=[[-1, P]], channel_multiplier=1)
            g.affine_select(out=below_s[:, :], in_=below_s[:, :], compare_op=ALU.is_gt, fill=0.0, base=0,
                            pattern=[[1, P]], channel_multiplier=-1)
            g.affine_select(out=causal[:, :], in_=causal[:, :], compare_op=ALU.is_ge, fill=-3.0e38, base=0,
                            pattern=[[-1, P]], channel_multiplier=1)
            then(g.iota(whole[:, 0:1], pattern=[[0, 1]], base=T, channel_multiplier=1))
            then(g.tensor_copy(empty[:, C:C + 1], whole[:, 0:1]))
            for dst, args in ((table[:, :, 0], dict(pattern=[[P, NT]], base=0, channel_multiplier=1)),
                              (prio[:, :, :], dict(pattern=[[0, NT], [-1, E]], base=E, channel_multiplier=0)),
                              (base[:, :, :], dict(pattern=[[0, NT], [CAP, E]], base=0, channel_multiplier=0))):
                n = NT if dst is table[:, :, 0] or len(args["pattern"]) == 1 else NT * E
                src = whole[:, 0:n] if n == NT else whole.rearrange("p (t e) -> p t e", e=E)
                then(g.iota(src, **args))
                then(g.tensor_copy(dst, src))
            assert k[0] == POOL_CONSTS, k[0]
            pool.sem_inc(sm["sums_done"], 4)

            def ln(f):
                def body(s):
                    after((sm["ln_var"], s.at(lambda b: NB * f + b + 1)))
                    cols = bass.ds(s.at(lambda b: BT * b), BT)
                    g.tensor_tensor(rstd[:, cols], vare[:, cols], mhalf[:, 0:BT], ALU.pow).then_inc(sm["ln_rstd"], 1)
                sweep(pool, NB, 2, body)

            def scatter(f):
                def body(s):
                    par = s.mod % 2
                    w = s.at(lambda t: 32 * (NT // 2 * f + t // 2))
                    if not isinstance(w, int) or w:
                        after((scat[par], w))
                    t = s.at(lambda t: t)
                    g.dma_start(srow[:, par, 0:C], zn_rows[:, bass.ds(t, 1), :].rearrange("p a c -> p (a c)")).then_inc(sr_in[par], 16)
                    g.tensor_copy(srow[:, par, C:ROW], table[:, bass.ds(t, 1), :].rearrange("p a c -> p (a c)"))
                    g.tensor_copy(sidx[:, par, :], slot_i[:, :, bass.ds(t, 1)].rearrange("p a c -> p (a c)")).then_inc(sm["sidx_in"], 1)
                    after((sr_in[par], s.at(lambda t: 16 * (NT // 2 * f + t // 2 + 1))),
                          (sm["sidx_in"], s.at(lambda t: NT * f + t + 1)))
                    for c in range(TOPK):
                        g.indirect_dma_start(out=slots_d[f], out_offset=bass.IndirectOffsetOnAxis(ap=sidx[:, par, c:c + 1], axis=0),
                                             in_=srow[:, par, :], in_offset=None, bounds_check=E * CAP - 1,
                                             oob_is_err=False).then_inc(scat[par], 16)
                sweep(pool, NT, 2, body, head=3)

            def expert_sums(f):
                def body(s):
                    par, q = s.mod % 2, s.mod
                    w = s.at(lambda b: 48 * (XB * f + (b + 1) // 2))
                    wait(pool, sadd[1 - par], w)
                    pool.sem_inc(sm["sums_done"], 1)
                    after((sm["misc_free"], s.at(lambda b: use[(f, "O", "e", b)] + 1)))
                    for j, (at, rows) in enumerate(EPART):
                        g.indirect_dma_start(out=y_d[f], out_offset=bass.IndirectOffsetOnAxis(ap=tmeta[0:rows, q, j:j + 1], axis=0),
                                             in_=eo[0:rows, par, j, :], in_offset=None, bounds_check=T + P - 1,
                                             compute_op=ALU.add).then_inc(sadd[par], 16)
                sweep(pool, NEB, 4, body)

            for f in range(2):
                ln(f)
                pool.wait_ge(sm["rt_rms"], 2 * f + 1)
                g.tensor_tensor(rb[:, :], ra[:, :], mhalf[:, :], ALU.pow).then_inc(sm["rt_rs"], 1)
                pool.wait_ge(sm["rt"], RT * (f + 1))
                for par in range(2):
                    pool.wait_ge(zsv[par], 48 * (NB // 2 * (f + 1) + 1))
                pool.wait_ge(sm["init"], 64)
                scatter(f)
                for par in range(2):
                    pool.wait_ge(y_sv[par], 16 * NB // 2 * (f + 1))
                expert_sums(f)
                if f == 0:
                    def tile(s):
                        after((sm["av"], s.at(lambda b: AV * b + 3)))
                        g.tensor_tensor(ard[:, :], ast[:, 6:7], mhalf[:, 0:1], ALU.pow).then_inc(sm["apool"], 1)
                        after((sm["av"], s.at(lambda b: AV * b + 5)))
                        g.tensor_tensor(qkr[:, :], qke[:, :], mhalf[:, 0:2], ALU.pow).then_inc(sm["apool"], 1)
                    sweep(pool, NT, 2, tile)

        @block.sync
        def _(sp):
            def hold(semaphore, value):
                sp.wait_ge(semaphore, value)
                if not isinstance(value, int):
                    sp.sem_inc(sm["sp_step"], 1)

            def load_x(src, b, f):
                wait(sp, x_l[b % 2], 16 * (NB // 2 * f + b // 2))
                sp.dma_start(x[:, BT * b:BT * b + BT, :], src[:, BT * b:BT * b + BT, :]).then_inc(x_l[b % 2], 16)

            def load_piece(par, n, gate, up, down):
                st_ = stage[:, par, :]
                sp.dma_start(st_[:, 0:KC * P].rearrange("p (k i) -> p k i", k=KC), gate).then_inc(st_in[par], 16)
                sp.dma_start(st_[:, KC * P:2 * KC * P].rearrange("p (k i) -> p k i", k=KC), up).then_inc(st_in[par], 16)
                sp.dma_start(st_[:, 2 * KC * P:PIECE], down).then_inc(st_in[par], 16)

            def shared_piece(u, j):
                i0 = u * NCH + j
                view = lambda w: w.rearrange("(k p) i -> p k i", p=P)[:, :, bass.ds(i0 * P, P)]
                return view(sg), view(su), sd.rearrange("(i p) c -> p i c", p=P)[:, bass.ds(i0, 1), :].rearrange("p a c -> p (a c)")

            def expert_piece(e, j):
                view = lambda w: w.rearrange("e (k p) i -> p (e k) i", p=P)[:, bass.ds(e * KC, KC), j * P:(j + 1) * P]
                return view(rg), view(ru), rd.rearrange("e (i p) c -> p (e i) c", p=P)[:, bass.ds(e * NCH + j, 1), :].rearrange("p a c -> p (a c)")

            def ffn(f):
                for phase in ("s0", "s1", "e"):
                    def body(s, phase=phase):
                        last = s.reg is None and s.index == LEN[phase] - 1
                        if phase == "s0":
                            u = 1
                            hold(sm["wl_done"], s.at(lambda b: piece_of(f, u, b) - 1))
                            load_piece(s.mod % 2, None, *shared_piece(u, s.at(lambda b: b)))
                            if not last:
                                save_z(f, s, 1)
                        elif phase == "s1":
                            if not last:
                                load_z(f, s, 1)
                            hold(sm["wl_done"], s.at(lambda b: piece_of(f, 2, b) - 1))
                            load_piece(s.mod % 2, None, *expert_piece_at(s))
                            if not s.first:
                                save_x(f, s.at(lambda b: use[(f, "O", "s1", b - 1)] + 1), s.at(lambda b: b - 1), (s.mod - 1) % 2)
                        else:
                            if not (s.reg is None and s.index >= NEB - 2):
                                load_rows(f, s, 2)
                            half = s.index % 2
                            for jj in range(4):
                                j = 4 * half + jj
                                if s.reg is None and s.index >= NEB - 2:
                                    if f == 0:
                                        hold(sm["wl_done"], piece_of(1, 0, j) - 1)
                                        load_piece(j % 2, None, *shared_piece(0, j))
                                    continue
                                hold(sm["wl_done"], s.at(lambda b: piece_of(f, SU + b // 2 + 1, j) - 1))
                                load_piece(j % 2, None, *expert_piece(s.at(lambda b: b // 2 + 1), j))
                                if s.first and jj == 0:
                                    save_x(f, use[(f, "O", "s1", NB - 1)] + 1, NB - 1, 1)
                    sweep(sp, LEN[phase], 4 if phase == "e" else 2, body, tail=2 if phase == "e" else 0)
                    if phase == "s0":
                        load_z(f, Step(0, 2), 0)
                    if phase == "s1":
                        for par in range(2):
                            hold(scat[par], 32 * (NT // 2 * (f + 1)))
                        load_rows(f, Step(0, 4), 0)
                        load_rows(f, Step(1, 4), 0)

            def expert_piece_at(s):
                j = s.at(lambda b: b)
                view = lambda w: w[0, :, :].rearrange("(k p) i -> p k i", p=P)[:, :, bass.ds(j * P, P)]
                return view(rg), view(ru), rd[0, :, :].rearrange("(i p) c -> p i c", p=P)[:, bass.ds(j, 1), :].rearrange("p a c -> p (a c)")

            def save_z(f, s, off):
                par = (s.mod + off) % 2
                b_ = s.at(lambda b: b + off)
                hold(sm["misc_free"], s.at(lambda b: use[(f, "T", "s0", b + off)] + 1))
                cols = bass.ds(b_ * SB, SB)
                sp.dma_start(zh_d[:, :, cols], zh[:, par, :, :].bitcast(F32)).then_inc(zsv[par], 16)
                sp.dma_start(zl_d[:, :, cols], zl[:, par, :, :].bitcast(F32)).then_inc(zsv[par], 16)
                sp.dma_start(zn_rows[:, bass.ds(b_ * BT, BT), :], zn[:, par, :, :]).then_inc(zsv[par], 16)

            def load_z(f, s, off):
                par = (s.mod + off) % 2
                hold(sm["up_full"], s.at(lambda b: NCH * (blk(f, "s1", b + off) - 1)))
                if s.first and off == 0:
                    for q in zsv:
                        hold(q, 48 * (NB // 2 * (f + 1) + 1))
                cols = bass.ds(s.at(lambda b: (b + off) * SB), SB)
                sp.dma_start(zh[:, par, :, :].bitcast(F32), zh_d[:, :, cols]).then_inc(zin[par], 16)
                sp.dma_start(zl[:, par, :, :].bitcast(F32), zl_d[:, :, cols]).then_inc(zin[par], 16)

            def load_rows(f, s, off):
                par = (s.mod + off) % 2
                if off:
                    hold(sm["misc_free"], s.at(lambda b: use[(f, "T", "e", b)] + 1))
                    hold(sm["meta_done"], s.at(lambda b: NEB * f + b + 1))
                at = s.at(lambda b: EB * (b + off))
                sp.dma_start(xr[:, par, 0:2, :], slots_d[f][bass.ds(at, 2 * P), :].rearrange("(j p) c -> p j c", p=P)).then_inc(xr_in[par], 16)
                sp.dma_start(xr[0:EB - 2 * P, par, 2, :], slots_d[f][bass.ds(at + 2 * P, EB - 2 * P), :]).then_inc(xr_in[par], 16)

            def save_x(f, count, b, par):
                hold(sm["misc_free"], count)
                t = bass.ds(b * BT, BT)
                sp.dma_start(y_rows[f][:, t, :], x[:, t, :]).then_inc(y_sv[par], 16)

            for q in zsv:
                sp.sem_inc(q, 48)
            load_x(x_rows, 0, 0)
            load_x(x_rows, 1, 0)
            for kk in range(KC):
                sp.dma_start(router_s[:, kk, :], router_w[:, kk * P:(kk + 1) * P].rearrange("e p -> p e"),
                             allow_slow_non_contiguous=True).then_inc(sm["r_in"], 16)
            for j in range(NCH):
                wait(sp, sm["wl_done"], j - 1)
                load_piece(j % 2, None, *shared_piece(0, j))
                if j < NB - 2:
                    load_x(x_rows, j + 2, 0)
            hold(sm["pool_const"], POOL_CONSTS)
            for f in range(2):
                sp.dma_start(slots_d[f].rearrange("(t p) c -> p t c", p=P),
                             empty[:, :].unsqueeze(1).broadcast_to([P, E * CAP // P, ROW])).then_inc(sm["init"], 16)
                sp.dma_start(y_d[f][T:T + P, :], empty[:, 0:C]).then_inc(sm["init"], 16)
            save_z(0, Step(0, 2), 0)
            ffn(0)
            for par in range(2):
                hold(sadd[par], 48 * XB)
            sp.dma_start(aw_s[:, :, 0:3 * C], w_qkv.rearrange("(k p) d -> p k d", p=P)).then_inc(sm["aw_in"], 16)
            sp.dma_start(aw_s[:, :, 3 * C:4 * C], w_proj.rearrange("(k p) d -> p k d", p=P)).then_inc(sm["aw_in"], 16)
            sp.dma_start(lnw[:, :], ln_w.rearrange("(a c) -> a c", a=1).broadcast_to([P, C])).then_inc(sm["aw_in"], 16)
            for b in range(NB):
                load_x(y_rows[0], b, 1)
            save_z(1, Step(0, 2), 0)
            ffn(1)
            for par in range(2):
                hold(sadd[par], 48 * 2 * XB)
            sp.dma_start(out_rows.rearrange("(p a) c -> p (a c)", p=P),
                         y_d[1][0:T, :].rearrange("(p a) c -> p (a c)", p=P)).then_inc(sm["out_done"], 16)
            hold(sm["out_done"], 16)


_INS = ["L0_attn_x", "L0_attn_w_qkv", "L0_attn_ln_w", "L0_attn_w_proj", "L0_ffn_router_w", "L0_ffn_rg", "L0_ffn_ru",
        "L0_ffn_rd", "L0_ffn_sg", "L0_ffn_su", "L0_ffn_sd"]
_OUT = ((2, 2048, 256), "float32")


def kernel(**inputs):
    import numpy as np
    import concourse.bacc as bacc
    from concourse.bass_utils import run_bass_kernel_spmd

    nc = bacc.Bacc("TRN2", target_bir_lowering=False, num_devices=1)
    arrays, args = {}, []
    for name in _INS:
        a = np.ascontiguousarray(inputs[name])
        arrays[f"in_{name}"] = a
        args.append(nc.dram_tensor(f"in_{name}", a.shape, mybir.dt.from_np(a.dtype), kind="ExternalInput").ap())
    shape, dtype = _OUT
    args.append(nc.dram_tensor("out_dram", shape, mybir.dt.from_np(np.dtype(dtype)), kind="ExternalOutput").ap())
    program(nc, *args)
    r = run_bass_kernel_spmd(nc, [arrays], core_ids=[0])
    return r.results[0]["out_dram"]
```

```python
from contextlib import ExitStack

import concourse.bass as bass
from concourse import mybir

F32 = mybir.dt.float32
F32R = mybir.dt.float32r
I32 = mybir.dt.int32
ALU = mybir.AluOpType
ACT = mybir.ActivationFunctionType
AX = mybir.AxisListType.X

P = 128
LN_EPS = 1e-5
RMS_EPS = 1e-6
ROUTER_EPS = 2.0 ** -23
FAR = 1.0e6
GROUP = 64
HD = 16


class Step:

    def __init__(self, index, period, reg=None, count=0):
        self.index, self.period, self.reg, self.count = index, period, reg, count
        self.first = index == 0
        self.mod = index % period

    def shift(self, k, n):
        if self.reg is None:
            return Step(self.index + k, self.period) if 0 <= self.index + k < n else None
        assert 0 <= self.index + k and self.index + k + self.period * (self.count - 1) < n
        return Step(self.index + k, self.period, self.reg, self.count)

    def at(self, f):
        if self.reg is None:
            return f(self.index)
        v = [f(self.index + self.period * n) for n in range(self.count)]
        slope = v[1] - v[0] if self.count > 1 else 0
        assert all(v[n] == v[0] + n * slope for n in range(self.count))
        return v[0] if slope == 0 else self.reg * slope + v[0]


def wait(eng, semaphore, value):
    if not isinstance(value, int) or value > 0:
        eng.wait_ge(semaphore, value)


def sweep(eng, n, period, body, head=1, tail=0):
    for b in range(head):
        body(Step(b, period))
    count = (n - head - tail) // period
    done = head
    if count > 1:
        with eng.Fori(0, count) as i:
            for r in range(period):
                body(Step(head + r, period, i, count))
        done += period * count
    for b in range(done, n):
        body(Step(b, period))


def program(nc, x_in, w_qkv, ln_w, w_proj, router_w, rg, ru, rd, sg, su, sd, out):
    B, S, C = x_in.shape
    T = B * S
    E = router_w.shape[0]
    I = rg.shape[2]
    SU = sg.shape[1] // I
    TOPK = 2
    CAP = int(1.25 * T / E)
    KC = C // P
    NCH = I // P
    NT = T // P
    BT = 512 // P
    NB = T // 512
    SB = 512
    EB = CAP // 2
    NEB = 2 * E
    NH = C // HD
    assert C == 256 and KC == 2 and I == 1024 and SU == 2 and NCH == 8 and EB == 320 and NB == 8
    PIECE = 2 * KC * P + C
    ROW = C + 1 + E
    EPART = [(0, 128), (128, 128), (256, 64)]
    UNITS = SU + E
    FB = SU * NB + NEB

    x_rows = x_in.rearrange("b s c -> (b s) c").rearrange("(t p) c -> p t c", p=P)
    out_rows = out.rearrange("b s c -> (b s) c")

    with ExitStack() as ctx:
        def dram(name, shape, dt):
            return nc.dram_tensor(name, shape, dt, kind="Internal").ap()

        def sb(name, shape, dt, on=ctx):
            return on.enter_context(nc.sbuf_tensor(name, shape, dt))

        def psum(name, shape):
            return ctx.enter_context(nc.psum_tensor(name, shape, F32))

        def sem(name):
            return ctx.enter_context(nc.semaphore(name))

        zh_d = dram("zh_d", [P, KC, T], F32)
        zl_d = dram("zl_d", [P, KC, T], F32)
        zn_d = dram("zn_d", [T, C], F32)
        slots_d = [dram(f"slots{f}_d", [E * CAP, ROW], F32) for f in range(2)]
        y_d = [dram(f"y{f}_d", [T + P, C], F32) for f in range(2)]
        zn_rows = zn_d.rearrange("(t p) c -> p t c", p=P)
        y_rows = [y[0:T, :].rearrange("(t p) c -> p t c", p=P) for y in y_d]

        x = sb("x", [P, NT, C], F32)
        w0 = sb("w0", [P, 2, NCH, PIECE], F32R)
        stage = sb("stage", [P, 2, PIECE], F32)
        ident = sb("ident", [P, P], F32)
        below_s = sb("below_s", [P, P], F32)
        below = sb("below", [P, P], F32R)
        causal = sb("causal", [P, P], F32)
        one_row = sb("one_row", [P, NT], F32)
        empty = sb("empty", [P, ROW], F32)
        ones = sb("ones", [P, P], F32R)
        router = sb("router", [P, KC, 2, E], F32R)
        router_s = sb("router_s", [P, KC, E], F32)
        mhalf = sb("mhalf", [P, NT], F32)
        st = sb("st", [P, BT, 6], F32)
        lnd = sb("lnd", [P, BT], F32)
        lnm = sb("lnm", [P, BT], F32)
        lnv = sb("lnv", [P, BT], F32)
        lndd = sb("lndd", [P, BT], F32)
        lnv2 = sb("lnv2", [P, BT], F32)
        mean = sb("mean", [P, BT], F32)
        var = sb("var", [P, NT], F32)
        vare = sb("vare", [P, NT], F32)
        rstd = sb("rstd", [P, NT], F32)
        ra = sb("ra", [P, NT], F32)
        rb = sb("rb", [P, NT], F32)
        m1 = sb("m1", [P, NT], F32)
        m2 = sb("m2", [P, NT], F32)
        lg = sb("lg", [P, NT, E], F32)
        pr = sb("pr", [P, NT, E], F32)
        pick = sb("pick", [P, NT, E], F32)
        oh = sb("oh", [P, TOPK, NT, E], F32)
        mask = sb("mask", [P, NT, E], F32R)
        prio = sb("prio", [P, NT, E], F32)
        base = sb("base", [P, NT, E], F32)
        slot_i = sb("slot_i", [P, TOPK, NT], I32)
        table = sb("table", [P, NT, 1 + E], F32)
        srow = sb("srow", [P, 2, ROW], F32)
        sidx = sb("sidx", [P, 2, TOPK], I32)
        wmeta = sb("wmeta", [P, 4, 3], F32)
        tmeta = sb("tmeta", [P, 4, 3], I32)
        o_t = sb("o_t", [P, KC, SB], F32)
        ffn_mem = ExitStack()
        w1 = sb("w1", [P, 2, NCH, PIECE], F32R, ffn_mem)
        zh = sb("zh", [P, 2, KC, SB], F32R, ffn_mem)
        zl = sb("zl", [P, 2, KC, SB], F32R, ffn_mem)
        sg_s = sb("sg_s", [P, 2, SB], F32, ffn_mem)
        h_s = sb("h_s", [P, 2, SB], F32, ffn_mem)
        hh = sb("hh", [P, 2, SB], F32R, ffn_mem)
        hl = sb("hl", [P, 2, SB], F32R, ffn_mem)
        zn = sb("zn", [P, 2, BT, C], F32, ffn_mem)
        xr = sb("xr", [P, 2, 3, ROW], F32, ffn_mem)
        eo = sb("eo", [P, 2, 3, C], F32, ffn_mem)
        ffn_mem.close()
        att = ExitStack()
        aw_s = sb("aw_s", [P, KC, 4 * C], F32, att)
        aw = sb("aw", [P, 2, KC, 4 * C], F32R, att)
        lnw = sb("lnw", [P, C], F32, att)
        azn = sb("azn", [P, 2, C], F32, att)
        azh = sb("azh", [P, 2, KC, P], F32R, att)
        azl = sb("azl", [P, 2, KC, P], F32R, att)
        qk = sb("qk", [P, 2, C], F32, att)
        qcat = sb("qcat", [P, NH, 64], F32, att)
        kcat = sb("kcat", [P, NH, 64], F32, att)
        q_t = sb("q_t", [P, NH // 2, P], F32R, att)
        k_t = sb("k_t", [P, NH // 2, 2, P], F32R, att)
        s_s = sb("s_s", [P, NH, GROUP], F32, att)
        p_s = sb("p_s", [P, NH, GROUP], F32, att)
        smax = sb("smax", [P, NH], F32, att)
        ph = sb("ph", [P, NH // 2, P], F32R, att)
        pl = sb("pl", [P, NH // 2, P], F32R, att)
        vh = sb("vh", [P, 4, NH // 2, 66], F32R, att)
        vl = sb("vl", [P, 4, NH // 2, 66], F32R, att)
        rden = sb("rden", [P, NH], F32, att)
        y_s = sb("y_s", [P, C], F32, att)
        yh = sb("yh", [P, KC, P], F32R, att)
        yl = sb("yl", [P, KC, P], F32R, att)
        sqj = sb("sqj", [P, 2, C], F32, att)
        ssq = sb("ssq", [P, 2], F32, att)
        qke = sb("qke", [P, 2], F32, att)
        qkr = sb("qkr", [P, 2], F32, att)
        ast = sb("ast", [P, 6], F32, att)
        amv = sb("amv", [P, 2, 2], F32, att)
        ave = sb("ave", [P, 2], F32, att)
        ard = sb("ard", [P, 2], F32, att)
        att.close()

        gate_p = psum("gate_p", [P, 2, 512])
        quad = psum("quad", [P, 4, 512])
        up_p, out_p = quad[:, 0:2, :], quad[:, 2:4, :]
        misc = psum("misc", [P, 2, 512])

        names = """const x_l0 x_l1 gate_full silu_done up_full h_done hh_done down_done hl_done out_full
            ot_act ot_dve misc_full misc_free st_in0 st_in1 wh_done wl_done ln_st ln_a ln_b ln_c ln_var
            ln_rstd ln_z zh_done zsv0 zsv1 zin0 zin1 r_in rt rt_rms rt_rs rt_exp rt_in rt_mask
            rt_pos sr_in0 sr_in1 sidx_in scat0 scat1 pool_step routed xr_in0 xr_in1 meta_done
            eo_done sadd0 sadd1 x_sh y_sv0 y_sv1 init out_done
            aw_in aw_h aw_l av x2_in a_zn a_rs a_qke a_qr a_sub a_t a_zh a_zl a_qkv a_sq a_qn a_qc a_qlo a_qt a_qe a_s a_mk
            a_exp a_pt a_ph a_pl a_vh a_vl a_y a_yn a_yt a_yh a_yl a_o a_x a_const a_ke a_kt
            sums_done sp_step dve_step a_masked a_max a_rden pool_const""".split()
        sm = {n: sem(n) for n in names}
        W = [w0, w1]
        x_l = [sm["x_l0"], sm["x_l1"]]
        zsv = [sm["zsv0"], sm["zsv1"]]
        zin = [sm["zin0"], sm["zin1"]]
        st_in = [sm["st_in0"], sm["st_in1"]]
        sr_in = [sm["sr_in0"], sm["sr_in1"]]
        scat = [sm["scat0"], sm["scat1"]]
        xr_in = [sm["xr_in0"], sm["xr_in1"]]
        sadd = [sm["sadd0"], sm["sadd1"]]
        y_sv = [sm["y_sv0"], sm["y_sv1"]]

        PH = {"s0": 0, "s1": NB, "e": 2 * NB}
        LEN = {"s0": NB, "s1": NB, "e": NEB}

        def blk(f, phase, b):
            return FB * f + PH[phase] + b

        use = {}
        for f in range(2):
            def add(*key):
                use[(f, *key)] = len(use)
            add("T", "s0", 0)
            add("R", "s0", 0)
            for b in range(NB):
                if b:
                    add("O", "s0", b - 1)
                if b < NB - 1:
                    add("T", "s0", b + 1)
                    add("R", "s0", b + 1)
            add("M", "s0", 0)
            for b in range(NB):
                add("O", *(("s1", b - 1) if b else ("s0", NB - 1)))
            add("T", "e", 0)
            for b in range(NEB):
                add("O", *(("e", b - 1) if b else ("s1", NB - 1)))
                if b < NEB - 1:
                    add("T", "e", b + 1)
            add("O", "e", NEB - 1)

        POOL_CONSTS = 9

        def hooks(f, phase, s):
            b, n = s.index, LEN[phase]
            last = s.reg is None and b == n - 1
            got = {}
            if phase == "s0":
                if not s.first:
                    got[1] = ("O", "s0", -1)
                if not last:
                    got[3] = ("T", "s0", 1)
                    got[5] = ("R", "s0", 1)
            elif phase == "s1":
                got[1] = ("O", "s0", NB - 1) if s.first else ("O", "s1", -1)
            else:
                got[1] = ("O", "s1", NB - 1) if s.first else ("O", "e", -1)
                if not last:
                    got[4] = ("T", "e", 1)
            return got

        def use_at(f, phase, s, hook):
            what, ph2, off = hook
            if s.first and ph2 != phase:
                return use[(f, what, ph2, off)]
            return s.at(lambda b: use[(f, what, ph2, b + off)])

        def out_used(f, phase, s):
            def count(b):
                if b >= 2:
                    return use[(f, "O", phase, b - 2)] + 1
                if phase == "s0":
                    return use[(f, "O", "s0", 0)] - 3 + 1
                return use[(f, "O", {"s1": "s0", "e": "s1"}[phase], NB - 2 + b)] + 1
            return s.at(count)

        def piece_of(f, unit, j):
            return (f * UNITS + unit) * NCH + j

        def splits(f, phase, s):
            if phase == "e":
                cs = {1: 0, 3: 1, 5: 2, 7: 3}
                return {c: (s.index % 2) * 4 + j for c, j in cs.items()}
            return {6: None}

        def split_piece(f, phase, s, c):
            cs = splits(f, phase, s)
            if c not in cs:
                return None
            if phase == "e":
                j = cs[c]
                unit = lambda b: SU + b // 2 + 1
                if s.reg is None and s.index >= NEB - 2 and f == 1:
                    return None
                return (s.at(lambda b: piece_of(f, unit(b), 0) + j), j, unit(s.index) % 2)
            u = 1 if phase == "s0" else 2
            return (s.at(lambda b: piece_of(f, u, b)), None, u % 2)

        LEAD = 3
        RT = 35
        XB = NEB // 2
        block = ctx.enter_context(nc.Block())

        @block.tensor
        def _(pe):
            def split_product(dst, pairs, n):
                k = 0
                for ah, al, bh, bl in pairs:
                    for a, b in ((ah, bh), (ah, bl), (al, bh)):
                        last = pe.matmul(dst, a, b, start=(k == 0), stop=(k == 3 * n - 1))
                        k += 1
                return last

            def gate_up(f, phase, s, c, buf, ncol):
                par = c % 2
                n = lambda b: NCH * blk(f, phase, b) + c
                z = s.mod % 2
                g0 = 0
                for which, psb, done in ((0, gate_p, "gate_full"), (1, up_p, "up_full")):
                    if n(s.index) >= 2:
                        pe.wait_ge(sm["silu_done" if which == 0 else "h_done"], s.at(lambda b: n(b) - 1))
                    k0 = which * KC * P
                    w = W[buf]
                    split_product(psb[:, par, 0:ncol],
                                  [(w[:, 0, c, k0 + k * P:k0 + (k + 1) * P], w[:, 1, c, k0 + k * P:k0 + (k + 1) * P],
                                    zh[:, z, k, 0:ncol], zl[:, z, k, 0:ncol]) for k in range(KC)], KC).then_inc(sm[done], 1)

            def down(n_of, s, c, buf, ncol, blk_of):
                pe.wait_ge(sm["hl_done"], s.at(lambda b: n_of(b) + 1))
                if c == 0 and blk_of(s.index) > 0:
                    pe.wait_ge(sm["ot_act"], s.at(blk_of))
                    pe.wait_ge(sm["ot_dve"], s.at(blk_of))
                w = W[buf]
                par = c % 2
                for k in range(KC):
                    o = 2 * KC * P + k * P
                    for j, (hi, a) in enumerate(((0, hh), (0, hl), (1, hh))):
                        last = pe.matmul(out_p[:, k, 0:ncol], w[:, hi, c, o:o + P], a[:, par, 0:ncol],
                                         start=(c == 0 and j == 0), stop=(c == NCH - 1 and j == 2))
                last.then_inc(sm["down_done"], 1)

            def z_transposes(f, phase, s, off, m):
                nxt = lambda b: b + off
                if phase == "s0":
                    pe.wait_ge(sm["ln_z"], s.at(lambda b: NB * f + nxt(b) + 1))
                else:
                    par = (s.mod + off) % 2
                    pe.wait_ge(xr_in[par], s.at(lambda b: 32 * (XB * f + nxt(b) // 2 + 1)))
                wait(pe, sm["misc_free"], m)
                par = (s.mod + off) % 2
                for k in range(KC):
                    if phase == "s0":
                        for j in range(BT):
                            last = pe.transpose(misc[:, k, j * P:(j + 1) * P], zn[:, par, j, k * P:(k + 1) * P], ident[:, :])
                    else:
                        for j, (at, rows) in enumerate(EPART):
                            last = pe.transpose(misc[:, k, at:at + rows], xr[0:rows, par, j, k * P:(k + 1) * P],
                                                ident[0:rows, 0:rows])
                last.then_inc(sm["misc_full"], 1)

            def router_product(s, off, m):
                pe.wait_ge(sm["misc_free"], m)
                par = (s.mod + off) % 2
                for j in range(BT):
                    c = slice(j * P, (j + 1) * P)
                    last = split_product(misc[:, 0, j * E:(j + 1) * E],
                                         [(zh[:, par, k, c], zl[:, par, k, c], router[:, k, 0, :], router[:, k, 1, :])
                                          for k in range(KC)], KC)
                last.then_inc(sm["misc_full"], 1)

            def out_transposes(expert, count, m):
                pe.wait_ge(sm["ot_act"], count)
                pe.wait_ge(sm["ot_dve"], count)
                pe.wait_ge(sm["misc_free"], m)
                parts = EPART if expert else [(j * P, P) for j in range(BT)]
                for j, (at, rows) in enumerate(parts):
                    for k in range(KC):
                        o = (j % 2) * C + k * P
                        last = pe.transpose(misc[0:rows, j // 2, o:o + P], o_t[:, k, at:at + rows], ident[:, :])
                last.then_inc(sm["misc_full"], 1)

            def route_product(f, m):
                pe.wait_ge(sm["rt_mask"], f + 1)
                pe.wait_ge(sm["misc_free"], m)
                mk = mask[:, :, :].rearrange("p t e -> p (t e)")
                pe.matmul(misc[:, 0, 0:NT * E], below[:, :], mk, start=True, stop=True)
                pe.matmul(misc[:, 1, 0:NT * E], ones[:, :], mk, start=True, stop=True).then_inc(sm["misc_full"], 1)

            def do_hook(f, phase, s, hook):
                what, ph2, off = hook
                m = use_at(f, phase, s, hook)
                if what == "T":
                    z_transposes(f, ph2, s, off, m)
                elif what == "R":
                    router_product(s, off, m)
                else:
                    out_transposes(ph2 == "e", s.at(lambda b: blk(f, phase, b)), m)

            def ffn(f):
                z_transposes(f, "s0", Step(0, 2), 0, use[(f, "T", "s0", 0)])
                if f == 0:
                    pe.wait_ge(sm["rt_in"], 2)
                router_product(Step(0, 2), 0, use[(f, "R", "s0", 0)])
                prev = [None]
                for phase in ("s0", "s1", "e"):
                    period = 4 if phase == "e" else 2
                    ncol = EB if phase == "e" else SB

                    def body(s, phase=phase, ncol=ncol):
                        unit = (lambda b: SU + b // 2) if phase == "e" else (lambda b: 0 if phase == "s0" else 1)
                        buf = unit(s.index) % 2
                        first_of_unit = s.first or (phase == "e" and s.index % 2 == 0)
                        if phase == "s1":
                            pe.wait_ge(zin[s.mod % 2], s.at(lambda b: 32 * (NB // 2 * f + b // 2 + 1)))
                        else:
                            pe.wait_ge(sm["misc_free"], s.at(lambda b: use[(f, "T", phase, b)] + 1))
                        hk = hooks(f, phase, s)
                        for c in range(NCH):
                            if first_of_unit:
                                pe.wait_ge(sm["wl_done"], s.at(lambda b: piece_of(f, unit(b), c) + 1))
                            gate_up(f, phase, s, c, buf, ncol)
                            if c:
                                down(lambda b: NCH * blk(f, phase, b) + c - 1, s, c - 1, buf, ncol,
                                     lambda b: blk(f, phase, b))
                            elif not (phase == "s0" and s.first):
                                if s.first:
                                    pbuf = 0 if phase == "s1" else 1
                                    pcol = SB
                                else:
                                    pbuf = unit(s.index - 1) % 2
                                    pcol = ncol
                                down(lambda b: NCH * blk(f, phase, b) - 1, s, NCH - 1, pbuf, pcol,
                                     lambda b: blk(f, phase, b) - 1)
                            if c in hk:
                                do_hook(f, phase, s, hk[c])

                    sweep(pe, LEN[phase], period, body)
                    if phase == "s0":
                        route_product(f, use[(f, "M", "s0", 0)])
                    if phase == "s1":
                        z_transposes(f, "e", Step(0, 4), 0, use[(f, "T", "e", 0)])
                s = Step(FB * f + FB, 1)
                down(lambda b: NCH * b - 1, s, NCH - 1, (UNITS - 1) % 2, EB, lambda b: b - 1)
                out_transposes(True, FB * (f + 1), use[(f, "O", "e", NEB - 1)])

            def attention():
                z_p, y_p = quad[:, 2, 0:C], quad[:, 3, 0:C]
                side = gate_p[:, 1, C:2 * C]

                def c(t, k=1):
                    return t.at(lambda b: min(max(b + k, 0), NT))

                def z_transpose(t):
                    pe.wait_ge(sm["a_zn"], c(t))
                    wait(pe, sm["a_masked"], c(t, -2))
                    for k in range(KC):
                        last = pe.transpose(z_p[:, k * P:(k + 1) * P], azn[:, t.index % 2, k * P:(k + 1) * P], ident[:, :])
                    last.then_inc(sm["a_t"], 1)

                def qkv(t):
                    pe.wait_ge(sm["a_zl"], c(t))
                    wait(pe, sm["a_qn"], c(t, 0))
                    z = t.index % 2
                    for dst, c0, c1 in ((gate_p[:, 0, :], 0, 2 * C), (gate_p[:, 1, 0:C], 2 * C, 3 * C)):
                        if c0:
                            wait(pe, sm["a_vl"], c(t, 0))
                            wait(pe, sm["a_o"], c(t, -3))
                        last = split_product(dst, [(azh[:, z, k, :], azl[:, z, k, :], aw[:, 0, k, c0:c1], aw[:, 1, k, c0:c1])
                                                   for k in range(KC)], KC)
                    last.then_inc(sm["a_qkv"], 1)

                def pair_transposes(src, done):
                    for j in range(NH // 2):
                        last = pe.transpose(misc[:, j // 4, (j % 4) * P:(j % 4 + 1) * P],
                                            src[:, 2 * j:2 * j + 2, :].rearrange("p h d -> p (h d)"), ident[:, :])
                    last.then_inc(sm[done], 1)

                def scores(t):
                    pe.wait_ge(sm["a_ke"], c(t))
                    wait(pe, sm["a_masked"], c(t, 0))
                    wait(pe, sm["a_yn"], c(t, -1))
                    wait(pe, sm["a_yl"], c(t, -1))
                    pe.wait_ge(sm["a_zl"], c(t, 3))
                    for j in range(NH // 2):
                        o = (j % 2) * 2 * P
                        last = pe.matmul(quad[:, j // 2, o:o + 2 * P], q_t[:, j, :], k_t[:, j, :, :].rearrange("p r c -> p (r c)"),
                                         start=True, stop=True)
                    last.then_inc(sm["a_s"], 1)

                def values(t):
                    pe.wait_ge(sm["a_pl"], c(t))
                    pe.wait_ge(sm["a_vl"], c(t))
                    pe.wait_ge(sm["a_masked"], c(t, 2))
                    q = t.index % 4
                    for j in range(NH // 2):
                        o = (j % 4) * 66
                        last = split_product(quad[:, j // 4, o:o + 66], [(ph[:, j, :], pl[:, j, :], vh[:, q, j, :], vl[:, q, j, :])], 1)
                    last.then_inc(sm["a_y"], 1)

                def step(s):
                    t = s.shift(-LEAD - 2, NT)
                    if t:
                        pe.wait_ge(sm["a_exp"], c(t))
                        pe.wait_ge(sm["a_ke"], c(t, 2))
                        pair_transposes(p_s, "a_pt")
                    t = s.shift(2 - LEAD, NT)
                    if t:
                        z_transpose(t)
                    t = s.shift(1 - LEAD, NT)
                    if t:
                        qkv(t)
                    t = s.shift(-LEAD, NT)
                    if t:
                        pe.wait_ge(sm["a_qlo"], c(t))
                        wait(pe, sm["a_pl"], c(t, -1))
                        pair_transposes(qcat, "a_qt")
                    t = s.shift(-LEAD - 2, NT)
                    if t:
                        values(t)
                    t = s.shift(-LEAD, NT)
                    if t:
                        pe.wait_ge(sm["a_qe"], c(t))
                        pair_transposes(kcat, "a_kt")
                    t = s.shift(-LEAD - 2, NT)
                    if t:
                        pe.wait_ge(sm["a_yn"], c(t))
                        for k in range(KC):
                            last = pe.transpose(y_p[:, k * P:(k + 1) * P], y_s[:, k * P:(k + 1) * P], ident[:, :])
                        last.then_inc(sm["a_yt"], 1)
                    t = s.shift(-LEAD, NT)
                    if t:
                        scores(t)
                    t = s.shift(-LEAD - 2, NT)
                    if t:
                        pe.wait_ge(sm["a_yl"], c(t))
                        pe.wait_ge(sm["a_vl"], c(t, 4))
                        split_product(side, [(yh[:, k, :], yl[:, k, :], aw[:, 0, k, 3 * C:4 * C], aw[:, 1, k, 3 * C:4 * C])
                                             for k in range(KC)], KC).then_inc(sm["a_x"], 1)

                pe.wait_ge(sm["aw_l"], 1)
                sweep(pe, NT + LEAD + 2, 4, step, head=LEAD + 4, tail=LEAD + 2)

            pe.wait_ge(sm["const"], 1)
            ffn(0)
            attention()
            ffn(1)

        @block.scalar
        def _(act):
            def z_high(f, phase, s, off, m):
                par = (s.mod + off) % 2
                ncol = SB if phase == "s0" else EB
                act.wait_ge(sm["misc_full"], m + 1)
                wait(act, sm["up_full"], s.at(lambda b: NCH * (blk(f, phase, b + off) - 1)))
                if phase == "s0":
                    act.wait_ge(zsv[par], s.at(lambda b: 48 * (NB // 2 * f + (b + off) // 2 + 1)))
                nc.scalar.copy(zh[:, par, :, 0:ncol], misc[:, :, 0:ncol]).then_inc(sm["zh_done"], 1)

            def ffn(f):
                z_high(f, "s0", Step(0, 2), 0, use[(f, "T", "s0", 0)])
                for phase in ("s0", "s1", "e"):
                    period = 4 if phase == "e" else 2
                    ncol = EB if phase == "e" else SB

                    def body(s, phase=phase, ncol=ncol):
                        hk = hooks(f, phase, s)
                        for c in range(NCH):
                            par = c % 2
                            n = lambda b: NCH * blk(f, phase, b) + c
                            act.wait_ge(sm["gate_full"], s.at(lambda b: n(b) + 1))
                            if n(s.index) >= 2:
                                act.wait_ge(sm["h_done"], s.at(lambda b: n(b) - 1))
                            nc.scalar.activation(sg_s[:, par, 0:ncol], gate_p[:, par, 0:ncol], ACT.Silu).then_inc(sm["silu_done"], 1)
                            if c == 0 and not (phase == "s0" and s.first):
                                g = lambda b: blk(f, phase, b)
                                pcol = ncol if not s.first else SB
                                act.wait_ge(sm["down_done"], s.at(lambda b: NCH * g(b)))
                                act.wait_ge(sm["misc_full"], out_used(f, phase, s))
                                nc.scalar.copy(o_t[:, 0, 0:pcol], out_p[:, 0, 0:pcol]).then_inc(sm["ot_act"], 1)
                            if c in hk and hk[c][0] == "T":
                                z_high(f, hk[c][1], s, hk[c][2], use_at(f, phase, s, hk[c]))
                            piece = split_piece(f, phase, s, c)
                            if piece is not None:
                                weights_high(f, phase, s, c, piece)
                            act.wait_ge(sm["h_done"], s.at(lambda b: n(b) + 1))
                            if n(s.index) >= 2:
                                act.wait_ge(sm["down_done"], s.at(lambda b: n(b) - 1))
                            nc.scalar.copy(hh[:, par, 0:ncol], h_s[:, par, 0:ncol]).then_inc(sm["hh_done"], 1)

                    sweep(act, LEN[phase], period, body)
                    if phase == "s0":
                        act.wait_ge(sm["rt_rms"], 2 * f + 2)
                        nc.scalar.activation(pr[:, :, :], lg[:, :, :], ACT.Exp).then_inc(sm["rt_exp"], 1)
                    if phase == "s1":
                        z_high(f, "e", Step(0, 4), 0, use[(f, "T", "e", 0)])
                act.wait_ge(sm["down_done"], NCH * FB * (f + 1))
                act.wait_ge(sm["misc_full"], use[(f, "O", "e", NEB - 2)] + 1)
                nc.scalar.copy(o_t[:, 0, 0:EB], out_p[:, 0, 0:EB]).then_inc(sm["ot_act"], 1)

            def weights_high(f, phase, s, c, piece):
                n, j, buf = piece
                par = (s.mod if j is None else j) % 2
                if phase == "e":
                    v = s.at(lambda b: 48 * (piece_of(f, SU + b // 2 + 1, j) // 2 + 1))
                    u = s.at(lambda b: NCH * blk(f, "e", b // 2 * 2))
                else:
                    v = s.at(lambda b: 48 * (piece_of(f, 1 if phase == "s0" else 2, b) // 2 + 1))
                    u = NCH * blk(f, phase, 0)
                act.wait_ge(st_in[par], v)
                wait(act, sm["down_done"], u)
                if j is None:
                    dst = W[buf][:, 0, bass.ds(s.at(lambda b: b), 1), :].rearrange("p a c -> p (a c)") if s.reg is not None \
                        else W[buf][:, 0, s.index, :]
                else:
                    dst = W[buf][:, 0, j, :]
                nc.scalar.copy(dst, stage[:, par, :]).then_inc(sm["wh_done"], 1)

            def attention():
                act.wait_ge(sm["aw_in"], 48)
                nc.scalar.copy(aw[:, 0, :, :], aw_s[:, :, :]).then_inc(sm["aw_h"], 1)

                chunks = lambda ap: ap.rearrange("p (k c) -> p k c", k=KC)
                heads = lambda ap: ap.rearrange("p (h d) -> p h d", d=HD)
                z_p, y_p = quad[:, 2, 0:C], quad[:, 3, 0:C]
                side = gate_p[:, 1, C:2 * C]
                pairs = misc[:, :, :].rearrange("p b (j c) -> p (b j) c", c=P)
                high = lambda ap: ap.bitcast(F32R)

                def c(t, k=1):
                    return t.at(lambda b: min(max(b + k, 0), NT))

                def values(t):
                    wait(act, sm["a_y"], c(t, -3))
                    for g in range(2):
                        for r in range(2):
                            src = gate_p[64 * g:64 * g + 64, 1, 0:C].rearrange("p (j r d) -> p j r d", r=2, d=HD)[:, :, r, :]
                            o = 32 * g + HD * r
                            last = nc.scalar.copy(vh[64 * r:64 * r + 64, t.index % 4, :, o:o + HD], src)
                    last.then_inc(sm["a_vh"], 1)

                def step(s):
                    t = s.shift(-LEAD - 2, NT)
                    if t:
                        act.wait_ge(sm["a_pt"], c(t))
                        wait(act, sm["a_y"], c(t, 0))
                        nc.scalar.copy(ph[:, :, :], pairs).then_inc(sm["a_ph"], 1)
                    t = s.shift(2 - LEAD, NT)
                    if t:
                        act.wait_ge(sm["a_t"], c(t))
                        wait(act, sm["a_qkv"], c(t, -1))
                        nc.scalar.copy(azh[:, t.index % 2, :, :], chunks(z_p)).then_inc(sm["a_zh"], 1)
                    t = s.shift(1 - LEAD, NT)
                    if t:
                        act.wait_ge(sm["a_qkv"], c(t))
                        wait(act, sm["a_qke"], c(t, 0))
                        for j in range(2):
                            nc.scalar.activation(sqj[:, j, :], gate_p[:, 0, j * C:(j + 1) * C], ACT.Square,
                                                 accum_out=ssq[:, j:j + 1]).then_inc(sm["a_sq"], 1)
                        values(t)
                    t = s.shift(-LEAD, NT)
                    if t:
                        act.wait_ge(sm["a_qt"], c(t))
                        wait(act, sm["a_s"], c(t, 0))
                        nc.scalar.copy(q_t[:, :, :], pairs).then_inc(sm["a_qe"], 1)
                        act.wait_ge(sm["a_kt"], c(t))
                        for r in range(2):
                            rows = slice(64 * r, 64 * r + 64)
                            last = nc.scalar.copy(k_t[rows, :, r, :], pairs[rows])
                        last.then_inc(sm["a_ke"], 1)
                    t = s.shift(-LEAD - 2, NT)
                    if t:
                        act.wait_ge(sm["a_yt"], c(t))
                        wait(act, sm["a_x"], c(t, 0))
                        nc.scalar.copy(yh[:, :, :], chunks(y_p)).then_inc(sm["a_yh"], 1)
                    t = s.shift(-LEAD - 1, NT)
                    if t:
                        act.wait_ge(sm["a_sub"], c(t))
                        wait(act, sm["a_pt"], c(t, 0))
                        nc.scalar.activation(p_s[:, :, :], s_s[:, :, :], ACT.Exp, scale=float(HD) ** -0.5).then_inc(sm["a_exp"], 1)
                    t = s.shift(1 - LEAD, NT)
                    if t:
                        act.wait_ge(sm["a_qn"], c(t))
                        wait(act, sm["a_kt"], c(t, 0))
                        for dst, q, at in ((qcat, 0, 0), (qcat, 0, HD), (kcat, 1, 0), (kcat, 1, 2 * HD)):
                            last = nc.scalar.copy(high(dst[:, :, at:at + HD]), heads(qk[:, q, :]))
                        last.then_inc(sm["a_qc"], 1)

                act.wait_ge(sm["a_const"], 3)
                sweep(act, NT + LEAD + 2, 4, step, head=LEAD + 4, tail=LEAD + 2)

            for j in range(NCH):
                act.wait_ge(st_in[j % 2], 48 * (j // 2 + 1))
                nc.scalar.copy(w0[:, 0, j, :], stage[:, j % 2, :]).then_inc(sm["wh_done"], 1)
            act.wait_ge(sm["r_in"], 16 * KC)
            nc.scalar.copy(router[:, :, 0, :], router_s[:, :, :]).then_inc(sm["rt_in"], 1)
            ffn(0)
            attention()
            ffn(1)

        @block.vector
        def _(dve):
            v = nc.vector

            def ln(f, s, off):
                par = (s.mod + off) % 2
                nb = lambda b: b + off
                L = lambda k: s.at(lambda b: NB * f + nb(b) + k)
                if f == 0:
                    dve.wait_ge(x_l[par], s.at(lambda b: 16 * (nb(b) // 2 + 1)))
                elif s.first and off == 0:
                    dve.wait_ge(sm["a_o"], NT)
                xt = s.at(lambda b: BT * nb(b))
                for j in range(BT):
                    last = v.bn_stats(st[:, j, :], xtile(s, off, j))
                last.then_inc(sm["ln_st"], 1)
                dve.wait_ge(sm["ln_st"], L(1))
                v.tensor_tensor(lnd[:, :], st[:, :, 1], st[:, :, 4], ALU.subtract)
                v.tensor_tensor(lnm[:, :], st[:, :, 1], st[:, :, 4], ALU.add)
                v.tensor_tensor(lnv[:, :], st[:, :, 2], st[:, :, 5], ALU.add).then_inc(sm["ln_a"], 1)
                dve.wait_ge(sm["ln_a"], L(1))
                v.tensor_tensor(lndd[:, :], lnd[:, :], lnd[:, :], ALU.mult)
                v.tensor_scalar(mean[:, :], lnm[:, :], 0.5, None, ALU.mult).then_inc(sm["ln_b"], 1)
                dve.wait_ge(sm["ln_b"], L(1))
                v.scalar_tensor_tensor(out=lnv2[:, :], in0=lndd[:, :], scalar=C / 4.0, in1=lnv[:, :],
                                       op0=ALU.mult, op1=ALU.add).then_inc(sm["ln_c"], 1)
                dve.wait_ge(sm["ln_c"], L(1))
                cols = bass.ds(xt, BT)
                v.tensor_scalar(var[:, cols], lnv2[:, :], 1.0 / C, None, ALU.mult)
                v.tensor_scalar(vare[:, cols], lnv2[:, :], 1.0 / C, LN_EPS, ALU.mult, ALU.add).then_inc(sm["ln_var"], 1)

            def xtile(s, off, j):
                t = s.at(lambda b: BT * (b + off) + j)
                return x[:, bass.ds(t, 1), :].rearrange("p a c -> p (a c)")

            def ln_rows(f, s, off):
                par = (s.mod + off) % 2
                nb = lambda b: b + off
                dve.wait_ge(sm["ln_rstd"], s.at(lambda b: NB * f + nb(b) + 1))
                dve.wait_ge(zsv[par], s.at(lambda b: 48 * (NB // 2 * f + nb(b) // 2 + 1)))
                for j in range(BT):
                    t = s.at(lambda b: BT * nb(b) + j)
                    last = v.tensor_scalar(zn[:, par, j, :], xtile(s, off, j), mean[:, j:j + 1],
                                           rstd[:, bass.ds(t, 1)], ALU.subtract, ALU.mult)
                last.then_inc(sm["ln_z"], 1)

            def z_low(f, phase, s, off, m):
                par = (s.mod + off) % 2
                ncol = SB if phase == "s0" else EB
                if phase == "s0":
                    dve.wait_ge(sm["zh_done"], s.at(lambda b: (NB + NEB) * f + b + off + 1))
                else:
                    dve.wait_ge(sm["zh_done"], s.at(lambda b: (NB + NEB) * f + NB + b + off + 1))
                v.tensor_tensor(zl[:, par, :, 0:ncol], misc[:, :, 0:ncol], zh[:, par, :, 0:ncol],
                                ALU.subtract).then_inc(sm["misc_free"], 1)

            def meta(f, s, off):
                par, q = (s.mod + off) % 2, (s.mod + off) % 4
                nb = lambda b: b + off
                dve.wait_ge(xr_in[par], s.at(lambda b: 32 * (XB * f + nb(b) // 2 + 1)))
                dve.wait_ge(sm["sums_done"], s.at(lambda b: NEB * f + nb(b) + 2))
                col = s.at(lambda b: C + 1 + nb(b) // 2)
                for j, (at, rows) in enumerate(EPART):
                    v.tensor_copy(wmeta[0:rows, q, j:j + 1], xr[0:rows, par, j, bass.ds(col, 1)])
                    last = v.tensor_copy(tmeta[0:rows, q, j:j + 1], xr[0:rows, par, j, C:C + 1])
                last.then_inc(sm["meta_done"], 1)

            def logits(f, s, off, m):
                dve.wait_ge(sm["misc_full"], m + 1)
                t = s.at(lambda b: BT * (b + off))
                v.tensor_copy(lg[:, bass.ds(t, BT), :], misc[:, 0, 0:BT * E].rearrange("p (t e) -> p t e", e=E)).then_inc(sm["misc_free"], 1)

            def add_shared(f, phase, s, tile0, m):
                dve.wait_ge(sm["misc_full"], m + 1)
                xs = x[:, bass.ds(tile0, BT), :].rearrange("p t c -> p (t c)")
                v.scalar_tensor_tensor(out=xs, in0=misc[:, :, :].rearrange("p a b -> p (a b)"), scalar=0.5, in1=xs,
                                       op0=ALU.mult, op1=ALU.add).then_inc(sm["misc_free"], 1)

            def expert_rows(f, b_at, par, q, m):
                dve.wait_ge(sm["misc_full"], m + 1)
                dve.wait_ge(sm["sums_done"], b_at(lambda b: NEB * f + b + 4))
                for j, (at, rows) in enumerate(EPART):
                    o = (j % 2) * C
                    last = v.tensor_scalar(eo[0:rows, par, j, :], misc[0:rows, j // 2, o:o + C], wmeta[0:rows, q, j:j + 1],
                                           0.5, ALU.mult, ALU.mult)
                last.then_inc(sm["misc_free"], 1)

            def weights_low(f, phase, s, c, piece):
                n, j, buf = piece
                par = (s.mod if j is None else j) % 2
                dve.wait_ge(sm["wh_done"], s.at(lambda b: (piece_of(f, 1 if phase == 's0' else 2, b) if j is None else piece_of(f, SU + b // 2 + 1, j)) + 1))
                if j is None:
                    jj = bass.ds(s.at(lambda b: b), 1)
                    hi = W[buf][:, 0, jj, :].rearrange("p a c -> p (a c)")
                    lo = W[buf][:, 1, jj, :].rearrange("p a c -> p (a c)")
                else:
                    hi, lo = W[buf][:, 0, j, :], W[buf][:, 1, j, :]
                v.tensor_tensor(lo, stage[:, par, :], hi, ALU.subtract).then_inc(sm["wl_done"], 1)

            def route(f):
                k = [0]

                def then(ins):
                    k[0] += 1
                    ins.then_inc(sm["rt"], 1)
                    dve.wait_ge(sm["rt"], RT * f + k[0])

                bc = lambda t: t[:, :].unsqueeze(2).broadcast_to([P, NT, E])
                TT, TS = v.tensor_tensor, v.tensor_scalar
                a = [P, NT, E]
                then(TT(ra[:, :], rstd[:, :], rstd[:, :], ALU.mult))
                then(TT(ra[:, :], ra[:, :], var[:, :], ALU.mult))
                v.tensor_scalar(ra[:, :], ra[:, :], ROUTER_EPS, None, ALU.add).then_inc(sm["rt_rms"], 1)
                dve.wait_ge(sm["rt_rs"], f + 1)
                then(TT(lg[:, :, :], lg[:, :, :], bc(rb), ALU.mult))
                then(v.tensor_reduce(m1[:, :], lg[:, :, :], AX, ALU.max))
                TT(lg[:, :, :], lg[:, :, :], bc(m1), ALU.subtract).then_inc(sm["rt_rms"], 1)
                dve.wait_ge(sm["rt_exp"], f + 1)
                then(v.tensor_reduce(ra[:, :], pr[:, :, :], AX, ALU.add))
                then(v.reciprocal(rb[:, :], ra[:, :]))
                then(TT(pr[:, :, :], pr[:, :, :], bc(rb), ALU.mult))
                for c, best in enumerate((m1, m2)):
                    then(v.tensor_reduce(best[:, :], pr[:, :, :], AX, ALU.max))
                    then(TT(pick[:, :, :], pr[:, :, :], bc(best), ALU.is_equal))
                    then(TT(pick[:, :, :], pick[:, :, :], prio[:, :, :], ALU.mult))
                    then(v.tensor_reduce(ra[:, :], pick[:, :, :], AX, ALU.max))
                    then(TT(oh[:, c, :, :], pick[:, :, :], bc(ra), ALU.is_equal))
                    if c == 0:
                        then(v.scalar_tensor_tensor(out=pr[:, :, :], in0=oh[:, 0, :, :], scalar=-2.0, in1=pr[:, :, :],
                                                    op0=ALU.mult, op1=ALU.add))
                TT(mask[:, :, :], oh[:, 0, :, :], oh[:, 1, :, :], ALU.add).then_inc(sm["rt_mask"], 1)
                then(TT(ra[:, :], m1[:, :], m2[:, :], ALU.add))
                then(v.reciprocal(rb[:, :], ra[:, :]))
                TT(m1[:, :], m1[:, :], rb[:, :], ALU.mult)
                then(TT(m2[:, :], m2[:, :], rb[:, :], ALU.mult))
                TT(lg[:, :, :], oh[:, 0, :, :], bc(m1), ALU.mult)
                then(TT(pick[:, :, :], oh[:, 1, :, :], bc(m2), ALU.mult))
                then(TT(table[:, :, 1:1 + E], lg[:, :, :], pick[:, :, :], ALU.add))
                dve.wait_ge(sm["misc_full"], use[(f, "M", "s0", 0)] + 1)
                v.tensor_copy(pick[:, :, :], misc[:, 1, 0:NT * E].rearrange("p (t e) -> p t e", e=E))
                then(v.tensor_copy(lg[:, :, :], misc[:, 0, 0:NT * E].rearrange("p (t e) -> p t e", e=E)))
                for e in range(E):
                    last = v.tensor_tensor_scan(pr[:, :, e], one_row[:, :], pick[:, :, e], 0.0, ALU.mult, ALU.add)
                then(last)
                then(TT(lg[:, :, :], lg[:, :, :], pr[:, :, :], ALU.add))
                TT(lg[:, :, :], lg[:, :, :], pick[:, :, :], ALU.subtract).then_inc(sm["misc_free"], 1)
                dve.wait_ge(sm["misc_free"], use[(f, "M", "s0", 0)] + 1)
                then(TS(pick[:, :, :], lg[:, :, :], float(CAP), FAR, ALU.is_ge, ALU.mult))
                then(TT(lg[:, :, :], lg[:, :, :], pick[:, :, :], ALU.add))
                then(TT(lg[:, :, :], lg[:, :, :], base[:, :, :], ALU.add))
                for c in range(TOPK):
                    then(TT(pick[:, :, :], oh[:, c, :, :], lg[:, :, :], ALU.mult))
                    then(v.tensor_reduce(ra[:, :], pick[:, :, :], AX, ALU.add))
                    then(v.tensor_copy(slot_i[:, c, :], ra[:, :]))
                assert k[0] == RT, k[0]

            def ffn(f):
                s0 = Step(0, 2)
                ln(f, s0, 0)
                ln_rows(f, s0, 0)
                z_low(f, "s0", s0, 0, use[(f, "T", "s0", 0)])
                if f == 0:
                    dve.wait_ge(sm["rt_in"], 1)
                    v.tensor_tensor(router[:, :, 1, :], router_s[:, :, :], router[:, :, 0, :], ALU.subtract).then_inc(sm["rt_in"], 1)
                logits(f, s0, 0, use[(f, "R", "s0", 0)])
                for phase in ("s0", "s1", "e"):
                    period = 4 if phase == "e" else 2
                    ncol = EB if phase == "e" else SB

                    def body(s, phase=phase, ncol=ncol):
                        hk = hooks(f, phase, s)
                        last = s.reg is None and s.index == LEN[phase] - 1
                        for c in range(NCH):
                            par = c % 2
                            n = lambda b: NCH * blk(f, phase, b) + c
                            dve.wait_ge(sm["silu_done"], s.at(lambda b: n(b) + 1))
                            dve.wait_ge(sm["up_full"], s.at(lambda b: n(b) + 1))
                            v.tensor_tensor(h_s[:, par, 0:ncol], up_p[:, par, 0:ncol], sg_s[:, par, 0:ncol],
                                            ALU.mult).then_inc(sm["h_done"], 1)
                            if c == 0 and not (phase == "s0" and s.first):
                                pcol = ncol if not s.first else SB
                                dve.wait_ge(sm["down_done"], s.at(lambda b: NCH * blk(f, phase, b)))
                                dve.wait_ge(sm["misc_full"], out_used(f, phase, s))
                                v.tensor_copy(o_t[:, 1, 0:pcol], out_p[:, 1, 0:pcol]).then_inc(sm["ot_dve"], 1)
                            if phase == "s0" and not last and c == 1:
                                ln(f, s, 1)
                            if phase == "s0" and not last and c == 2:
                                ln_rows(f, s, 1)
                            if phase == "e" and not last and c == 3:
                                meta(f, s, 1)
                            piece = split_piece(f, phase, s, c)
                            if piece is not None:
                                weights_low(f, phase, s, c, piece)
                            if c in hk:
                                what, ph2, off = hk[c]
                                m = use_at(f, phase, s, hk[c])
                                if what == "T":
                                    z_low(f, ph2, s, off, m)
                                elif what == "R":
                                    logits(f, s, off, m)
                                elif ph2 == "e":
                                    expert_rows(f, lambda g: s.at(lambda b: g(b - 1)), (s.mod - 1) % 2, (s.mod - 1) % 4, m)
                                else:
                                    t0 = BT * off if off > 0 else s.at(lambda b: BT * (b - 1))
                                    add_shared(f, ph2, s, t0, m)
                            dve.wait_ge(sm["hh_done"], s.at(lambda b: n(b) + 1))
                            v.tensor_tensor(hl[:, par, 0:ncol], h_s[:, par, 0:ncol], hh[:, par, 0:ncol],
                                            ALU.subtract).then_inc(sm["hl_done"], 1)

                    sweep(dve, LEN[phase], period, body)
                    if phase == "s0":
                        route(f)
                    if phase == "s1":
                        meta(f, Step(0, 4), 0)
                        z_low(f, "e", Step(0, 4), 0, use[(f, "T", "e", 0)])
                dve.wait_ge(sm["down_done"], NCH * FB * (f + 1))
                dve.wait_ge(sm["misc_full"], use[(f, "O", "e", NEB - 2)] + 1)
                v.tensor_copy(o_t[:, 1, 0:EB], out_p[:, 1, 0:EB]).then_inc(sm["ot_dve"], 1)
                expert_rows(f, lambda g: g(NEB - 1), 1, 3, use[(f, "O", "e", NEB - 1)])

            def attention():
                dve.wait_ge(sm["aw_h"], 1)
                v.tensor_tensor(aw[:, 1, :, :], aw_s[:, :, :], aw[:, 0, :, :], ALU.subtract).then_inc(sm["aw_l"], 1)
                v.memset(qcat[:, :, :], 0.0)
                v.memset(kcat[:, :, :], 0.0)
                v.memset(k_t[:, :, :, :].bitcast(F32), 0.0)
                v.memset(vh[:, :, :, :].bitcast(F32), 0.0)
                v.memset(vl[:, :, :, :].bitcast(F32), 0.0).then_inc(sm["a_const"], 1)
                dve.wait_ge(sm["a_const"], 1)
                for r in range(2):
                    v.memset(vh[64 * r:64 * r + 64, :, :, 64 + r:65 + r].bitcast(F32), 1.0).then_inc(sm["a_const"], 1)
                chunks = lambda ap: ap.rearrange("p (k c) -> p k c", k=KC)
                heads = lambda ap: ap.rearrange("p (h d) -> p h d", d=HD)
                z_p, y_p = quad[:, 2, 0:C], quad[:, 3, 0:C]
                side = gate_p[:, 1, C:2 * C]
                pairs = misc[:, :, :].rearrange("p b (j c) -> p (b j) c", c=P)

                def c(t, k=1):
                    return t.at(lambda b: min(max(b + k, 0), NT))

                def row(t):
                    return x[:, bass.ds(t.at(lambda b: b), 1), :].rearrange("p a c -> p (a c)")

                def stats(t):
                    a = lambda k: t.at(lambda b: 3 * b + k)
                    dve.wait_ge(sm["x2_in"], t.at(lambda b: 16 * (b // 4 + 1)))
                    v.bn_stats(ast[:, :], row(t)).then_inc(sm["av"], 1)
                    dve.wait_ge(sm["av"], a(1))
                    dve.sem_inc(sm["dve_step"], 1)
                    m = t.index % 2
                    v.bn_aggr(amv[:, m, :], ast[:, :]).then_inc(sm["av"], 1)
                    dve.wait_ge(sm["av"], a(2))
                    v.tensor_scalar(ave[:, m:m + 1], amv[:, m, 1:2], LN_EPS, None, ALU.add).then_inc(sm["av"], 1)

                def masked(t):
                    dve.wait_ge(sm["a_s"], c(t))
                    wait(dve, sm["a_exp"], c(t, 0))
                    for g in range(2):
                        rows = slice(64 * g, 64 * g + 64)
                        src = quad[rows, :, :].rearrange("p b (h c) -> p (b h) c", c=P)[:, :, rows]
                        last = v.tensor_tensor(s_s[rows, :, :], src, causal[rows, rows].unsqueeze(1).broadcast_to([64, NH, GROUP]), ALU.add)
                    last.then_inc(sm["a_masked"], 1)

                def values(t):
                    dve.wait_ge(sm["a_vh"], c(t))
                    q = t.index % 4
                    for g in range(2):
                        for r in range(2):
                            src = gate_p[64 * g:64 * g + 64, 1, 0:C].rearrange("p (j r d) -> p j r d", r=2, d=HD)[:, :, r, :]
                            o = 32 * g + HD * r
                            rows = slice(64 * r, 64 * r + 64)
                            last = v.tensor_tensor(vl[rows, q, :, o:o + HD], src, vh[rows, q, :, o:o + HD], ALU.subtract)
                    last.then_inc(sm["a_vl"], 1)

                def outputs(t):
                    dve.wait_ge(sm["a_y"], c(t))
                    wait(dve, sm["a_yt"], c(t, 0))
                    yp = quad[:, 0:2, 0:4 * 66].rearrange("p b (j c) -> p b j c", c=66)
                    rd4 = rden[:, :].rearrange("p (b j r) -> p b j r", b=2, r=2)
                    for b in range(2):
                        last = v.reciprocal(rd4[:, b, :, :], yp[:, b, :, 64:66])
                    last.then_inc(sm["a_rden"], 1)
                    dve.wait_ge(sm["a_rden"], c(t))
                    for g in range(2):
                        rows = slice(64 * g, 64 * g + 64)
                        for b in range(2):
                            src = yp[rows, b, :, 32 * g:32 * g + 32].rearrange("p j (r d) -> p j r d", d=HD)
                            dst = y_s[rows, :].rearrange("p (b j r d) -> p b j r d", b=2, r=2, d=HD)[:, b]
                            last = v.tensor_tensor(dst, src, rd4[rows, b].unsqueeze(3).broadcast_to([64, 4, 2, HD]), ALU.mult)
                    last.then_inc(sm["a_yn"], 1)

                def step(s):
                    t = s.shift(-LEAD - 1, NT)
                    if t:
                        masked(t)
                    t = s.shift(2 - LEAD, NT)
                    if t:
                        m = t.index % 2
                        dve.wait_ge(sm["a_rs"], c(t))
                        wait(dve, sm["a_t"], c(t, -1))
                        v.tensor_scalar(azn[:, m, :], row(t), amv[:, m, 0:1], ard[:, m:m + 1], ALU.subtract, ALU.mult).then_inc(sm["a_zn"], 1)
                    t = s.shift(-LEAD - 2, NT)
                    if t:
                        dve.wait_ge(sm["a_ph"], c(t))
                        v.tensor_tensor(pl[:, :, :], pairs, ph[:, :, :], ALU.subtract).then_inc(sm["a_pl"], 1)
                    t = s.shift(-LEAD - 1, NT)
                    if t:
                        dve.wait_ge(sm["a_masked"], c(t))
                        wait(dve, sm["a_sub"], c(t, 0))
                        v.tensor_reduce(smax[:, :], s_s[:, :, :], AX, ALU.max).then_inc(sm["a_max"], 1)
                    t = s.shift(2 - LEAD, NT)
                    if t:
                        dve.wait_ge(sm["a_zh"], c(t))
                        v.tensor_tensor(azl[:, t.index % 2, :, :], chunks(z_p), azh[:, t.index % 2, :, :], ALU.subtract).then_inc(sm["a_zl"], 1)
                    t = s.shift(1 - LEAD, NT)
                    if t:
                        dve.wait_ge(sm["a_sq"], t.at(lambda b: 2 * b + 2))
                        wait(dve, sm["a_qr"], c(t, 0))
                        v.tensor_scalar(qke[:, :], ssq[:, :], 1.0 / C, RMS_EPS, ALU.mult, ALU.add).then_inc(sm["a_qke"], 1)
                        values(t)
                    t = s.shift(-LEAD - 2, NT)
                    if t:
                        outputs(t)
                    t = s.shift(1 - LEAD, NT)
                    if t:
                        dve.wait_ge(sm["a_qr"], c(t))
                        for j in range(2):
                            last = v.scalar_tensor_tensor(out=qk[:, j, :], in0=gate_p[:, 0, j * C:(j + 1) * C], scalar=qkr[:, j:j + 1],
                                                          in1=lnw[:, :], op0=ALU.mult, op1=ALU.mult)
                        last.then_inc(sm["a_qn"], 1)
                    t = s.shift(3 - LEAD, NT)
                    if t:
                        stats(t)
                    t = s.shift(-LEAD - 2, NT)
                    if t:
                        dve.wait_ge(sm["a_yh"], c(t))
                        v.tensor_tensor(yl[:, :, :], chunks(y_p), yh[:, :, :], ALU.subtract).then_inc(sm["a_yl"], 1)
                    t = s.shift(1 - LEAD, NT)
                    if t:
                        dve.wait_ge(sm["a_qc"], c(t))
                        v.tensor_tensor(qcat[:, :, 2 * HD:3 * HD].bitcast(F32R), heads(qk[:, 0, :]), qcat[:, :, 0:HD], ALU.subtract)
                        v.tensor_tensor(kcat[:, :, HD:2 * HD].bitcast(F32R), heads(qk[:, 1, :]), kcat[:, :, 0:HD], ALU.subtract).then_inc(sm["a_qlo"], 1)
                    t = s.shift(-LEAD - 2, NT)
                    if t:
                        dve.wait_ge(sm["a_x"], c(t))
                        v.tensor_tensor(row(t), side, row(t), ALU.add).then_inc(sm["a_o"], 1)

                sweep(dve, NT + LEAD + 2, 4, step, head=LEAD + 4, tail=LEAD + 2)

            v.memset(ones[:, :].bitcast(F32), 1.0)
            v.memset(mhalf[:, :], -0.5)
            v.memset(one_row[:, :], 1.0)
            dve.wait_ge(sm["pool_const"], POOL_CONSTS)
            v.tensor_copy(below[:, :], below_s[:, :]).then_inc(sm["const"], 1)
            for j in range(NCH):
                dve.wait_ge(sm["wh_done"], j + 1)
                v.tensor_tensor(w0[:, 1, j, :], stage[:, j % 2, :], w0[:, 0, j, :], ALU.subtract).then_inc(sm["wl_done"], 1)
            ffn(0)
            attention()
            ffn(1)

        @block.gpsimd
        def _(pool):
            g = nc.gpsimd

            def after(*counts):
                for semaphore, value in counts:
                    pool.wait_ge(semaphore, value)
                pool.sem_inc(sm["pool_step"], 1)

            k = [0]
            whole = pick[:, :, :].rearrange("p t e -> p (t e)").bitcast(I32)

            def then(ins):
                k[0] += 1
                ins.then_inc(sm["pool_const"], 1)
                pool.wait_ge(sm["pool_const"], k[0])

            g.memset(ident[:, :], 0.0)
            g.memset(below_s[:, :], 1.0)
            g.memset(causal[:, :], 0.0)
            then(g.memset(empty[:, :], 0.0))
            g.affine_select(out=ident[:, :], in_=ident[:, :], compare_op=ALU.not_equal, fill=1.0, base=0,
                            pattern=[[-1, P]], channel_multiplier=1)
            g.affine_select(out=below_s[:, :], in_=below_s[:, :], compare_op=ALU.is_gt, fill=0.0, base=0,
                            pattern=[[1, P]], channel_multiplier=-1)
            g.affine_select(out=causal[:, :], in_=causal[:, :], compare_op=ALU.is_ge, fill=-3.0e38, base=0,
                            pattern=[[-1, P]], channel_multiplier=1)
            then(g.iota(whole[:, 0:1], pattern=[[0, 1]], base=T, channel_multiplier=1))
            then(g.tensor_copy(empty[:, C:C + 1], whole[:, 0:1]))
            for dst, args in ((table[:, :, 0], dict(pattern=[[P, NT]], base=0, channel_multiplier=1)),
                              (prio[:, :, :], dict(pattern=[[0, NT], [-1, E]], base=E, channel_multiplier=0)),
                              (base[:, :, :], dict(pattern=[[0, NT], [CAP, E]], base=0, channel_multiplier=0))):
                n = NT if dst is table[:, :, 0] or len(args["pattern"]) == 1 else NT * E
                src = whole[:, 0:n] if n == NT else whole.rearrange("p (t e) -> p t e", e=E)
                then(g.iota(src, **args))
                then(g.tensor_copy(dst, src))
            assert k[0] == POOL_CONSTS, k[0]
            def attention():
                def step(s):
                    t = s.shift(1 - LEAD, NT)
                    if t:
                        after((sm["a_qke"], t.at(lambda b: b + 1)))
                        g.tensor_tensor(qkr[:, :], qke[:, :], mhalf[:, 0:2], ALU.pow).then_inc(sm["a_qr"], 1)
                    t = s.shift(-LEAD - 1, NT)
                    if t:
                        after((sm["a_max"], t.at(lambda b: b + 1)))
                        g.tensor_tensor(s_s[:, :, :], s_s[:, :, :], smax[:, :].unsqueeze(2).broadcast_to([P, NH, GROUP]),
                                        ALU.subtract).then_inc(sm["a_sub"], 1)
                    t = s.shift(3 - LEAD, NT)
                    if t:
                        m = t.index % 2
                        after((sm["av"], t.at(lambda b: 3 * b + 3)))
                        g.tensor_tensor(ard[:, m:m + 1], ave[:, m:m + 1], mhalf[:, 0:1], ALU.pow).then_inc(sm["a_rs"], 1)
                sweep(pool, NT + LEAD + 2, 4, step, head=LEAD + 4, tail=LEAD + 2)

            pool.sem_inc(sm["sums_done"], 4)

            def ln(f):
                def body(s):
                    after((sm["ln_var"], s.at(lambda b: NB * f + b + 1)))
                    cols = bass.ds(s.at(lambda b: BT * b), BT)
                    g.tensor_tensor(rstd[:, cols], vare[:, cols], mhalf[:, 0:BT], ALU.pow).then_inc(sm["ln_rstd"], 1)
                sweep(pool, NB, 2, body)

            def scatter(f):
                def body(s):
                    par = s.mod % 2
                    w = s.at(lambda t: 32 * (NT // 2 * f + t // 2))
                    if not isinstance(w, int) or w:
                        after((scat[par], w))
                    t = s.at(lambda t: t)
                    g.dma_start(srow[:, par, 0:C], zn_rows[:, bass.ds(t, 1), :].rearrange("p a c -> p (a c)")).then_inc(sr_in[par], 16)
                    g.tensor_copy(srow[:, par, C:ROW], table[:, bass.ds(t, 1), :].rearrange("p a c -> p (a c)"))
                    g.tensor_copy(sidx[:, par, :], slot_i[:, :, bass.ds(t, 1)].rearrange("p a c -> p (a c)")).then_inc(sm["sidx_in"], 1)
                    after((sr_in[par], s.at(lambda t: 16 * (NT // 2 * f + t // 2 + 1))),
                          (sm["sidx_in"], s.at(lambda t: NT * f + t + 1)))
                    for c in range(TOPK):
                        g.indirect_dma_start(out=slots_d[f], out_offset=bass.IndirectOffsetOnAxis(ap=sidx[:, par, c:c + 1], axis=0),
                                             in_=srow[:, par, :], in_offset=None, bounds_check=E * CAP - 1,
                                             oob_is_err=False).then_inc(scat[par], 16)
                sweep(pool, NT, 2, body, head=3)

            def expert_sums(f):
                def body(s):
                    par, q = s.mod % 2, s.mod
                    w = s.at(lambda b: 48 * (XB * f + (b + 1) // 2))
                    wait(pool, sadd[1 - par], w)
                    pool.sem_inc(sm["sums_done"], 1)
                    after((sm["misc_free"], s.at(lambda b: use[(f, "O", "e", b)] + 1)))
                    for j, (at, rows) in enumerate(EPART):
                        g.indirect_dma_start(out=y_d[f], out_offset=bass.IndirectOffsetOnAxis(ap=tmeta[0:rows, q, j:j + 1], axis=0),
                                             in_=eo[0:rows, par, j, :], in_offset=None, bounds_check=T + P - 1,
                                             compute_op=ALU.add).then_inc(sadd[par], 16)
                sweep(pool, NEB, 4, body)

            for f in range(2):
                ln(f)
                pool.wait_ge(sm["rt_rms"], 2 * f + 1)
                g.tensor_tensor(rb[:, :], ra[:, :], mhalf[:, :], ALU.pow).then_inc(sm["rt_rs"], 1)
                pool.wait_ge(sm["rt"], RT * (f + 1))
                for par in range(2):
                    pool.wait_ge(zsv[par], 48 * (NB // 2 * (f + 1) + 1))
                pool.wait_ge(sm["init"], 64)
                scatter(f)
                for par in range(2):
                    pool.wait_ge(y_sv[par], 16 * NB // 2 * (f + 1))
                expert_sums(f)
                if f == 0:
                    attention()

        @block.sync
        def _(sp):
            def hold(semaphore, value):
                sp.wait_ge(semaphore, value)
                if not isinstance(value, int):
                    sp.sem_inc(sm["sp_step"], 1)

            def load_x(src, b, f):
                wait(sp, x_l[b % 2], 16 * (NB // 2 * f + b // 2))
                sp.dma_start(x[:, BT * b:BT * b + BT, :], src[:, BT * b:BT * b + BT, :]).then_inc(x_l[b % 2], 16)

            def load_piece(par, n, gate, up, down):
                st_ = stage[:, par, :]
                sp.dma_start(st_[:, 0:KC * P].rearrange("p (k i) -> p k i", k=KC), gate).then_inc(st_in[par], 16)
                sp.dma_start(st_[:, KC * P:2 * KC * P].rearrange("p (k i) -> p k i", k=KC), up).then_inc(st_in[par], 16)
                sp.dma_start(st_[:, 2 * KC * P:PIECE], down).then_inc(st_in[par], 16)

            def shared_piece(u, j):
                i0 = u * NCH + j
                view = lambda w: w.rearrange("(k p) i -> p k i", p=P)[:, :, bass.ds(i0 * P, P)]
                return view(sg), view(su), sd.rearrange("(i p) c -> p i c", p=P)[:, bass.ds(i0, 1), :].rearrange("p a c -> p (a c)")

            def expert_piece(e, j):
                view = lambda w: w.rearrange("e (k p) i -> p (e k) i", p=P)[:, bass.ds(e * KC, KC), j * P:(j + 1) * P]
                return view(rg), view(ru), rd.rearrange("e (i p) c -> p (e i) c", p=P)[:, bass.ds(e * NCH + j, 1), :].rearrange("p a c -> p (a c)")

            def ffn(f):
                for phase in ("s0", "s1", "e"):
                    def body(s, phase=phase):
                        last = s.reg is None and s.index == LEN[phase] - 1
                        if phase == "s0":
                            u = 1
                            hold(sm["wl_done"], s.at(lambda b: piece_of(f, u, b) - 1))
                            load_piece(s.mod % 2, None, *shared_piece(u, s.at(lambda b: b)))
                            if not last:
                                save_z(f, s, 1)
                        elif phase == "s1":
                            if not last:
                                load_z(f, s, 1)
                            hold(sm["wl_done"], s.at(lambda b: piece_of(f, 2, b) - 1))
                            load_piece(s.mod % 2, None, *expert_piece_at(s))
                            if not s.first:
                                save_x(f, s.at(lambda b: use[(f, "O", "s1", b - 1)] + 1), s.at(lambda b: b - 1), (s.mod - 1) % 2)
                        else:
                            if not (s.reg is None and s.index >= NEB - 2):
                                load_rows(f, s, 2)
                            half = s.index % 2
                            for jj in range(4):
                                j = 4 * half + jj
                                if s.reg is None and s.index >= NEB - 2:
                                    if f == 0:
                                        hold(sm["wl_done"], piece_of(1, 0, j) - 1)
                                        load_piece(j % 2, None, *shared_piece(0, j))
                                    continue
                                hold(sm["wl_done"], s.at(lambda b: piece_of(f, SU + b // 2 + 1, j) - 1))
                                load_piece(j % 2, None, *expert_piece(s.at(lambda b: b // 2 + 1), j))
                                if s.first and jj == 0:
                                    save_x(f, use[(f, "O", "s1", NB - 1)] + 1, NB - 1, 1)
                    sweep(sp, LEN[phase], 4 if phase == "e" else 2, body, tail=2 if phase == "e" else 0)
                    if phase == "s0":
                        load_z(f, Step(0, 2), 0)
                    if phase == "s1":
                        for par in range(2):
                            hold(scat[par], 32 * (NT // 2 * (f + 1)))
                        load_rows(f, Step(0, 4), 0)
                        load_rows(f, Step(1, 4), 0)

            def expert_piece_at(s):
                j = s.at(lambda b: b)
                view = lambda w: w[0, :, :].rearrange("(k p) i -> p k i", p=P)[:, :, bass.ds(j * P, P)]
                return view(rg), view(ru), rd[0, :, :].rearrange("(i p) c -> p i c", p=P)[:, bass.ds(j, 1), :].rearrange("p a c -> p (a c)")

            def save_z(f, s, off):
                par = (s.mod + off) % 2
                b_ = s.at(lambda b: b + off)
                hold(sm["misc_free"], s.at(lambda b: use[(f, "T", "s0", b + off)] + 1))
                cols = bass.ds(b_ * SB, SB)
                sp.dma_start(zh_d[:, :, cols], zh[:, par, :, :].bitcast(F32)).then_inc(zsv[par], 16)
                sp.dma_start(zl_d[:, :, cols], zl[:, par, :, :].bitcast(F32)).then_inc(zsv[par], 16)
                sp.dma_start(zn_rows[:, bass.ds(b_ * BT, BT), :], zn[:, par, :, :]).then_inc(zsv[par], 16)

            def load_z(f, s, off):
                par = (s.mod + off) % 2
                hold(sm["up_full"], s.at(lambda b: NCH * (blk(f, "s1", b + off) - 1)))
                if s.first and off == 0:
                    for q in zsv:
                        hold(q, 48 * (NB // 2 * (f + 1) + 1))
                cols = bass.ds(s.at(lambda b: (b + off) * SB), SB)
                sp.dma_start(zh[:, par, :, :].bitcast(F32), zh_d[:, :, cols]).then_inc(zin[par], 16)
                sp.dma_start(zl[:, par, :, :].bitcast(F32), zl_d[:, :, cols]).then_inc(zin[par], 16)

            def load_rows(f, s, off):
                par = (s.mod + off) % 2
                if off:
                    hold(sm["misc_free"], s.at(lambda b: use[(f, "T", "e", b)] + 1))
                    hold(sm["meta_done"], s.at(lambda b: NEB * f + b + 1))
                at = s.at(lambda b: EB * (b + off))
                sp.dma_start(xr[:, par, 0:2, :], slots_d[f][bass.ds(at, 2 * P), :].rearrange("(j p) c -> p j c", p=P)).then_inc(xr_in[par], 16)
                sp.dma_start(xr[0:EB - 2 * P, par, 2, :], slots_d[f][bass.ds(at + 2 * P, EB - 2 * P), :]).then_inc(xr_in[par], 16)

            def save_x(f, count, b, par):
                hold(sm["misc_free"], count)
                t = bass.ds(b * BT, BT)
                sp.dma_start(y_rows[f][:, t, :], x[:, t, :]).then_inc(y_sv[par], 16)

            for q in zsv:
                sp.sem_inc(q, 48)
            load_x(x_rows, 0, 0)
            load_x(x_rows, 1, 0)
            for kk in range(KC):
                sp.dma_start(router_s[:, kk, :], router_w[:, kk * P:(kk + 1) * P].rearrange("e p -> p e"),
                             allow_slow_non_contiguous=True).then_inc(sm["r_in"], 16)
            for j in range(NCH):
                wait(sp, sm["wl_done"], j - 1)
                load_piece(j % 2, None, *shared_piece(0, j))
                if j < NB - 2:
                    load_x(x_rows, j + 2, 0)
            hold(sm["pool_const"], POOL_CONSTS)
            for f in range(2):
                sp.dma_start(slots_d[f].rearrange("(t p) c -> p t c", p=P),
                             empty[:, :].unsqueeze(1).broadcast_to([P, E * CAP // P, ROW])).then_inc(sm["init"], 16)
                sp.dma_start(y_d[f][T:T + P, :], empty[:, 0:C]).then_inc(sm["init"], 16)
            save_z(0, Step(0, 2), 0)
            ffn(0)
            for par in range(2):
                hold(sadd[par], 48 * XB)
            sp.dma_start(aw_s[:, :, 0:3 * C], w_qkv.rearrange("(k p) d -> p k d", p=P)).then_inc(sm["aw_in"], 16)
            sp.dma_start(aw_s[:, :, 3 * C:4 * C], w_proj.rearrange("(k p) d -> p k d", p=P)).then_inc(sm["aw_in"], 16)
            sp.dma_start(lnw[:, :], ln_w.rearrange("(a c) -> a c", a=1).broadcast_to([P, C])).then_inc(sm["aw_in"], 16)
            for b in range(NB):
                wait(sp, sm["x2_in"], 16 * b)
                sp.dma_start(x[:, BT * b:BT * b + BT, :], y_rows[0][:, BT * b:BT * b + BT, :]).then_inc(sm["x2_in"], 16)
            save_z(1, Step(0, 2), 0)
            ffn(1)
            for par in range(2):
                hold(sadd[par], 48 * 2 * XB)
            sp.dma_start(out_rows.rearrange("(p a) c -> p (a c)", p=P),
                         y_d[1][0:T, :].rearrange("(p a) c -> p (a c)", p=P)).then_inc(sm["out_done"], 16)
            hold(sm["out_done"], 16)


_INS = ["L0_attn_x", "L0_attn_w_qkv", "L0_attn_ln_w", "L0_attn_w_proj", "L0_ffn_router_w", "L0_ffn_rg", "L0_ffn_ru",
        "L0_ffn_rd", "L0_ffn_sg", "L0_ffn_su", "L0_ffn_sd"]
_OUT = ((2, 2048, 256), "float32")


def kernel(**inputs):
    import numpy as np
    import concourse.bacc as bacc
    from concourse.bass_utils import run_bass_kernel_spmd

    nc = bacc.Bacc("TRN2", target_bir_lowering=False, num_devices=1)
    arrays, args = {}, []
    for name in _INS:
        a = np.ascontiguousarray(inputs[name])
        arrays[f"in_{name}"] = a
        args.append(nc.dram_tensor(f"in_{name}", a.shape, mybir.dt.from_np(a.dtype), kind="ExternalInput").ap())
    shape, dtype = _OUT
    args.append(nc.dram_tensor("out_dram", shape, mybir.dt.from_np(np.dtype(dtype)), kind="ExternalOutput").ap())
    program(nc, *args)
    r = run_bass_kernel_spmd(nc, [arrays], core_ids=[0])
    return r.results[0]["out_dram"]
```

```python
from contextlib import ExitStack

import concourse.bass as bass
from concourse import mybir

F32 = mybir.dt.float32
F32R = mybir.dt.float32r
I32 = mybir.dt.int32
ALU = mybir.AluOpType
ACT = mybir.ActivationFunctionType
AX = mybir.AxisListType.X

P = 128
LN_EPS = 1e-5
RMS_EPS = 1e-6
ROUTER_EPS = 2.0 ** -23
FAR = 1.0e6
GROUP = 64
HD = 16


class Step:

    def __init__(self, index, period, reg=None, count=0):
        self.index, self.period, self.reg, self.count = index, period, reg, count
        self.first = index == 0
        self.mod = index % period

    def shift(self, k, n):
        if self.reg is None:
            return Step(self.index + k, self.period) if 0 <= self.index + k < n else None
        assert 0 <= self.index + k and self.index + k + self.period * (self.count - 1) < n
        return Step(self.index + k, self.period, self.reg, self.count)

    def at(self, f):
        if self.reg is None:
            return f(self.index)
        v = [f(self.index + self.period * n) for n in range(self.count)]
        slope = v[1] - v[0] if self.count > 1 else 0
        assert all(v[n] == v[0] + n * slope for n in range(self.count))
        return v[0] if slope == 0 else self.reg * slope + v[0]


def wait(eng, semaphore, value):
    if not isinstance(value, int) or value > 0:
        eng.wait_ge(semaphore, value)


def sweep(eng, n, period, body, head=1, tail=0):
    for b in range(head):
        body(Step(b, period))
    count = (n - head - tail) // period
    done = head
    if count > 1:
        with eng.Fori(0, count) as i:
            for r in range(period):
                body(Step(head + r, period, i, count))
        done += period * count
    for b in range(done, n):
        body(Step(b, period))


def program(nc, x_in, w_qkv, ln_w, w_proj, router_w, rg, ru, rd, sg, su, sd, out):
    B, S, C = x_in.shape
    T = B * S
    E = router_w.shape[0]
    I = rg.shape[2]
    SU = sg.shape[1] // I
    TOPK = 2
    CAP = int(1.25 * T / E)
    KC = C // P
    NCH = I // P
    NT = T // P
    BT = 512 // P
    NB = T // 512
    SB = 512
    EB = CAP // 2
    NEB = 2 * E
    NH = C // HD
    assert C == 256 and KC == 2 and I == 1024 and SU == 2 and NCH == 8 and EB == 320 and NB == 8
    PIECE = 2 * KC * P + C
    HALF_PIECE = PIECE // 2
    ROW = C + 1 + E
    EPART = [(0, 128), (128, 128), (256, 64)]
    UNITS = SU + E
    FB = SU * NB + NEB

    x_rows = x_in.rearrange("b s c -> (b s) c").rearrange("(t p) c -> p t c", p=P)
    out_rows = out.rearrange("b s c -> (b s) c")

    with ExitStack() as ctx:
        def dram(name, shape, dt):
            return nc.dram_tensor(name, shape, dt, kind="Internal").ap()

        def sb(name, shape, dt, on=ctx):
            return on.enter_context(nc.sbuf_tensor(name, shape, dt))

        def psum(name, shape):
            return ctx.enter_context(nc.psum_tensor(name, shape, F32))

        def sem(name):
            return ctx.enter_context(nc.semaphore(name))

        zh_d = dram("zh_d", [P, KC, T], F32)
        zl_d = dram("zl_d", [P, KC, T], F32)
        zn_d = dram("zn_d", [T, C], F32)
        slots_d = [dram(f"slots{f}_d", [E * CAP, ROW], F32) for f in range(2)]
        y_d = [dram("y0_d", [T, C], F32), out_rows]
        zn_rows = zn_d.rearrange("(t p) c -> p t c", p=P)
        y_rows = [y.rearrange("(t p) c -> p t c", p=P) for y in y_d]

        x = sb("x", [P, NT, C], F32)
        w0 = sb("w0", [P, 2, NCH, PIECE], F32R)
        stage = sb("stage", [P, 2, PIECE], F32)
        ident = sb("ident", [P, P], F32)
        below_s = sb("below_s", [P, P], F32)
        below = sb("below", [P, P], F32R)
        causal = sb("causal", [P, GROUP], F32)
        one_row = sb("one_row", [P, NT], F32)
        empty = sb("empty", [P, ROW], F32)
        ones = sb("ones", [P, P], F32R)
        router = sb("router", [P, KC, 2, E], F32R)
        router_s = sb("router_s", [P, KC, E], F32)
        mhalf = sb("mhalf", [P, NT], F32)
        st = sb("st", [P, BT, 6], F32)
        lnd = sb("lnd", [P, BT], F32)
        lnm = sb("lnm", [P, BT], F32)
        lnv = sb("lnv", [P, BT], F32)
        lndd = sb("lndd", [P, BT], F32)
        lnv2 = sb("lnv2", [P, BT], F32)
        mean = sb("mean", [P, BT], F32)
        var = sb("var", [P, NT], F32)
        vare = sb("vare", [P, NT], F32)
        rstd = sb("rstd", [P, NT], F32)
        ra = sb("ra", [P, NT], F32)
        rb = sb("rb", [P, NT], F32)
        m1 = sb("m1", [P, NT], F32)
        m2 = sb("m2", [P, NT], F32)
        lg = sb("lg", [P, NT, E], F32)
        pr = sb("pr", [P, NT, E], F32)
        pick = sb("pick", [P, NT, E], F32)
        oh = sb("oh", [P, TOPK, NT, E], F32)
        mask = sb("mask", [P, NT, E], F32R)
        prio = sb("prio", [P, NT, E], F32)
        base = sb("base", [P, NT, E], F32)
        slot_i = sb("slot_i", [P, TOPK, NT], I32)
        table = sb("table", [P, NT, 1 + E], F32)
        srow = sb("srow", [P, 2, ROW], F32)
        sidx = sb("sidx", [P, 2, TOPK], I32)
        wmeta = sb("wmeta", [P, 4, 3], F32)
        tmeta = sb("tmeta", [P, 4, 3], I32)
        o_t = sb("o_t", [P, KC, SB], F32)
        start_mem = ExitStack()
        raw = sb("raw", [P, NCH, PIECE], F32, start_mem)
        start_mem.close()
        ffn_mem = ExitStack()
        w1 = sb("w1", [P, 2, NCH, PIECE], F32R, ffn_mem)
        zh = sb("zh", [P, 2, KC, SB], F32R, ffn_mem)
        zl = sb("zl", [P, 2, KC, SB], F32R, ffn_mem)
        sg_s = sb("sg_s", [P, 2, SB], F32, ffn_mem)
        h_s = sb("h_s", [P, 2, SB], F32, ffn_mem)
        hh = sb("hh", [P, 2, SB], F32R, ffn_mem)
        hl = sb("hl", [P, 2, SB], F32R, ffn_mem)
        zn = sb("zn", [P, 2, BT, C], F32, ffn_mem)
        xr = sb("xr", [P, 2, 3, ROW], F32, ffn_mem)
        eo = sb("eo", [P, 2, 3, C], F32, ffn_mem)
        ffn_mem.close()
        att = ExitStack()
        aw_s = sb("aw_s", [P, KC, 4 * C], F32, att)
        aw = sb("aw", [P, 2, KC, 4 * C], F32R, att)
        qcat = sb("qcat", [P, NH, 64], F32, att)
        kcat = sb("kcat", [P, NH, 64], F32, att)
        q_t = sb("q_t", [P, NH // 2, 2, P], F32R, att)
        k_t = sb("k_t", [P, NH // 2, 2, P], F32R, att)
        vh = sb("vh", [P, 4, NH // 2, 66], F32R, att)
        vl = sb("vl", [P, 4, NH // 2, 66], F32R, att)
        lnw = sb("lnw", [P, C], F32, att)
        azn = sb("azn", [P, 2, C], F32, att)
        azh = sb("azh", [P, 2, KC, P], F32R, att)
        azl = sb("azl", [P, 2, KC, P], F32R, att)
        qk = sb("qk", [P, 2, C], F32, att)
        s_s = sb("s_s", [P, NH, GROUP], F32, att)
        p_s = sb("p_s", [P, NH, GROUP], F32, att)
        smax = sb("smax", [P, NH], F32, att)
        ph = sb("ph", [P, NH // 2, P], F32R, att)
        pl = sb("pl", [P, NH // 2, P], F32R, att)
        rden = sb("rden", [P, NH], F32, att)
        y_s = sb("y_s", [P, C], F32, att)
        yh = sb("yh", [P, KC, P], F32R, att)
        yl = sb("yl", [P, KC, P], F32R, att)
        sqj = sb("sqj", [P, 2, C], F32, att)
        ssq = sb("ssq", [P, 2], F32, att)
        qke = sb("qke", [P, 2], F32, att)
        qkr = sb("qkr", [P, 2], F32, att)
        ast = sb("ast", [P, 6], F32, att)
        amv = sb("amv", [P, 2, 2], F32, att)
        ave = sb("ave", [P, 2], F32, att)
        ard = sb("ard", [P, 2], F32, att)
        att.close()

        gate_p = psum("gate_p", [P, 2, 512])
        quad = psum("quad", [P, 4, 512])
        up_p, out_p = quad[:, 0:2, :], quad[:, 2:4, :]
        misc = psum("misc", [P, 2, 512])

        names = (
            "pool_const const pool_step sp_step dve_step "
            "x_l0 x_l1 r_in first_in0 first_in1 first_in2 st_in0 st_in1 "
            "wh_half wh_done wl_done rt_in "
            "gate_full silu_done up_full h_done hh_done hl_done down_done "
            "shared_added ot_act ot_dve misc_full misc_free "
            "ln_st ln_a ln_b ln_c ln_var ln_rstd ln_z zh_done zsv0 zsv1 zin0 zin1 "
            "rt rt_rms rt_rs rt_exp rt_mask "
            "init sr_in0 sr_in1 sidx_in scat0 scat1 "
            "xr_in0 xr_in1 meta_done sums_done sadd0 sadd1 y_sv0 y_sv1 "
            "aw_in aw_h aw_l x2_in a_const av a_rs a_zn a_t a_zh a_zl "
            "a_qk a_v a_sq a_qke a_qr a_qn a_qc a_qlo a_vh a_vl "
            "a_qt a_qe a_kt a_ke0 a_ke1 a_s a_masked a_max a_sub0 a_sub1 a_exp "
            "a_pt a_ph a_pl a_y a_rden a_yn a_yt a_yh a_yl a_x a_o"
        ).split()
        sm = {n: sem(n) for n in names}
        W = [w0, w1]
        first_in = [sm["first_in0"], sm["first_in1"], sm["first_in2"]]
        FIRST_COUNT = [48, 48, 80]
        x_l = [sm["x_l0"], sm["x_l1"]]
        zsv = [sm["zsv0"], sm["zsv1"]]
        zin = [sm["zin0"], sm["zin1"]]
        st_in = [sm["st_in0"], sm["st_in1"]]
        sr_in = [sm["sr_in0"], sm["sr_in1"]]
        scat = [sm["scat0"], sm["scat1"]]
        xr_in = [sm["xr_in0"], sm["xr_in1"]]
        sadd = [sm["sadd0"], sm["sadd1"]]
        y_sv = [sm["y_sv0"], sm["y_sv1"]]

        PH = {"s0": 0, "s1": NB, "e": 2 * NB}
        LEN = {"s0": NB, "s1": NB, "e": NEB}
        HEAD = {"s0": 1, "s1": 2, "e": 1}

        def blk(f, phase, b):
            return FB * f + PH[phase] + b

        use = {}
        for f in range(2):
            def add(*key):
                use[(f, *key)] = len(use)
            add("T", "s0", 0)
            add("R", "s0", 0)
            for b in range(NB - 1):
                add("T", "s0", b + 1)
                add("R", "s0", b + 1)
            add("M", "s1", 1)
            add("T", "e", 0)
            for b in range(NEB):
                if b:
                    add("O", "e", b - 1)
                if b < NEB - 1:
                    add("T", "e", b + 1)
            add("O", "e", NEB - 1)

        POOL_CONSTS = 12

        def hooks(f, phase, s):
            b, n = s.index, LEN[phase]
            last = s.reg is None and b == n - 1
            got = {}
            if phase == "s0":
                if not last:
                    got[3] = ("T", "s0", 1)
                    got[5] = ("R", "s0", 1)
            elif phase == "s1":
                if s.reg is None and b == 1:
                    got[0] = ("M", "s1", 0)
            else:
                if not s.first:
                    got[1] = ("O", "e", -1)
                if not last:
                    got[4] = ("T", "e", 1)
            return got

        def use_at(f, phase, s, hook):
            what, ph2, off = hook
            return s.at(lambda b: use[(f, what, ph2, b + off)])

        def out_used(f, s):
            return s.at(lambda b: (use[(f, "O", "e", b - 2)] if b > 1 else use[(f, "O", "e", 0)] - 2) + 1)

        def shared_before(f, phase, b):
            return 2 * NB * f + {"s0": 0, "s1": NB, "e": 2 * NB}[phase] + b

        def piece_of(f, unit, j):
            return (f * UNITS + unit) * NCH + j

        def splits(f, phase, s):
            if phase == "e":
                return {c: (s.index % 2) * 4 + c // 2 for c in range(NCH)}
            return {6: None}

        def split_piece(f, phase, s, c):
            cs = splits(f, phase, s)
            if c not in cs:
                return None
            if phase == "e":
                j = cs[c]
                unit = lambda b: SU + b // 2 + 1
                if s.reg is None and s.index >= NEB - 2 and f == 1:
                    return None
                return (s.at(lambda b: piece_of(f, unit(b), 0) + j), j, unit(s.index) % 2)
            u = 1 if phase == "s0" else 2
            return (s.at(lambda b: piece_of(f, u, b)), None, u % 2)

        HALF = 8
        LEAD = 3
        RT = 35
        XB = NEB // 2
        block = ctx.enter_context(nc.Block())

        @block.tensor
        def _(pe):
            def split_product(dst, pairs, n):
                k = 0
                for ah, al, bh, bl in pairs:
                    for a, b in ((ah, bh), (ah, bl), (al, bh)):
                        last = pe.matmul(dst, a, b, start=(k == 0), stop=(k == 3 * n - 1))
                        k += 1
                return last

            def gate_up(f, phase, s, c, buf, ncol):
                par = c % 2
                n = lambda b: NCH * blk(f, phase, b) + c
                z = s.mod % 2
                for which, psb, done in ((0, gate_p, "gate_full"), (1, up_p, "up_full")):
                    if n(s.index) >= 2:
                        pe.wait_ge(sm["silu_done" if which == 0 else "h_done"], s.at(lambda b: n(b) - 1))
                    k0 = which * KC * P
                    w = W[buf]
                    split_product(psb[:, par, 0:ncol],
                                  [(w[:, 0, c, k0 + k * P:k0 + (k + 1) * P], w[:, 1, c, k0 + k * P:k0 + (k + 1) * P],
                                    zh[:, z, k, 0:ncol], zl[:, z, k, 0:ncol]) for k in range(KC)], KC).then_inc(sm[done], 1)

            def out_free(f, phase, s):
                if phase == "e" and not s.first:
                    pe.wait_ge(sm["ot_act"], s.at(lambda b: NEB * f + b))
                    pe.wait_ge(sm["ot_dve"], s.at(lambda b: NEB * f + b))
                elif phase != "s0" or not s.first:
                    pe.wait_ge(sm["shared_added"], s.at(lambda b: shared_before(f, phase, b)))

            def down_shared(n_of, s, c, buf):
                pe.wait_ge(sm["hl_done"], s.at(lambda b: n_of(b) + 1))
                w = W[buf][:, :, c, 2 * KC * P:PIECE]
                par = c % 2
                for j in range(BT):
                    o = (j % 2) * C
                    cols = slice(j * P, (j + 1) * P)
                    for n, (a, hi) in enumerate(((hh, 0), (hl, 0), (hh, 1))):
                        last = pe.matmul(out_p[:, j // 2, o:o + C], a[:, par, cols], w[:, hi, :],
                                         start=(c == 0 and n == 0 and j % 2 == 0), stop=(c == NCH - 1 and n == 2 and j % 2 == 1))
                last.then_inc(sm["down_done"], 1)

            def down(n_of, s, c, buf, ncol):
                pe.wait_ge(sm["hl_done"], s.at(lambda b: n_of(b) + 1))
                w = W[buf]
                par = c % 2
                for k in range(KC):
                    o = 2 * KC * P + k * P
                    for j, (hi, a) in enumerate(((0, hh), (0, hl), (1, hh))):
                        last = pe.matmul(out_p[:, k, 0:ncol], w[:, hi, c, o:o + P], a[:, par, 0:ncol],
                                         start=(c == 0 and j == 0), stop=(c == NCH - 1 and j == 2))
                last.then_inc(sm["down_done"], 1)

            def z_transposes(f, phase, s, off, m):
                nxt = lambda b: b + off
                if phase == "s0":
                    pe.wait_ge(sm["ln_z"], s.at(lambda b: NB * f + nxt(b) + 1))
                else:
                    par = (s.mod + off) % 2
                    pe.wait_ge(xr_in[par], s.at(lambda b: 32 * (XB * f + nxt(b) // 2 + 1)))
                wait(pe, sm["misc_free"], m)
                par = (s.mod + off) % 2
                for k in range(KC):
                    if phase == "s0":
                        for j in range(BT):
                            last = pe.transpose(misc[:, k, j * P:(j + 1) * P], zn[:, par, j, k * P:(k + 1) * P], ident[:, :])
                    else:
                        for j, (at, rows) in enumerate(EPART):
                            last = pe.transpose(misc[:, k, at:at + rows], xr[0:rows, par, j, k * P:(k + 1) * P],
                                                ident[0:rows, 0:rows])
                last.then_inc(sm["misc_full"], 1)

            def router_product(s, off, m):
                pe.wait_ge(sm["misc_free"], m)
                par = (s.mod + off) % 2
                for j in range(BT):
                    c = slice(j * P, (j + 1) * P)
                    for k in range(KC):
                        pe.matmul(misc[:, 0, 2 * E * j:2 * E * (j + 1)], zh[:, par, k, c], router[:, k, :, :].rearrange("p a e -> p (a e)"),
                                  start=(k == 0), stop=False)
                        last = pe.matmul(misc[:, 0, 2 * E * j:2 * E * j + E], zl[:, par, k, c], router[:, k, 0, :],
                                         start=False, stop=(k == KC - 1))
                last.then_inc(sm["misc_full"], 1)

            def out_transposes(count, m):
                pe.wait_ge(sm["ot_act"], count)
                pe.wait_ge(sm["ot_dve"], count)
                pe.wait_ge(sm["misc_free"], m)
                for j, (at, rows) in enumerate(EPART):
                    for k in range(KC):
                        o = (j % 2) * C + k * P
                        last = pe.transpose(misc[0:rows, j // 2, o:o + P], o_t[:, k, at:at + rows], ident[:, :])
                last.then_inc(sm["misc_full"], 1)

            def route_product(f, m):
                pe.wait_ge(sm["const"], 1)
                pe.wait_ge(sm["rt_mask"], f + 1)
                pe.wait_ge(sm["misc_free"], m)
                mk = mask[:, :, :].rearrange("p t e -> p (t e)")
                pe.matmul(misc[:, 0, 0:NT * E], below[:, :], mk, start=True, stop=True)
                pe.matmul(misc[:, 1, 0:NT * E], ones[:, :], mk, start=True, stop=True).then_inc(sm["misc_full"], 1)

            def do_hook(f, phase, s, hook):
                what, ph2, off = hook
                m = use_at(f, phase, s, hook)
                if what == "T":
                    z_transposes(f, ph2, s, off, m)
                elif what == "R":
                    router_product(s, off, m)
                elif what == "M":
                    route_product(f, m)
                else:
                    out_transposes(s.at(lambda b: NEB * f + b), m)

            def ffn(f):
                z_transposes(f, "s0", Step(0, 2), 0, use[(f, "T", "s0", 0)])
                if f == 0:
                    pe.wait_ge(sm["rt_in"], 2)
                router_product(Step(0, 2), 0, use[(f, "R", "s0", 0)])
                for phase in ("s0", "s1", "e"):
                    period = 4 if phase == "e" else 2
                    ncol = EB if phase == "e" else SB

                    def body(s, phase=phase, ncol=ncol):
                        unit = (lambda b: SU + b // 2) if phase == "e" else (lambda b: 0 if phase == "s0" else 1)
                        buf = unit(s.index) % 2
                        first_of_unit = s.first or (phase == "e" and s.index % 2 == 0)
                        if phase == "s1":
                            pe.wait_ge(zin[s.mod % 2], s.at(lambda b: 32 * (NB // 2 * f + b // 2 + 1)))
                        else:
                            pe.wait_ge(sm["misc_free"], s.at(lambda b: use[(f, "T", phase, b)] + 1))
                        hk = hooks(f, phase, s)
                        for c in range(NCH):
                            if first_of_unit:
                                pe.wait_ge(sm["wl_done"], s.at(lambda b: piece_of(f, unit(b), c) + 1))
                            gate_up(f, phase, s, c, buf, ncol)
                            if c == 1:
                                out_free(f, phase, s)
                            n_of = lambda b: NCH * blk(f, phase, b) + c - 1
                            if c and phase == "e":
                                down(n_of, s, c - 1, buf, ncol)
                            elif c:
                                down_shared(n_of, s, c - 1, buf)
                            elif phase == "e" and not s.first:
                                down(n_of, s, NCH - 1, unit(s.index - 1) % 2, ncol)
                            elif not (phase == "s0" and s.first):
                                down_shared(n_of, s, NCH - 1, 1 - buf if s.first else buf)
                            if c in hk:
                                do_hook(f, phase, s, hk[c])

                    sweep(pe, LEN[phase], period, body, head=HEAD[phase])
                    if phase == "s1":
                        z_transposes(f, "e", Step(0, 4), 0, use[(f, "T", "e", 0)])
                s = Step(FB * f + FB, 1)
                down(lambda b: NCH * b - 1, s, NCH - 1, (UNITS - 1) % 2, EB)
                out_transposes(NEB * (f + 1), use[(f, "O", "e", NEB - 1)])

            def attention():
                z_p, y_p = quad[:, 0, 0:C], quad[:, 1, 0:C]
                side = gate_p[:, 1, C:2 * C]

                def c(t, k=1):
                    return t.at(lambda b: min(max(b + k, 0), NT))

                def z_transpose(t):
                    pe.wait_ge(sm["a_zn"], c(t))
                    wait(pe, sm["a_masked"], c(t, -2))
                    for k in range(KC):
                        last = pe.transpose(z_p[:, k * P:(k + 1) * P], azn[:, t.index % 2, k * P:(k + 1) * P], ident[:, :])
                    last.then_inc(sm["a_t"], 1)

                def qkv(t):
                    pe.wait_ge(sm["a_zl"], c(t))
                    wait(pe, sm["a_qn"], c(t, 0))
                    z = t.index % 2
                    for dst, c0, c1 in ((gate_p[:, 0, :], 0, 2 * C), (gate_p[:, 1, 0:C], 2 * C, 3 * C)):
                        if c0:
                            wait(pe, sm["a_vl"], c(t, 0))
                            wait(pe, sm["a_o"], c(t, -3))
                        done = "a_v" if c0 else "a_qk"
                        split_product(dst, [(azh[:, z, k, :], azl[:, z, k, :], aw[:, 0, k, c0:c1], aw[:, 1, k, c0:c1])
                                                   for k in range(KC)], KC).then_inc(sm[done], 1)

                def pair_transposes(src, done):
                    for j in range(NH // 2):
                        last = pe.transpose(misc[:, j // 4, (j % 4) * P:(j % 4 + 1) * P],
                                            src[:, 2 * j:2 * j + 2, :].rearrange("p h d -> p (h d)"), ident[:, :])
                    last.then_inc(sm[done], 1)

                def scores(t):
                    pe.wait_ge(sm["a_ke0"], c(t))
                    pe.wait_ge(sm["a_ke1"], c(t))
                    wait(pe, sm["a_masked"], c(t, 0))
                    wait(pe, sm["a_yl"], c(t, -1))
                    pe.wait_ge(sm["a_zl"], c(t, 3))
                    for j in range(NH // 2):
                        o = (j % 4) * P
                        for g in range(2):
                            own = slice(GROUP * g, GROUP * g + GROUP)
                            last = pe.matmul(quad[:, j // 4, o:o + P].rearrange("p (r c) -> p r c", r=2), q_t[:, j, g, :],
                                             k_t[:, j, :, own], start=(g == 0), stop=(g == 1))
                    last.then_inc(sm["a_s"], 1)

                def values(t):
                    pe.wait_ge(sm["a_pl"], c(t))
                    pe.wait_ge(sm["a_vl"], c(t))
                    wait(pe, sm["a_yn"], c(t, 0))
                    q = t.index % 4
                    for j in range(NH // 2):
                        o = (j % 4) * 66
                        last = split_product(quad[:, 2 + j // 4, o:o + 66], [(ph[:, j, :], pl[:, j, :], vh[:, q, j, :], vl[:, q, j, :])], 1)
                    last.then_inc(sm["a_y"], 1)

                def step(s):
                    probs, keys = s.shift(-LEAD - 2, NT), s.shift(-LEAD, NT)
                    t = s.shift(1 - LEAD, NT)
                    if t:
                        qkv(t)
                    if keys:
                        t = keys
                        pe.wait_ge(sm["a_qlo"], c(t))
                        wait(pe, sm["a_pl"], c(t, -1))
                        pair_transposes(qcat, "a_qt")
                    t = s.shift(2 - LEAD, NT)
                    if t:
                        z_transpose(t)
                    if probs:
                        values(probs)
                    if keys:
                        pe.wait_ge(sm["a_qe"], c(keys))
                        pair_transposes(kcat, "a_kt")
                    if probs:
                        t = probs
                        pe.wait_ge(sm["a_yn"], c(t))
                        pe.wait_ge(sm["a_masked"], c(t, 2))
                        for k in range(KC):
                            last = pe.transpose(y_p[:, k * P:(k + 1) * P], y_s[:, k * P:(k + 1) * P], ident[:, :])
                        last.then_inc(sm["a_yt"], 1)
                    t = s.shift(-LEAD - 1, NT)
                    if t:
                        pe.wait_ge(sm["a_exp"], c(t))
                        pe.wait_ge(sm["a_ke0"], c(t, 2))
                        pe.wait_ge(sm["a_ke1"], c(t, 2))
                        pair_transposes(p_s, "a_pt")
                    if keys:
                        scores(keys)
                    if probs:
                        t = probs
                        pe.wait_ge(sm["a_yl"], c(t))
                        pe.wait_ge(sm["a_vl"], c(t, 4))
                        split_product(side, [(yh[:, k, :], yl[:, k, :], aw[:, 0, k, 3 * C:4 * C], aw[:, 1, k, 3 * C:4 * C])
                                             for k in range(KC)], KC).then_inc(sm["a_x"], 1)

                pe.wait_ge(sm["aw_l"], 1)
                sweep(pe, NT + LEAD + 3, 4, step, head=LEAD + 4, tail=LEAD + 3)

            pe.wait_ge(sm["pool_const"], POOL_CONSTS)
            ffn(0)
            attention()
            ffn(1)

        @block.scalar
        def _(act):
            def z_high(f, phase, s, off, m):
                par = (s.mod + off) % 2
                ncol = SB if phase == "s0" else EB
                act.wait_ge(sm["misc_full"], m + 1)
                wait(act, sm["up_full"], s.at(lambda b: NCH * (blk(f, phase, b + off) - 1)))
                if phase == "s0":
                    act.wait_ge(zsv[par], s.at(lambda b: 48 * (NB // 2 * f + (b + off) // 2 + 1)))
                nc.scalar.copy(zh[:, par, :, 0:ncol], misc[:, :, 0:ncol]).then_inc(sm["zh_done"], 1)

            def ffn(f):
                if f == 0:
                    first_high(0)
                    act.wait_ge(sm["r_in"], 16 * KC)
                    nc.scalar.copy(router[:, :, 0, :], router_s[:, :, :]).then_inc(sm["rt_in"], 1)
                z_high(f, "s0", Step(0, 2), 0, use[(f, "T", "s0", 0)])
                if f == 0:
                    for j in range(1, NCH):
                        first_high(j)
                for phase in ("s0", "s1", "e"):
                    period = 4 if phase == "e" else 2
                    ncol = EB if phase == "e" else SB

                    def body(s, phase=phase, ncol=ncol):
                        hk = hooks(f, phase, s)
                        for c in range(NCH):
                            par = c % 2
                            n = lambda b: NCH * blk(f, phase, b) + c
                            act.wait_ge(sm["gate_full"], s.at(lambda b: n(b) + 1))
                            if n(s.index) >= 2:
                                act.wait_ge(sm["h_done"], s.at(lambda b: n(b) - 1))
                            nc.scalar.activation(sg_s[:, par, 0:ncol], gate_p[:, par, 0:ncol], ACT.Silu).then_inc(sm["silu_done"], 1)
                            if c == 0 and phase == "e" and not s.first:
                                act.wait_ge(sm["down_done"], s.at(lambda b: NCH * blk(f, phase, b)))
                                act.wait_ge(sm["misc_full"], out_used(f, s))
                                nc.scalar.copy(o_t[:, 0, 0:ncol], out_p[:, 0, 0:ncol]).then_inc(sm["ot_act"], 1)
                            act.wait_ge(sm["h_done"], s.at(lambda b: n(b) + 1))
                            if n(s.index) >= 2:
                                act.wait_ge(sm["down_done"], s.at(lambda b: n(b) - 1))
                            nc.scalar.copy(hh[:, par, 0:ncol], h_s[:, par, 0:ncol]).then_inc(sm["hh_done"], 1)
                            if phase == "s1" and s.first and c == 2:
                                act.wait_ge(sm["rt_rms"], 2 * f + 2)
                                nc.scalar.activation(pr[:, :, :], lg[:, :, :], ACT.Exp).then_inc(sm["rt_exp"], 1)
                            if c in hk and hk[c][0] == "T":
                                z_high(f, hk[c][1], s, hk[c][2], use_at(f, phase, s, hk[c]))
                            piece = split_piece(f, phase, s, c)
                            if piece is not None:
                                weights_high(f, phase, s, c, piece)

                    sweep(act, LEN[phase], period, body, head=HEAD[phase])
                    if phase == "s1":
                        z_high(f, "e", Step(0, 4), 0, use[(f, "T", "e", 0)])
                act.wait_ge(sm["down_done"], NCH * FB * (f + 1))
                act.wait_ge(sm["misc_full"], use[(f, "O", "e", NEB - 2)] + 1)
                nc.scalar.copy(o_t[:, 0, 0:EB], out_p[:, 0, 0:EB]).then_inc(sm["ot_act"], 1)

            def first_high(j):
                act.wait_ge(first_in[min(j, 2)], FIRST_COUNT[min(j, 2)])
                nc.scalar.copy(w0[:, 0, j, :], raw[:, j, :]).then_inc(sm["wh_done"], 1)

            def weights_high(f, phase, s, c, piece):
                n, j, buf = piece
                par = (s.mod if j is None else j) % 2
                if phase == "e":
                    v = s.at(lambda b: 48 * (piece_of(f, SU + b // 2 + 1, j) // 2 + 1))
                    u = s.at(lambda b: NCH * blk(f, "e", b // 2 * 2))
                else:
                    v = s.at(lambda b: 48 * (piece_of(f, 1 if phase == "s0" else 2, b) // 2 + 1))
                    u = NCH * blk(f, phase, 0)
                act.wait_ge(st_in[par], v)
                wait(act, sm["down_done"], u)
                if phase == "e":
                    o = c % 2 * HALF_PIECE
                    nc.scalar.copy(W[buf][:, 0, j, o:o + HALF_PIECE], stage[:, par, o:o + HALF_PIECE]).then_inc(
                        sm["wh_done" if o else "wh_half"], 1)
                    return
                if j is None:
                    dst = W[buf][:, 0, bass.ds(s.at(lambda b: b), 1), :].rearrange("p a c -> p (a c)") if s.reg is not None \
                        else W[buf][:, 0, s.index, :]
                else:
                    dst = W[buf][:, 0, j, :]
                nc.scalar.copy(dst, stage[:, par, :]).then_inc(sm["wh_done"], 1)

            def attention():
                act.wait_ge(sm["aw_in"], 48)
                nc.scalar.copy(aw[:, 0, :, :], aw_s[:, :, :]).then_inc(sm["aw_h"], 1)

                chunks = lambda ap: ap.rearrange("p (k c) -> p k c", k=KC)
                heads = lambda ap: ap.rearrange("p (h d) -> p h d", d=HD)
                z_p, y_p = quad[:, 0, 0:C], quad[:, 1, 0:C]
                side = gate_p[:, 1, C:2 * C]
                pairs = misc[:, :, :].rearrange("p b (j c) -> p (b j) c", c=P)
                high = lambda ap: ap.bitcast(F32R)

                def c(t, k=1):
                    return t.at(lambda b: min(max(b + k, 0), NT))

                def values(t):
                    wait(act, sm["a_y"], c(t, -3))
                    for g in range(2):
                        for r in range(2):
                            src = gate_p[64 * g:64 * g + 64, 1, 0:C].rearrange("p (j r d) -> p j r d", r=2, d=HD)[:, :, r, :]
                            o = 32 * g + HD * r
                            last = nc.scalar.copy(vh[64 * r:64 * r + 64, t.index % 4, :, o:o + HD], src)
                    last.then_inc(sm["a_vh"], 1)

                def step(s):
                    t = s.shift(1 - LEAD, NT)
                    if t:
                        act.wait_ge(sm["a_qk"], c(t))
                        wait(act, sm["a_qke"], c(t, 0))
                        for j in range(2):
                            nc.scalar.activation(sqj[:, j, :], gate_p[:, 0, j * C:(j + 1) * C], ACT.Square,
                                                 accum_out=ssq[:, j:j + 1]).then_inc(sm["a_sq"], 1)
                        act.wait_ge(sm["a_v"], c(t))
                        values(t)
                    t = s.shift(2 - LEAD, NT)
                    if t:
                        act.wait_ge(sm["a_t"], c(t))
                        wait(act, sm["a_v"], c(t, -1))
                        nc.scalar.copy(azh[:, t.index % 2, :, :], chunks(z_p)).then_inc(sm["a_zh"], 1)
                    keys = s.shift(-LEAD, NT)
                    if keys:
                        act.wait_ge(sm["a_qt"], c(keys))
                        wait(act, sm["a_s"], c(keys, 0))
                        for g in range(2):
                            own = slice(GROUP * g, GROUP * g + GROUP)
                            last = nc.scalar.copy(q_t[:, :, g, own], pairs[:, :, own])
                        last.then_inc(sm["a_qe"], 1)
                    t = s.shift(-LEAD - 1, NT)
                    if t:
                        act.wait_ge(sm["a_sub0"], c(t))
                        act.wait_ge(sm["a_sub1"], c(t))
                        wait(act, sm["a_pt"], c(t, 0))
                        nc.scalar.activation(p_s[:, :, :], s_s[:, :, :], ACT.Exp, scale=float(HD) ** -0.5).then_inc(sm["a_exp"], 1)
                    if keys:
                        act.wait_ge(sm["a_kt"], c(keys))
                        nc.scalar.copy(k_t[0:64, :, 0, :], pairs[0:64]).then_inc(sm["a_ke0"], 1)
                    t = s.shift(-LEAD - 2, NT)
                    if t:
                        act.wait_ge(sm["a_yt"], c(t))
                        wait(act, sm["a_x"], c(t, 0))
                        nc.scalar.copy(yh[:, :, :], chunks(y_p)).then_inc(sm["a_yh"], 1)
                    t = s.shift(-LEAD - 1, NT)
                    if t:
                        act.wait_ge(sm["a_pt"], c(t))
                        wait(act, sm["a_y"], c(t, 0))
                        nc.scalar.copy(ph[:, :, :], pairs).then_inc(sm["a_ph"], 1)
                    t = s.shift(1 - LEAD, NT)
                    if t:
                        act.wait_ge(sm["a_qn"], c(t))
                        wait(act, sm["a_kt"], c(t, 0))
                        for dst, q, apart in ((qcat, 0, HD), (kcat, 1, 2 * HD)):
                            twice = dst[:, :, 0:2 * apart].rearrange("p h (n d) -> p h n d", d=apart)[:, :, :, 0:HD]
                            last = nc.scalar.copy(high(twice), heads(qk[:, q, :]).unsqueeze(2).broadcast_to([P, NH, 2, HD]))
                        last.then_inc(sm["a_qc"], 1)

                act.wait_ge(sm["a_const"], 3)
                sweep(act, NT + LEAD + 3, 4, step, head=LEAD + 4, tail=LEAD + 3)

            ffn(0)
            attention()
            ffn(1)

        @block.vector
        def _(dve):
            v = nc.vector

            def ln(f, s, off):
                par = (s.mod + off) % 2
                nb = lambda b: b + off
                L = lambda k: s.at(lambda b: NB * f + nb(b) + k)
                if f == 0:
                    dve.wait_ge(x_l[par], s.at(lambda b: 16 * (nb(b) // 2 + 1)))
                elif s.first and off == 0:
                    dve.wait_ge(sm["a_o"], NT)
                xt = s.at(lambda b: BT * nb(b))
                for j in range(BT):
                    last = v.bn_stats(st[:, j, :], xtile(s, off, j))
                last.then_inc(sm["ln_st"], 1)
                dve.wait_ge(sm["ln_st"], L(1))
                v.tensor_tensor(lnd[:, :], st[:, :, 1], st[:, :, 4], ALU.subtract)
                v.tensor_tensor(lnm[:, :], st[:, :, 1], st[:, :, 4], ALU.add)
                v.tensor_tensor(lnv[:, :], st[:, :, 2], st[:, :, 5], ALU.add).then_inc(sm["ln_a"], 1)
                dve.wait_ge(sm["ln_a"], L(1))
                v.tensor_tensor(lndd[:, :], lnd[:, :], lnd[:, :], ALU.mult)
                v.tensor_scalar(mean[:, :], lnm[:, :], 0.5, None, ALU.mult).then_inc(sm["ln_b"], 1)
                dve.wait_ge(sm["ln_b"], L(1))
                v.scalar_tensor_tensor(out=lnv2[:, :], in0=lndd[:, :], scalar=C / 4.0, in1=lnv[:, :],
                                       op0=ALU.mult, op1=ALU.add).then_inc(sm["ln_c"], 1)
                dve.wait_ge(sm["ln_c"], L(1))
                cols = bass.ds(xt, BT)
                v.tensor_scalar(var[:, cols], lnv2[:, :], 1.0 / C, None, ALU.mult)
                v.tensor_scalar(vare[:, cols], lnv2[:, :], 1.0 / C, LN_EPS, ALU.mult, ALU.add).then_inc(sm["ln_var"], 1)

            def xtile(s, off, j):
                t = s.at(lambda b: BT * (b + off) + j)
                return x[:, bass.ds(t, 1), :].rearrange("p a c -> p (a c)")

            def ln_rows(f, s, off):
                par = (s.mod + off) % 2
                nb = lambda b: b + off
                dve.wait_ge(sm["ln_rstd"], s.at(lambda b: NB * f + nb(b) + 1))
                dve.wait_ge(zsv[par], s.at(lambda b: 48 * (NB // 2 * f + nb(b) // 2 + 1)))
                for j in range(BT):
                    t = s.at(lambda b: BT * nb(b) + j)
                    last = v.tensor_scalar(zn[:, par, j, :], xtile(s, off, j), mean[:, j:j + 1],
                                           rstd[:, bass.ds(t, 1)], ALU.subtract, ALU.mult)
                last.then_inc(sm["ln_z"], 1)

            def z_low(f, phase, s, off, m):
                par = (s.mod + off) % 2
                ncol = SB if phase == "s0" else EB
                if phase == "s0":
                    dve.wait_ge(sm["zh_done"], s.at(lambda b: (NB + NEB) * f + b + off + 1))
                else:
                    dve.wait_ge(sm["zh_done"], s.at(lambda b: (NB + NEB) * f + NB + b + off + 1))
                v.tensor_tensor(zl[:, par, :, 0:ncol], misc[:, :, 0:ncol], zh[:, par, :, 0:ncol],
                                ALU.subtract).then_inc(sm["misc_free"], 1)

            def meta(f, s, off):
                par, q = (s.mod + off) % 2, (s.mod + off) % 4
                nb = lambda b: b + off
                dve.wait_ge(xr_in[par], s.at(lambda b: 32 * (XB * f + nb(b) // 2 + 1)))
                dve.wait_ge(sm["sums_done"], s.at(lambda b: NEB * f + nb(b) + 2))
                col = s.at(lambda b: C + 1 + nb(b) // 2)
                for j, (at, rows) in enumerate(EPART):
                    v.tensor_copy(wmeta[0:rows, q, j:j + 1], xr[0:rows, par, j, bass.ds(col, 1)])
                    last = v.tensor_copy(tmeta[0:rows, q, j:j + 1], xr[0:rows, par, j, C:C + 1])
                last.then_inc(sm["meta_done"], 1)

            def logits(f, s, off, m):
                dve.wait_ge(sm["misc_full"], m + 1)
                t = s.at(lambda b: BT * (b + off))
                both = misc[:, 0, 0:2 * BT * E].rearrange("p (t a e) -> p t e a", a=2, e=E)
                v.tensor_reduce(lg[:, bass.ds(t, BT), :], both, AX, ALU.add).then_inc(sm["misc_free"], 1)

            def add_shared(f, phase, s):
                dve.wait_ge(sm["down_done"], s.at(lambda b: NCH * blk(f, phase, b)))
                tile0 = BT * (NB - 1) if s.first else s.at(lambda b: BT * (b - 1))
                xs = x[:, bass.ds(tile0, BT), :].rearrange("p t c -> p (t c)")
                v.scalar_tensor_tensor(out=xs, in0=out_p.rearrange("p a b -> p (a b)"), scalar=0.5, in1=xs,
                                       op0=ALU.mult, op1=ALU.add).then_inc(sm["shared_added"], 1)

            def expert_rows(f, b_at, par, q, m, parts):
                dve.wait_ge(sm["misc_full"], m + 1)
                dve.wait_ge(sm["sums_done"], b_at(lambda b: NEB * f + b + 4))
                for j in parts:
                    rows = EPART[j][1]
                    o = (j % 2) * C
                    last = v.tensor_scalar(eo[0:rows, par, j, :], misc[0:rows, j // 2, o:o + C], wmeta[0:rows, q, j:j + 1],
                                           0.5, ALU.mult, ALU.mult)
                if j == len(EPART) - 1:
                    last.then_inc(sm["misc_free"], 1)

            def first_low(j):
                dve.wait_ge(sm["wh_done"], j + 1)
                v.tensor_tensor(w0[:, 1, j, :], raw[:, j, :], w0[:, 0, j, :], ALU.subtract).then_inc(sm["wl_done"], 1)

            def weights_low(f, phase, s, c, piece):
                n, j, buf = piece
                par = (s.mod if j is None else j) % 2
                if phase == "e":
                    o = c % 2 * HALF_PIECE
                    cols = slice(o, o + HALF_PIECE)
                    if o:
                        dve.wait_ge(sm["wh_done"], s.at(lambda b: piece_of(f, SU + b // 2 + 1, j) + 1))
                    else:
                        dve.wait_ge(sm["wh_half"], s.at(lambda b: (NEB * f + b) * NCH // 2 + c // 2 + 1))
                    ins = v.tensor_tensor(W[buf][:, 1, j, cols], stage[:, par, cols], W[buf][:, 0, j, cols], ALU.subtract)
                    if o:
                        ins.then_inc(sm["wl_done"], 1)
                    return
                dve.wait_ge(sm["wh_done"], s.at(lambda b: (piece_of(f, 1 if phase == 's0' else 2, b) if j is None else piece_of(f, SU + b // 2 + 1, j)) + 1))
                if j is None:
                    jj = bass.ds(s.at(lambda b: b), 1)
                    hi = W[buf][:, 0, jj, :].rearrange("p a c -> p (a c)")
                    lo = W[buf][:, 1, jj, :].rearrange("p a c -> p (a c)")
                else:
                    hi, lo = W[buf][:, 0, j, :], W[buf][:, 1, j, :]
                v.tensor_tensor(lo, stage[:, par, :], hi, ALU.subtract).then_inc(sm["wl_done"], 1)

            counted = [0]

            def route(f, part):
                def then(ins):
                    counted[0] += 1
                    ins.then_inc(sm["rt"], 1)
                    dve.wait_ge(sm["rt"], counted[0])

                bc = lambda t: t[:, :].unsqueeze(2).broadcast_to([P, NT, E])
                TT, TS = v.tensor_tensor, v.tensor_scalar

                def best_of(best):
                    then(v.tensor_reduce(best[:, :], pr[:, :, :], AX, ALU.max))
                    then(TT(pick[:, :, :], pr[:, :, :], bc(best), ALU.is_equal))
                    then(TT(pick[:, :, :], pick[:, :, :], prio[:, :, :], ALU.mult))

                def first_of(c):
                    then(v.tensor_reduce(ra[:, :], pick[:, :, :], AX, ALU.max))
                    then(TT(oh[:, c, :, :], pick[:, :, :], bc(ra), ALU.is_equal))

                def slots(c):
                    then(TT(pick[:, :, :], oh[:, c, :, :], lg[:, :, :], ALU.mult))
                    then(v.tensor_reduce(ra[:, :], pick[:, :, :], AX, ALU.add))
                    then(v.tensor_copy(slot_i[:, c, :], ra[:, :]))

                if part == 0:
                    then(TT(ra[:, :], rstd[:, :], rstd[:, :], ALU.mult))
                    then(TT(ra[:, :], ra[:, :], var[:, :], ALU.mult))
                    v.tensor_scalar(ra[:, :], ra[:, :], ROUTER_EPS, None, ALU.add).then_inc(sm["rt_rms"], 1)
                elif part == 1:
                    dve.wait_ge(sm["rt_rs"], f + 1)
                    then(TT(lg[:, :, :], lg[:, :, :], bc(rb), ALU.mult))
                    then(v.tensor_reduce(m1[:, :], lg[:, :, :], AX, ALU.max))
                    TT(lg[:, :, :], lg[:, :, :], bc(m1), ALU.subtract).then_inc(sm["rt_rms"], 1)
                elif part == 3:
                    dve.wait_ge(sm["rt_exp"], f + 1)
                    then(v.tensor_reduce(ra[:, :], pr[:, :, :], AX, ALU.add))
                    then(v.reciprocal(rb[:, :], ra[:, :]))
                    then(TT(pr[:, :, :], pr[:, :, :], bc(rb), ALU.mult))
                elif part == 4:
                    best_of(m1)
                elif part == 5:
                    first_of(0)
                    then(v.scalar_tensor_tensor(out=pr[:, :, :], in0=oh[:, 0, :, :], scalar=-2.0, in1=pr[:, :, :],
                                                op0=ALU.mult, op1=ALU.add))
                elif part == 6:
                    best_of(m2)
                elif part == 7:
                    first_of(1)
                    TT(mask[:, :, :], oh[:, 0, :, :], oh[:, 1, :, :], ALU.add).then_inc(sm["rt_mask"], 1)
                elif part == 8:
                    dve.wait_ge(sm["misc_full"], use[(f, "M", "s1", 1)] + 1)
                    v.tensor_copy(pick[:, :, :], misc[:, 1, 0:NT * E].rearrange("p (t e) -> p t e", e=E))
                    v.tensor_copy(lg[:, :, :], misc[:, 0, 0:NT * E].rearrange("p (t e) -> p t e", e=E)).then_inc(sm["misc_free"], 1)
                elif part == 9:
                    dve.wait_ge(sm["misc_free"], use[(f, "M", "s1", 1)] + 1)
                    for e in range(E):
                        last = v.tensor_tensor_scan(pr[:, :, e], one_row[:, :], pick[:, :, e], 0.0, ALU.mult, ALU.add)
                    then(last)
                elif part == 10:
                    then(TT(lg[:, :, :], lg[:, :, :], pr[:, :, :], ALU.add))
                    then(TT(lg[:, :, :], lg[:, :, :], pick[:, :, :], ALU.subtract))
                    then(TS(pick[:, :, :], lg[:, :, :], float(CAP), FAR, ALU.is_ge, ALU.mult))
                elif part == 11:
                    then(TT(lg[:, :, :], lg[:, :, :], pick[:, :, :], ALU.add))
                    then(TT(lg[:, :, :], lg[:, :, :], base[:, :, :], ALU.add))
                elif part == 12:
                    slots(0)
                elif part == 13:
                    slots(1)
                elif part == 14:
                    then(TT(ra[:, :], m1[:, :], m2[:, :], ALU.add))
                    then(v.reciprocal(rb[:, :], ra[:, :]))
                    TT(m1[:, :], m1[:, :], rb[:, :], ALU.mult)
                    then(TT(m2[:, :], m2[:, :], rb[:, :], ALU.mult))
                elif part == 15:
                    TT(lg[:, :, :], oh[:, 0, :, :], bc(m1), ALU.mult)
                    then(TT(pick[:, :, :], oh[:, 1, :, :], bc(m2), ALU.mult))
                    then(TT(table[:, :, 1:1 + E], lg[:, :, :], pick[:, :, :], ALU.add))
                    assert counted[0] == RT * (f + 1), counted[0]

            def ffn(f):
                s0 = Step(0, 2)
                ln(f, s0, 0)
                ln_rows(f, s0, 0)
                if f == 0:
                    first_low(0)
                    dve.wait_ge(sm["pool_const"], POOL_CONSTS)
                    v.tensor_copy(below[:, :], below_s[:, :]).then_inc(sm["const"], 1)
                z_low(f, "s0", s0, 0, use[(f, "T", "s0", 0)])
                if f == 0:
                    dve.wait_ge(sm["rt_in"], 1)
                    v.tensor_tensor(router[:, :, 1, :], router_s[:, :, :], router[:, :, 0, :], ALU.subtract).then_inc(sm["rt_in"], 1)
                    first_low(1)
                logits(f, s0, 0, use[(f, "R", "s0", 0)])
                if f == 0:
                    for j in range(2, NCH):
                        first_low(j)
                for phase in ("s0", "s1", "e"):
                    period = 4 if phase == "e" else 2
                    ncol = EB if phase == "e" else SB

                    def body(s, phase=phase, ncol=ncol):
                        hk = hooks(f, phase, s)
                        last = s.reg is None and s.index == LEN[phase] - 1
                        for c in range(NCH):
                            par = c % 2
                            n = lambda b: NCH * blk(f, phase, b) + c
                            dve.wait_ge(sm["silu_done"], s.at(lambda b: n(b) + 1))
                            dve.wait_ge(sm["up_full"], s.at(lambda b: n(b) + 1))
                            v.tensor_tensor(h_s[:, par, 0:ncol], up_p[:, par, 0:ncol], sg_s[:, par, 0:ncol],
                                            ALU.mult).then_inc(sm["h_done"], 1)
                            if c == 0 and phase == "e" and not s.first:
                                dve.wait_ge(sm["down_done"], s.at(lambda b: NCH * blk(f, phase, b)))
                                dve.wait_ge(sm["misc_full"], out_used(f, s))
                                v.tensor_copy(o_t[:, 1, 0:ncol], out_p[:, 1, 0:ncol]).then_inc(sm["ot_dve"], 1)
                            dve.wait_ge(sm["hh_done"], s.at(lambda b: n(b) + 1))
                            v.tensor_tensor(hl[:, par, 0:ncol], h_s[:, par, 0:ncol], hh[:, par, 0:ncol],
                                            ALU.subtract).then_inc(sm["hl_done"], 1)
                            if c == 0 and not (phase == "s0" and s.first) and (phase != "e" or s.first):
                                add_shared(f, phase, s)
                            if phase == "s1" and s.reg is None and s.index < 2:
                                route(f, NCH * s.index + c)
                            if phase == "s0" and not last and c == 1:
                                ln(f, s, 1)
                            if phase == "s0" and not last and c == 2:
                                ln_rows(f, s, 1)
                            if phase == "e" and not last and c == 3:
                                meta(f, s, 1)
                            piece = split_piece(f, phase, s, c)
                            if piece is not None:
                                weights_low(f, phase, s, c, piece)
                            if c in hk:
                                what, ph2, off = hk[c]
                                m = use_at(f, phase, s, hk[c])
                                if what == "T":
                                    z_low(f, ph2, s, off, m)
                                elif what == "R":
                                    logits(f, s, off, m)
                            if phase == "e" and not s.first and 1 <= c <= len(EPART):
                                m = use_at(f, phase, s, hk[1])
                                expert_rows(f, lambda g: s.at(lambda b: g(b - 1)), (s.mod - 1) % 2, (s.mod - 1) % 4, m, [c - 1])

                    sweep(dve, LEN[phase], period, body, head=HEAD[phase])
                    if phase == "s1":
                        meta(f, Step(0, 4), 0)
                        z_low(f, "e", Step(0, 4), 0, use[(f, "T", "e", 0)])
                dve.wait_ge(sm["down_done"], NCH * FB * (f + 1))
                dve.wait_ge(sm["misc_full"], use[(f, "O", "e", NEB - 2)] + 1)
                v.tensor_copy(o_t[:, 1, 0:EB], out_p[:, 1, 0:EB]).then_inc(sm["ot_dve"], 1)
                expert_rows(f, lambda g: g(NEB - 1), 1, 3, use[(f, "O", "e", NEB - 1)], range(len(EPART)))

            def attention():
                v.memset(qcat[:, :, 3 * HD:64], 0.0)
                v.memset(kcat[:, :, 3 * HD:64], 0.0)
                v.memset(q_t[:, :, 0, GROUP:P].bitcast(F32), 0.0)
                v.memset(q_t[:, :, 1, 0:GROUP].bitcast(F32), 0.0)
                v.memset(k_t[0:64, :, 1, :].bitcast(F32), 0.0)
                v.memset(k_t[64:128, :, 0, :].bitcast(F32), 0.0)
                v.memset(vh[:, :, :, :].bitcast(F32), 0.0)
                v.memset(vl[:, :, :, :].bitcast(F32), 0.0).then_inc(sm["a_const"], 1)
                dve.wait_ge(sm["a_const"], 1)
                for r in range(2):
                    v.memset(vh[64 * r:64 * r + 64, :, :, 64 + r:65 + r].bitcast(F32), 1.0).then_inc(sm["a_const"], 1)
                dve.wait_ge(sm["aw_h"], 1)
                v.tensor_tensor(aw[:, 1, :, :], aw_s[:, :, :], aw[:, 0, :, :], ALU.subtract).then_inc(sm["aw_l"], 1)
                chunks = lambda ap: ap.rearrange("p (k c) -> p k c", k=KC)
                heads = lambda ap: ap.rearrange("p (h d) -> p h d", d=HD)
                z_p, y_p = quad[:, 0, 0:C], quad[:, 1, 0:C]
                side = gate_p[:, 1, C:2 * C]
                pairs = misc[:, :, :].rearrange("p b (j c) -> p (b j) c", c=P)

                def c(t, k=1):
                    return t.at(lambda b: min(max(b + k, 0), NT))

                def row(t):
                    return x[:, bass.ds(t.at(lambda b: b), 1), :].rearrange("p a c -> p (a c)")

                def stats(t):
                    a = lambda k: t.at(lambda b: 3 * b + k)
                    dve.wait_ge(sm["x2_in"], t.at(lambda b: 16 * (b // 4 + 1)))
                    v.bn_stats(ast[:, :], row(t)).then_inc(sm["av"], 1)
                    dve.wait_ge(sm["av"], a(1))
                    dve.sem_inc(sm["dve_step"], 1)
                    m = t.index % 2
                    v.bn_aggr(amv[:, m, :], ast[:, :]).then_inc(sm["av"], 1)
                    dve.wait_ge(sm["av"], a(2))
                    v.tensor_scalar(ave[:, m:m + 1], amv[:, m, 1:2], LN_EPS, None, ALU.add).then_inc(sm["av"], 1)

                def masked(t):
                    dve.wait_ge(sm["a_s"], c(t))
                    wait(dve, sm["a_exp"], c(t, 0))
                    v.tensor_tensor(s_s[:, :, :], quad[:, 0:2, :].rearrange("p b (h c) -> p (b h) c", c=GROUP),
                                    causal[:, :].unsqueeze(1).broadcast_to([P, NH, GROUP]), ALU.add).then_inc(sm["a_masked"], 1)

                def values(t):
                    dve.wait_ge(sm["a_vh"], c(t))
                    q = t.index % 4
                    for g in range(2):
                        for r in range(2):
                            src = gate_p[64 * g:64 * g + 64, 1, 0:C].rearrange("p (j r d) -> p j r d", r=2, d=HD)[:, :, r, :]
                            o = 32 * g + HD * r
                            rows = slice(64 * r, 64 * r + 64)
                            last = v.tensor_tensor(vl[rows, q, :, o:o + HD], src, vh[rows, q, :, o:o + HD], ALU.subtract)
                    last.then_inc(sm["a_vl"], 1)

                def outputs(t):
                    dve.wait_ge(sm["a_y"], c(t))
                    wait(dve, sm["a_yt"], c(t, 0))
                    yp = quad[:, 2:4, 0:4 * 66].rearrange("p b (j c) -> p b j c", c=66)
                    rd4 = rden[:, :].rearrange("p (b j r) -> p b j r", b=2, r=2)
                    for b in range(2):
                        last = v.reciprocal(rd4[:, b, :, :], yp[:, b, :, 64:66])
                    last.then_inc(sm["a_rden"], 1)
                    dve.wait_ge(sm["a_rden"], c(t))
                    for g in range(2):
                        rows = slice(64 * g, 64 * g + 64)
                        for b in range(2):
                            src = yp[rows, b, :, 32 * g:32 * g + 32].rearrange("p j (r d) -> p j r d", d=HD)
                            dst = y_s[rows, :].rearrange("p (b j r d) -> p b j r d", b=2, r=2, d=HD)[:, b]
                            last = v.tensor_tensor(dst, src, rd4[rows, b].unsqueeze(3).broadcast_to([64, 4, 2, HD]), ALU.mult)
                    last.then_inc(sm["a_yn"], 1)

                def add_output(t):
                    dve.wait_ge(sm["a_x"], c(t))
                    v.tensor_tensor(row(t), side, row(t), ALU.add).then_inc(sm["a_o"], 1)

                def step(s):
                    t = s.shift(-LEAD - 2, NT)
                    if t:
                        dve.wait_ge(sm["a_ph"], c(t))
                        v.tensor_tensor(pl[:, :, :], pairs, ph[:, :, :], ALU.subtract).then_inc(sm["a_pl"], 1)
                    t = s.shift(-LEAD - 3, NT)
                    if t:
                        add_output(t)
                    t = s.shift(2 - LEAD, NT)
                    if t:
                        m = t.index % 2
                        dve.wait_ge(sm["a_rs"], c(t))
                        wait(dve, sm["a_t"], c(t, -1))
                        v.tensor_scalar(azn[:, m, :], row(t), amv[:, m, 0:1], ard[:, m:m + 1], ALU.subtract, ALU.mult).then_inc(sm["a_zn"], 1)
                    t = s.shift(-LEAD - 1, NT)
                    if t:
                        masked(t)
                    t = s.shift(-LEAD - 1, NT)
                    if t:
                        dve.wait_ge(sm["a_masked"], c(t))
                        wait(dve, sm["a_sub0"], c(t, 0))
                        v.tensor_reduce(smax[:, :], s_s[:, :, :], AX, ALU.max).then_inc(sm["a_max"], 1)
                        dve.wait_ge(sm["a_max"], c(t))
                        v.tensor_tensor(s_s[:, HALF:NH, :], s_s[:, HALF:NH, :],
                                        smax[:, HALF:NH].unsqueeze(2).broadcast_to([P, NH - HALF, GROUP]),
                                        ALU.subtract).then_inc(sm["a_sub1"], 1)
                    t = s.shift(1 - LEAD, NT)
                    if t:
                        dve.wait_ge(sm["a_sq"], t.at(lambda b: 2 * b + 2))
                        wait(dve, sm["a_qr"], c(t, 0))
                        v.tensor_scalar(qke[:, :], ssq[:, :], 1.0 / C, RMS_EPS, ALU.mult, ALU.add).then_inc(sm["a_qke"], 1)
                        values(t)
                    t = s.shift(2 - LEAD, NT)
                    if t:
                        dve.wait_ge(sm["a_zh"], c(t))
                        v.tensor_tensor(azl[:, t.index % 2, :, :], chunks(z_p), azh[:, t.index % 2, :, :], ALU.subtract).then_inc(sm["a_zl"], 1)
                    t = s.shift(-LEAD - 2, NT)
                    if t:
                        outputs(t)
                    t = s.shift(-LEAD, NT)
                    if t:
                        dve.wait_ge(sm["a_kt"], c(t))
                        wait(dve, sm["a_s"], c(t, 0))
                        v.tensor_copy(k_t[64:128, :, 1, :], pairs[64:128]).then_inc(sm["a_ke1"], 1)
                    t = s.shift(-LEAD - 2, NT)
                    if t:
                        dve.wait_ge(sm["a_yh"], c(t))
                        v.tensor_tensor(yl[:, :, :], chunks(y_p), yh[:, :, :], ALU.subtract).then_inc(sm["a_yl"], 1)
                    t = s.shift(1 - LEAD, NT)
                    if t:
                        dve.wait_ge(sm["a_qr"], c(t))
                        wait(dve, sm["a_qlo"], c(t, 0))
                        for j in range(2):
                            last = v.scalar_tensor_tensor(out=qk[:, j, :], in0=gate_p[:, 0, j * C:(j + 1) * C], scalar=qkr[:, j:j + 1],
                                                          in1=lnw[:, :], op0=ALU.mult, op1=ALU.mult)
                        last.then_inc(sm["a_qn"], 1)
                    t = s.shift(3 - LEAD, NT)
                    if t:
                        stats(t)

                sweep(dve, NT + LEAD + 3, 4, step, head=LEAD + 4, tail=LEAD + 3)

            v.memset(ones[:, :].bitcast(F32), 1.0)
            v.memset(mhalf[:, :], -0.5)
            v.memset(one_row[:, :], 1.0)
            ffn(0)
            attention()
            ffn(1)

        @block.gpsimd
        def _(pool):
            g = nc.gpsimd

            def after(*counts):
                for semaphore, value in counts:
                    pool.wait_ge(semaphore, value)
                pool.sem_inc(sm["pool_step"], 1)

            k = [0]
            whole = pick[:, :, :].rearrange("p t e -> p (t e)").bitcast(I32)

            def then(ins):
                k[0] += 1
                ins.then_inc(sm["pool_const"], 1)
                pool.wait_ge(sm["pool_const"], k[0])

            g.memset(ident[:, :], 0.0)
            g.memset(below_s[:, :], 1.0)
            g.memset(causal[:, :], 0.0)
            then(g.memset(empty[:, :], 0.0))
            g.affine_select(out=ident[:, :], in_=ident[:, :], compare_op=ALU.not_equal, fill=1.0, base=0,
                            pattern=[[-1, P]], channel_multiplier=1)
            then(g.affine_select(out=below_s[:, :], in_=below_s[:, :], compare_op=ALU.is_gt, fill=0.0, base=0,
                                 pattern=[[1, P]], channel_multiplier=-1))
            for row in range(0, P, GROUP):
                own = causal[row:row + GROUP, :]
                then(g.affine_select(out=own, in_=own, compare_op=ALU.is_ge, fill=-3.0e38, base=0,
                                     pattern=[[-1, GROUP]], channel_multiplier=1))
            then(g.iota(whole[:, 0:1], pattern=[[0, 1]], base=T, channel_multiplier=1))
            then(g.tensor_copy(empty[:, C:C + 1], whole[:, 0:1]))
            for dst, args in ((table[:, :, 0], dict(pattern=[[P, NT]], base=0, channel_multiplier=1)),
                              (prio[:, :, :], dict(pattern=[[0, NT], [-1, E]], base=E, channel_multiplier=0)),
                              (base[:, :, :], dict(pattern=[[0, NT], [CAP, E]], base=0, channel_multiplier=0))):
                n = NT if dst is table[:, :, 0] or len(args["pattern"]) == 1 else NT * E
                src = whole[:, 0:n] if n == NT else whole.rearrange("p (t e) -> p t e", e=E)
                then(g.iota(src, **args))
                then(g.tensor_copy(dst, src))
            assert k[0] == POOL_CONSTS, k[0]
            def attention():
                def step(s):
                    t = s.shift(-LEAD - 1, NT)
                    if t:
                        after((sm["a_max"], t.at(lambda b: b + 1)))
                        g.tensor_tensor(s_s[:, 0:HALF, :], s_s[:, 0:HALF, :],
                                        smax[:, 0:HALF].unsqueeze(2).broadcast_to([P, HALF, GROUP]),
                                        ALU.subtract).then_inc(sm["a_sub0"], 1)
                    t = s.shift(1 - LEAD, NT)
                    if t:
                        after((sm["a_qke"], t.at(lambda b: b + 1)))
                        g.tensor_tensor(qkr[:, :], qke[:, :], mhalf[:, 0:2], ALU.pow).then_inc(sm["a_qr"], 1)
                    t = s.shift(3 - LEAD, NT)
                    if t:
                        m = t.index % 2
                        after((sm["av"], t.at(lambda b: 3 * b + 3)))
                        g.tensor_tensor(ard[:, m:m + 1], ave[:, m:m + 1], mhalf[:, 0:1], ALU.pow).then_inc(sm["a_rs"], 1)
                    t = s.shift(1 - LEAD, NT)
                    if t:
                        after((sm["a_qc"], t.at(lambda b: b + 1)))
                        heads = lambda ap: ap.rearrange("p (h d) -> p h d", d=HD)
                        g.tensor_tensor(qcat[:, :, 2 * HD:3 * HD].bitcast(F32R), heads(qk[:, 0, :]), qcat[:, :, 0:HD], ALU.subtract)
                        g.tensor_tensor(kcat[:, :, HD:2 * HD].bitcast(F32R), heads(qk[:, 1, :]), kcat[:, :, 0:HD],
                                        ALU.subtract).then_inc(sm["a_qlo"], 1)
                sweep(pool, NT + LEAD + 3, 4, step, head=LEAD + 4, tail=LEAD + 3)

            pool.sem_inc(sm["sums_done"], 4)

            def ln(f):
                def body(s):
                    after((sm["ln_var"], s.at(lambda b: NB * f + b + 1)))
                    cols = bass.ds(s.at(lambda b: BT * b), BT)
                    g.tensor_tensor(rstd[:, cols], vare[:, cols], mhalf[:, 0:BT], ALU.pow).then_inc(sm["ln_rstd"], 1)
                sweep(pool, NB, 2, body)

            def scatter(f):
                def body(s):
                    par = s.mod % 2
                    w = s.at(lambda t: 32 * (NT // 2 * f + t // 2))
                    if not isinstance(w, int) or w:
                        after((scat[par], w))
                    t = s.at(lambda t: t)
                    g.dma_start(srow[:, par, 0:C], zn_rows[:, bass.ds(t, 1), :].rearrange("p a c -> p (a c)")).then_inc(sr_in[par], 16)
                    g.tensor_copy(srow[:, par, C:ROW], table[:, bass.ds(t, 1), :].rearrange("p a c -> p (a c)"))
                    g.tensor_copy(sidx[:, par, :], slot_i[:, :, bass.ds(t, 1)].rearrange("p a c -> p (a c)")).then_inc(sm["sidx_in"], 1)
                    after((sr_in[par], s.at(lambda t: 16 * (NT // 2 * f + t // 2 + 1))),
                          (sm["sidx_in"], s.at(lambda t: NT * f + t + 1)))
                    for c in range(TOPK):
                        g.indirect_dma_start(out=slots_d[f], out_offset=bass.IndirectOffsetOnAxis(ap=sidx[:, par, c:c + 1], axis=0),
                                             in_=srow[:, par, :], in_offset=None, bounds_check=E * CAP - 1,
                                             oob_is_err=False).then_inc(scat[par], 16)
                sweep(pool, NT, 2, body, head=3)

            def expert_sums(f):
                def body(s):
                    par, q = s.mod % 2, s.mod
                    w = s.at(lambda b: 48 * (XB * f + (b + 1) // 2))
                    wait(pool, sadd[1 - par], w)
                    pool.sem_inc(sm["sums_done"], 1)
                    after((sm["misc_free"], s.at(lambda b: use[(f, "O", "e", b)] + 1)))
                    for j, (at, rows) in enumerate(EPART):
                        g.indirect_dma_start(out=y_d[f], out_offset=bass.IndirectOffsetOnAxis(ap=tmeta[0:rows, q, j:j + 1], axis=0),
                                             in_=eo[0:rows, par, j, :], in_offset=None, bounds_check=T - 1,
                                             oob_is_err=False, compute_op=ALU.add).then_inc(sadd[par], 16)
                sweep(pool, NEB, 4, body)

            for f in range(2):
                ln(f)
                pool.wait_ge(sm["rt_rms"], 2 * f + 1)
                g.tensor_tensor(rb[:, :], ra[:, :], mhalf[:, :], ALU.pow).then_inc(sm["rt_rs"], 1)
                pool.wait_ge(sm["rt"], RT * (f + 1))
                for par in range(2):
                    pool.wait_ge(zsv[par], 48 * (NB // 2 * (f + 1) + 1))
                pool.wait_ge(sm["init"], 16 * NB * (f + 1))
                scatter(f)
                for par in range(2):
                    pool.wait_ge(y_sv[par], 16 * NB // 2 * (f + 1))
                expert_sums(f)
                if f == 0:
                    attention()

        @block.sync
        def _(sp):
            def hold(semaphore, value):
                sp.wait_ge(semaphore, value)
                if not isinstance(value, int):
                    sp.sem_inc(sm["sp_step"], 1)

            def load_x(src, b, f):
                wait(sp, x_l[b % 2], 16 * (NB // 2 * f + b // 2))
                sp.dma_start(x[:, BT * b:BT * b + BT, :], src[:, BT * b:BT * b + BT, :]).then_inc(x_l[b % 2], 16)

            def load_piece(par, gate, up, down):
                st_ = stage[:, par, :]
                sp.dma_start(st_[:, 0:KC * P].rearrange("p (k i) -> p k i", k=KC), gate).then_inc(st_in[par], 16)
                sp.dma_start(st_[:, KC * P:2 * KC * P].rearrange("p (k i) -> p k i", k=KC), up).then_inc(st_in[par], 16)
                sp.dma_start(st_[:, 2 * KC * P:PIECE], down).then_inc(st_in[par], 16)

            def shared_piece(u, j):
                i0 = u * NCH + j
                view = lambda w: w.rearrange("(k p) i -> p k i", p=P)[:, :, bass.ds(i0 * P, P)]
                return view(sg), view(su), sd.rearrange("(i p) c -> p i c", p=P)[:, bass.ds(i0, 1), :].rearrange("p a c -> p (a c)")

            def expert_piece(e, j):
                view = lambda w: w.rearrange("e (k p) i -> p (e k) i", p=P)[:, bass.ds(e * KC, KC), j * P:(j + 1) * P]
                return view(rg), view(ru), rd.rearrange("e (i p) c -> p (e i) c", p=P)[:, bass.ds(e * NCH + j, 1), :].rearrange("p a c -> p (a c)")

            def ffn(f):
                for phase in ("s0", "s1", "e"):
                    def body(s, phase=phase):
                        last = s.reg is None and s.index == LEN[phase] - 1
                        if phase == "s0":
                            u = 1
                            hold(sm["wl_done"], s.at(lambda b: piece_of(f, u, b) - 1))
                            load_piece(s.mod % 2, *shared_piece(u, s.at(lambda b: b)))
                            tiles = E * CAP // P // NB
                            sp.dma_start(slots_d[f].rearrange("(t p) c -> p t c", p=P)[:, bass.ds(s.at(lambda b: b * tiles), tiles), :],
                                         empty[:, :].unsqueeze(1).broadcast_to([P, tiles, ROW])).then_inc(sm["init"], 16)
                            if not last:
                                save_z(f, s, 1)
                        elif phase == "s1":
                            if not last:
                                load_z(f, s, 1)
                            hold(sm["wl_done"], s.at(lambda b: piece_of(f, 2, b) - 1))
                            load_piece(s.mod % 2, *expert_piece_at(s))
                            if not s.first:
                                save_x(f, s.at(lambda b: shared_before(f, "s1", b)), s.at(lambda b: b - 1), (s.mod - 1) % 2)
                        else:
                            if not (s.reg is None and s.index >= NEB - 2):
                                load_rows(f, s, 2)
                            half = s.index % 2
                            for jj in range(4):
                                j = 4 * half + jj
                                if s.reg is None and s.index >= NEB - 2:
                                    if f == 0:
                                        hold(sm["wl_done"], piece_of(1, 0, j) - 1)
                                        load_piece(j % 2, *shared_piece(0, j))
                                    continue
                                hold(sm["wl_done"], s.at(lambda b: piece_of(f, SU + b // 2 + 1, j) - 1))
                                load_piece(j % 2, *expert_piece(s.at(lambda b: b // 2 + 1), j))
                                if s.first and jj == 0:
                                    save_x(f, shared_before(f, "e", 0), NB - 1, 1)
                    sweep(sp, LEN[phase], 4 if phase == "e" else 2, body, tail=2 if phase == "e" else 0)
                    if phase == "s0":
                        load_z(f, Step(0, 2), 0)
                    if phase == "s1":
                        for par in range(2):
                            hold(scat[par], 32 * (NT // 2 * (f + 1)))
                        load_rows(f, Step(0, 4), 0)
                        load_rows(f, Step(1, 4), 0)

            def expert_piece_at(s):
                j = s.at(lambda b: b)
                view = lambda w: w[0, :, :].rearrange("(k p) i -> p k i", p=P)[:, :, bass.ds(j * P, P)]
                return view(rg), view(ru), rd[0, :, :].rearrange("(i p) c -> p i c", p=P)[:, bass.ds(j, 1), :].rearrange("p a c -> p (a c)")

            def save_z(f, s, off):
                par = (s.mod + off) % 2
                b_ = s.at(lambda b: b + off)
                hold(sm["misc_free"], s.at(lambda b: use[(f, "T", "s0", b + off)] + 1))
                cols = bass.ds(b_ * SB, SB)
                sp.dma_start(zh_d[:, :, cols], zh[:, par, :, :].bitcast(F32)).then_inc(zsv[par], 16)
                sp.dma_start(zl_d[:, :, cols], zl[:, par, :, :].bitcast(F32)).then_inc(zsv[par], 16)
                sp.dma_start(zn_rows[:, bass.ds(b_ * BT, BT), :], zn[:, par, :, :]).then_inc(zsv[par], 16)

            def load_z(f, s, off):
                par = (s.mod + off) % 2
                hold(sm["up_full"], s.at(lambda b: NCH * (blk(f, "s1", b + off) - 1)))
                if s.first and off == 0:
                    for q in zsv:
                        hold(q, 48 * (NB // 2 * (f + 1) + 1))
                cols = bass.ds(s.at(lambda b: (b + off) * SB), SB)
                sp.dma_start(zh[:, par, :, :].bitcast(F32), zh_d[:, :, cols]).then_inc(zin[par], 16)
                sp.dma_start(zl[:, par, :, :].bitcast(F32), zl_d[:, :, cols]).then_inc(zin[par], 16)

            def load_rows(f, s, off):
                par = (s.mod + off) % 2
                if off:
                    hold(sm["misc_free"], s.at(lambda b: use[(f, "T", "e", b)] + 1))
                    hold(sm["meta_done"], s.at(lambda b: NEB * f + b + 1))
                at = s.at(lambda b: EB * (b + off))
                sp.dma_start(xr[:, par, 0:2, :], slots_d[f][bass.ds(at, 2 * P), :].rearrange("(j p) c -> p j c", p=P)).then_inc(xr_in[par], 16)
                sp.dma_start(xr[0:EB - 2 * P, par, 2, :], slots_d[f][bass.ds(at + 2 * P, EB - 2 * P), :]).then_inc(xr_in[par], 16)

            def save_x(f, count, b, par):
                hold(sm["shared_added"], count)
                t = bass.ds(b * BT, BT)
                sp.dma_start(y_rows[f][:, t, :], x[:, t, :]).then_inc(y_sv[par], 16)

            def first_piece(j):
                st_ = raw[:, j, :]
                gate, up, down_ = shared_piece(0, j)
                sp.dma_start(st_[:, 0:KC * P].rearrange("p (k i) -> p k i", k=KC), gate).then_inc(first_in[j], 16)
                sp.dma_start(st_[:, KC * P:2 * KC * P].rearrange("p (k i) -> p k i", k=KC), up).then_inc(first_in[j], 16)
                sp.dma_start(st_[:, 2 * KC * P:PIECE], down_).then_inc(first_in[j], 16)

            for q in zsv:
                sp.sem_inc(q, 48)
            load_x(x_rows, 0, 0)
            first_piece(0)
            for kk in range(KC):
                sp.dma_start(router_s[:, kk, :], router_w[:, kk * P:(kk + 1) * P].rearrange("e p -> p e"),
                             allow_slow_non_contiguous=True).then_inc(sm["r_in"], 16)
            first_piece(1)
            load_x(x_rows, 1, 0)
            for k in range(KC):
                for o, w in ((0, sg), (KC * P, su)):
                    sp.dma_start(raw[:, 2:NCH, o + k * P:o + (k + 1) * P],
                                 w[k * P:(k + 1) * P, 2 * P:NCH * P].rearrange("p (j i) -> p j i", i=P)).then_inc(first_in[2], 16)
            sp.dma_start(raw[:, 2:NCH, 2 * KC * P:PIECE],
                         sd[2 * P:NCH * P, :].rearrange("(j p) c -> p j c", p=P)).then_inc(first_in[2], 16)
            for par in range(2):
                sp.sem_inc(st_in[par], 48 * NCH // 2)
            for b in range(2, NB):
                load_x(x_rows, b, 0)
            hold(sm["pool_const"], POOL_CONSTS)
            save_z(0, Step(0, 2), 0)
            ffn(0)
            hold(sm["down_done"], NCH * FB)
            sp.dma_start(aw_s[:, :, 0:3 * C], w_qkv.rearrange("(k p) d -> p k d", p=P)).then_inc(sm["aw_in"], 16)
            sp.dma_start(aw_s[:, :, 3 * C:4 * C], w_proj.rearrange("(k p) d -> p k d", p=P)).then_inc(sm["aw_in"], 16)
            sp.dma_start(lnw[:, :], ln_w.rearrange("(a c) -> a c", a=1).broadcast_to([P, C])).then_inc(sm["aw_in"], 16)
            for par in range(2):
                hold(sadd[par], 48 * XB)
            for b in range(NB):
                wait(sp, sm["x2_in"], 16 * b)
                sp.dma_start(x[:, BT * b:BT * b + BT, :], y_rows[0][:, BT * b:BT * b + BT, :]).then_inc(sm["x2_in"], 16)
            save_z(1, Step(0, 2), 0)
            ffn(1)
            for par in range(2):
                hold(sadd[par], 48 * 2 * XB)


_INS = ["L0_attn_x", "L0_attn_w_qkv", "L0_attn_ln_w", "L0_attn_w_proj", "L0_ffn_router_w", "L0_ffn_rg", "L0_ffn_ru",
        "L0_ffn_rd", "L0_ffn_sg", "L0_ffn_su", "L0_ffn_sd"]
_OUT = ((2, 2048, 256), "float32")


def kernel(**inputs):
    import numpy as np
    import concourse.bacc as bacc
    from concourse.bass_utils import run_bass_kernel_spmd

    nc = bacc.Bacc("TRN2", target_bir_lowering=False, num_devices=1)
    arrays, args = {}, []
    for name in _INS:
        a = np.ascontiguousarray(inputs[name])
        arrays[f"in_{name}"] = a
        args.append(nc.dram_tensor(f"in_{name}", a.shape, mybir.dt.from_np(a.dtype), kind="ExternalInput").ap())
    shape, dtype = _OUT
    args.append(nc.dram_tensor("out_dram", shape, mybir.dt.from_np(np.dtype(dtype)), kind="ExternalOutput").ap())
    program(nc, *args)
    r = run_bass_kernel_spmd(nc, [arrays], core_ids=[0])
    return r.results[0]["out_dram"]
```
